# Optimizing a Trainium2 kernel written in Bass

```python
import numpy as np
import jax
import jax.numpy as jnp

def _softmax(x, axis=-1):
    return jax.nn.softmax(x, axis=axis)

def _gelu(x):
    return jax.nn.gelu(x, approximate=True)

def _silu(x):
    return jax.nn.silu(x)

def _sigmoid(x):
    return jax.nn.sigmoid(x)

def _layernorm(x, axis=-1, eps=1e-05):
    m = jnp.mean(x, axis=axis, keepdims=True)
    v = jnp.var(x, axis=axis, keepdims=True)
    return (x - m) / jnp.sqrt(v + eps)

def _scatter_add(tgt, idx, src, axis=0):
    return tgt.at[idx].add(src)

def _segment_sum(src, seg, n):
    return jax.ops.segment_sum(src, seg, n)
kernel_name = 'mk_xattn_ffn_d2_seqx_r4_83ab50'

def setup_inputs(seed: int=0):
    np.random.seed(seed)
    _w = jnp.asarray

    def _rec_inputs():
        import jax
        import jax.numpy as jnp
        _rk = jax.random.key(seed)
        x = -0.0002928 + 1 * jax.random.normal(jax.random.fold_in(_rk, 1), (4, 512, 512), jnp.float32)
        _lenS = 512 - jax.random.randint(jax.random.fold_in(_rk, 7), (4,), 0, max(1, 512 // 4) + 1, jnp.int32)
        _lenS2 = 1024 - jax.random.randint(jax.random.fold_in(_rk, 8), (4,), 0, max(1, 1024 // 4) + 1, jnp.int32)
        _ctx_512P = jax.random.normal(jax.random.fold_in(_rk, 11), (4, 16, 128), jnp.float32)
        _ctx_512c = jax.random.dirichlet(jax.random.fold_in(_rk, 511), 0.3 * jnp.ones((16,), jnp.float32), (4, 1024))
        _ctx_512t = jnp.einsum('bsk,bkd->bsd', _ctx_512c, _ctx_512P)
        _ctx_512t = _ctx_512t * jax.lax.rsqrt(jnp.mean(jnp.square(_ctx_512t)) + 1e-12) * 0.953939
        ctx_512 = 0.000227908 + 0.99994 * (_ctx_512t + 0.3 * jax.random.normal(jax.random.fold_in(_rk, 611), (4, 1024, 128), jnp.float32))
        return (x, ctx_512)
    x, ctx_512 = _rec_inputs()

    def _L0_xattn_setup():
        import jax, jax.numpy as jnp
        import numpy as np
        B, S, L = (2, 256, 256)
        DIM_Q, H, K, D_C, D_CQ, R = (512, 16, 128, 128, 384, 64)

        def _rope_tables(seq_len, dim, dtype):
            inv_freq = 1.0 / 10000.0 ** (jnp.arange(0, dim, 2, dtype=dtype) / dim)
            t = jnp.arange(seq_len, dtype=dtype)
            freqs = t[:, None] * inv_freq[None, :]
            sin = jnp.repeat(jnp.sin(freqs), 2, axis=-1)
            cos = jnp.repeat(jnp.cos(freqs), 2, axis=-1)
            return (sin, cos)

        def _rotate_half(x):
            h = x.shape[-1] // 2
            return jnp.concatenate([-x[..., h:], x[..., :h]], axis=-1)
        key = jax.random.key(seed)
        ks = jax.random.split(key, 8)
        s_in = 1.0 / np.sqrt(DIM_Q)
        s_k = 1.0 / np.sqrt(K)
        s_cq = 1.0 / np.sqrt(D_CQ)
        s_c = 1.0 / np.sqrt(D_C)
        return {'hidden_q': jax.random.normal(ks[0], (B, S, DIM_Q), jnp.float32), 'kv_c': jax.random.normal(ks[1], (B, L, D_C), jnp.float32), 'Wq': jax.random.normal(ks[2], (H * K, DIM_Q), jnp.float32) * s_in, 'w_kc_q': jax.random.normal(ks[3], (H, K, D_CQ), jnp.float32) * s_k, 'w_kc_kv': jax.random.normal(ks[4], (H, K, D_C), jnp.float32) * s_k, 'W_qr': jax.random.normal(ks[5], (H, D_CQ, R), jnp.float32) * s_cq / np.sqrt(R), 'W_kr': jax.random.normal(ks[6], (H, D_C, R), jnp.float32) * s_c, 'Wo': jax.random.normal(ks[7], (DIM_Q, H * K), jnp.float32) * s_k}
    _L0_xattn_all = _L0_xattn_setup()
    _L0_xattn_in = {k: v for k, v in _L0_xattn_all.items() if k in ('Wq', 'w_kc_q', 'w_kc_kv', 'W_qr', 'W_kr', 'Wo')}
    del _L0_xattn_all

    def _L0_ffn_setup():
        import jax, jax.numpy as jnp
        import numpy as np
        E = 8
        CAPACITY_FACTOR = 1.25
        B, T, H, I = (4, 256, 512, 352)
        key = jax.random.key(seed)
        k0, k1, k2, k3, k4 = jax.random.split(key, 5)
        x = jax.random.normal(k0, (B, T, H), jnp.float32)
        Wr = jax.random.normal(k1, (E, H), jnp.float32) * 0.02
        Wg = jax.random.normal(k2, (E, I, H), jnp.float32) * 0.02
        Wu = jax.random.normal(k3, (E, I, H), jnp.float32) * 0.02
        Wd = jax.random.normal(k4, (E, H, I), jnp.float32) * 0.02
        return {'x': x, 'Wr': Wr, 'Wg': Wg, 'Wu': Wu, 'Wd': Wd}
    _L0_ffn_all = _L0_ffn_setup()
    _L0_ffn_in = {k: v for k, v in _L0_ffn_all.items() if k in ('Wr', 'Wg', 'Wu', 'Wd')}
    del _L0_ffn_all

    def _L1_xattn_setup():
        import jax, jax.numpy as jnp
        import numpy as np
        B, S, H, NH, L = (2, 512, 512, 16, 128)
        HD = H // NH
        key = jax.random.key(seed)
        k1, k2, k3, k4, k5 = jax.random.split(key, 5)
        scale = 0.02
        return {'q': jax.random.normal(k1, (B, S, H), dtype=jnp.float32), 'latent_kv': jax.random.normal(k2, (B, S, L), dtype=jnp.float32), 'Wq': jax.random.normal(k3, (H, H), dtype=jnp.float32) * scale, 'Wkv_expand': jax.random.normal(k4, (2 * H, L), dtype=jnp.float32) * scale, 'Wout': jax.random.normal(k5, (H, H), dtype=jnp.float32) * scale}
    _L1_xattn_all = _L1_xattn_setup()
    _L1_xattn_in = {k: v for k, v in _L1_xattn_all.items() if k in ('Wq', 'Wkv_expand', 'Wout')}
    del _L1_xattn_all

    def _L1_ffn_setup():
        import jax, jax.numpy as jnp
        import numpy as np
        H = 512
        I = 256
        E = 32
        K = 4
        N_SHARED = 1
        EPS = 1e-06

        def _rmsnorm(x, w, eps=EPS):
            var = jnp.mean(jnp.square(x), axis=-1, keepdims=True)
            return x * jax.lax.rsqrt(var + eps) * w

        def _moe_core(x, gate_w, w13, w2):
            T = x.shape[0]
            N = T * K
            C = 2 * N // E
            logits = jnp.einsum('th,eh->te', x.astype(jnp.float32), gate_w.astype(jnp.float32))
            scores = jax.nn.softmax(logits, axis=-1)
            topk_w, topk_ids = jax.lax.top_k(scores, K)
            topk_w = topk_w / jnp.sum(topk_w, axis=-1, keepdims=True)
            flat_ids = topk_ids.reshape(-1)
            flat_w = topk_w.reshape(-1)
            order = jnp.argsort(flat_ids)
            sorted_eid = flat_ids[order]
            tok = order // K
            counts = jnp.zeros((E,), jnp.int32).at[flat_ids].add(1)
            starts = jnp.cumsum(counts) - counts
            pos = jnp.arange(N) - starts[sorted_eid]
            buf = jnp.zeros((E, C, x.shape[1]), x.dtype).at[sorted_eid, pos].set(x[tok], mode='drop')
            gu = jnp.einsum('ech,ehf->ecf', buf, w13)
            g, u = jnp.split(gu, 2, axis=-1)
            act = jax.nn.silu(g) * u
            eo = jnp.einsum('eci,eih->ech', act, w2)
            out_slots = eo[sorted_eid, pos]
            routed = jnp.zeros_like(x).at[tok].add(out_slots * flat_w[order][:, None])
            return routed
        key = jax.random.key(seed)
        ks = jax.random.split(key, 8)
        s = 1.0 / np.sqrt(H)
        si = 1.0 / np.sqrt(I)
        return {'hidden_states': jax.random.normal(ks[0], (1, 1024, H), jnp.float32), 'norm_w': jnp.ones((H,), jnp.float32), 'gate_w': jax.random.normal(ks[1], (E, H), jnp.float32) * s, 'w13': jax.random.normal(ks[2], (E, H, 2 * I), jnp.float32) * s, 'w2': jax.random.normal(ks[3], (E, I, H), jnp.float32) * si, 'shared_gate_w': jax.random.normal(ks[4], (H, I * N_SHARED), jnp.float32) * s, 'shared_up_w': jax.random.normal(ks[5], (H, I * N_SHARED), jnp.float32) * s, 'shared_down_w': jax.random.normal(ks[6], (I * N_SHARED, H), jnp.float32) * si}
    _L1_ffn_all = _L1_ffn_setup()
    _L1_ffn_in = {k: v for k, v in _L1_ffn_all.items() if k in ('norm_w', 'gate_w', 'w13', 'w2', 'shared_gate_w', 'shared_up_w', 'shared_down_w')}
    del _L1_ffn_all
    return {'x': x, 'ctx_512': ctx_512, 'L0_xattn_Wq': _L0_xattn_in['Wq'], 'L0_xattn_w_kc_q': _L0_xattn_in['w_kc_q'], 'L0_xattn_w_kc_kv': _L0_xattn_in['w_kc_kv'], 'L0_xattn_W_qr': _L0_xattn_in['W_qr'], 'L0_xattn_W_kr': _L0_xattn_in['W_kr'], 'L0_xattn_Wo': _L0_xattn_in['Wo'], 'L0_ffn_Wr': _L0_ffn_in['Wr'], 'L0_ffn_Wg': _L0_ffn_in['Wg'], 'L0_ffn_Wu': _L0_ffn_in['Wu'], 'L0_ffn_Wd': _L0_ffn_in['Wd'], 'L1_xattn_Wq': _L1_xattn_in['Wq'], 'L1_xattn_Wkv_expand': _L1_xattn_in['Wkv_expand'], 'L1_xattn_Wout': _L1_xattn_in['Wout'], 'L1_ffn_norm_w': _L1_ffn_in['norm_w'], 'L1_ffn_gate_w': _L1_ffn_in['gate_w'], 'L1_ffn_w13': _L1_ffn_in['w13'], 'L1_ffn_w2': _L1_ffn_in['w2'], 'L1_ffn_shared_gate_w': _L1_ffn_in['shared_gate_w'], 'L1_ffn_shared_up_w': _L1_ffn_in['shared_up_w'], 'L1_ffn_shared_down_w': _L1_ffn_in['shared_down_w']}

def reference(x, ctx_512, L0_xattn_Wq, L0_xattn_w_kc_q, L0_xattn_w_kc_kv, L0_xattn_W_qr, L0_xattn_W_kr, L0_xattn_Wo, L0_ffn_Wr, L0_ffn_Wg, L0_ffn_Wu, L0_ffn_Wd, L1_xattn_Wq, L1_xattn_Wkv_expand, L1_xattn_Wout, L1_ffn_norm_w, L1_ffn_gate_w, L1_ffn_w13, L1_ffn_w2, L1_ffn_shared_gate_w, L1_ffn_shared_up_w, L1_ffn_shared_down_w):
    import jax
    import jax.numpy as jnp

    def _L0_xattn_ref(hidden_q, kv_c, Wq, w_kc_q, w_kc_kv, W_qr, W_kr, Wo):
        import jax, jax.numpy as jnp
        import numpy as np
        B, S, L = (2, 256, 256)
        DIM_Q, H, K, D_C, D_CQ, R = (512, 16, 128, 128, 384, 64)

        def _rope_tables(seq_len, dim, dtype):
            inv_freq = 1.0 / 10000.0 ** (jnp.arange(0, dim, 2, dtype=dtype) / dim)
            t = jnp.arange(seq_len, dtype=dtype)
            freqs = t[:, None] * inv_freq[None, :]
            sin = jnp.repeat(jnp.sin(freqs), 2, axis=-1)
            cos = jnp.repeat(jnp.cos(freqs), 2, axis=-1)
            return (sin, cos)

        def _rotate_half(x):
            h = x.shape[-1] // 2
            return jnp.concatenate([-x[..., h:], x[..., :h]], axis=-1)
        b, s, _ = hidden_q.shape
        l = kv_c.shape[1]
        q_hk = (hidden_q @ Wq.T).reshape(b, s, H, K)
        q_big = jnp.einsum('bshk,hkq->bshq', q_hk, w_kc_q)
        sin, cos = _rope_tables(l, D_C, kv_c.dtype)
        kv_rope = kv_c * cos[None] + _rotate_half(kv_c) * sin[None]
        q_r = jnp.einsum('bshq,hqr->bhsr', q_big, W_qr)
        k_r = jnp.einsum('bld,hdr->bhlr', kv_rope, W_kr)
        scores = jnp.einsum('bhsr,bhlr->bhsl', q_r, k_r)
        attn = jax.nn.softmax(scores, axis=-1)
        ctx_c = jnp.einsum('bhsl,bld->bhsd', attn, kv_rope)
        ctx_lat = jnp.einsum('bhsd,hkd->bshk', ctx_c, w_kc_kv)
        out = ctx_lat.reshape(b, s, H * K) @ Wo.T
        return out

    def _L0_ffn_ref(x, Wr, Wg, Wu, Wd):
        import jax, jax.numpy as jnp
        import numpy as np
        E = 8
        CAPACITY_FACTOR = 1.25
        B, T, H, I = (4, 256, 512, 352)
        Bb, Tt, Hh = x.shape
        N = Bb * Tt
        cap = max(1, int(CAPACITY_FACTOR * (N * 2 / E)))
        xf = x.reshape(N, Hh)
        logits = jnp.einsum('nh,eh->ne', xf, Wr)
        gate = jax.nn.softmax(logits, axis=-1)
        top2_val, top2_idx = jax.lax.top_k(gate, 2)
        flat_idx = jnp.concatenate([top2_idx[:, 0], top2_idx[:, 1]])
        flat_val = jnp.concatenate([top2_val[:, 0], top2_val[:, 1]])
        onehot = jax.nn.one_hot(flat_idx, E, dtype=jnp.int32)
        rank = (jnp.cumsum(onehot, axis=0) * onehot).sum(-1)
        keep = rank <= cap
        w_assign = jnp.where(keep, flat_val, 0.0)
        tok = jnp.tile(jnp.arange(N), 2)
        comb = jnp.zeros((N, E), x.dtype).at[tok, flat_idx].add(w_assign)
        g = jax.nn.silu(jnp.einsum('nh,eih->eni', xf, Wg))
        u = jnp.einsum('nh,eih->eni', xf, Wu)
        out_e = jnp.einsum('eni,ehi->enh', g * u, Wd)
        y = jnp.einsum('ne,enh->nh', comb, out_e)
        return y.reshape(Bb, Tt, Hh)

    def _L1_xattn_ref(q, latent_kv, Wq, Wkv_expand, Wout):
        import jax, jax.numpy as jnp
        import numpy as np
        B, S, H, NH, L = (2, 512, 512, 16, 128)
        HD = H // NH
        b, sq, _ = q.shape
        sk = latent_kv.shape[1]
        qp = q @ Wq.T
        kv = latent_kv @ Wkv_expand.T
        k, v = jnp.split(kv, 2, axis=-1)
        qh = qp.reshape(b, sq, NH, HD).transpose(0, 2, 1, 3)
        kh = k.reshape(b, sk, NH, HD).transpose(0, 2, 1, 3)
        vh = v.reshape(b, sk, NH, HD).transpose(0, 2, 1, 3)
        inv_sqrt_d = 1.0 / jnp.sqrt(jnp.float32(HD))
        scores = jnp.einsum('bhqd,bhkd->bhqk', qh, kh) * inv_sqrt_d
        causal = jnp.tril(jnp.ones((sq, sk), dtype=bool))
        scores = jnp.where(causal, scores, jnp.finfo(scores.dtype).min)
        attn = jax.nn.softmax(scores, axis=-1)
        out = jnp.einsum('bhqk,bhkd->bhqd', attn, vh)
        out = out.transpose(0, 2, 1, 3).reshape(b, sq, H)
        return out @ Wout.T

    def _L1_ffn_ref(hidden_states, norm_w, gate_w, w13, w2, shared_gate_w, shared_up_w, shared_down_w):
        import jax, jax.numpy as jnp
        import numpy as np
        H = 512
        I = 256
        E = 32
        K = 4
        N_SHARED = 1
        EPS = 1e-06

        def _rmsnorm(x, w, eps=EPS):
            var = jnp.mean(jnp.square(x), axis=-1, keepdims=True)
            return x * jax.lax.rsqrt(var + eps) * w

        def _moe_core(x, gate_w, w13, w2):
            T = x.shape[0]
            N = T * K
            C = 2 * N // E
            logits = jnp.einsum('th,eh->te', x.astype(jnp.float32), gate_w.astype(jnp.float32))
            scores = jax.nn.softmax(logits, axis=-1)
            topk_w, topk_ids = jax.lax.top_k(scores, K)
            topk_w = topk_w / jnp.sum(topk_w, axis=-1, keepdims=True)
            flat_ids = topk_ids.reshape(-1)
            flat_w = topk_w.reshape(-1)
            order = jnp.argsort(flat_ids)
            sorted_eid = flat_ids[order]
            tok = order // K
            counts = jnp.zeros((E,), jnp.int32).at[flat_ids].add(1)
            starts = jnp.cumsum(counts) - counts
            pos = jnp.arange(N) - starts[sorted_eid]
            buf = jnp.zeros((E, C, x.shape[1]), x.dtype).at[sorted_eid, pos].set(x[tok], mode='drop')
            gu = jnp.einsum('ech,ehf->ecf', buf, w13)
            g, u = jnp.split(gu, 2, axis=-1)
            act = jax.nn.silu(g) * u
            eo = jnp.einsum('eci,eih->ech', act, w2)
            out_slots = eo[sorted_eid, pos]
            routed = jnp.zeros_like(x).at[tok].add(out_slots * flat_w[order][:, None])
            return routed
        B, S, Hd = hidden_states.shape
        residual = hidden_states
        h = _rmsnorm(hidden_states, norm_w)
        x = h.reshape(-1, Hd)
        routed = _moe_core(x, gate_w, w13, w2)
        shared = jax.nn.silu(x @ shared_gate_w) * (x @ shared_up_w) @ shared_down_w
        out = residual + (routed + shared).reshape(B, S, Hd)
        return out
    x = x + _L0_xattn_ref(_layernorm(x, axis=-1), ctx_512, L0_xattn_Wq, L0_xattn_w_kc_q, L0_xattn_w_kc_kv, L0_xattn_W_qr, L0_xattn_W_kr, L0_xattn_Wo)
    x = x + _L0_ffn_ref(_layernorm(x, axis=-1), L0_ffn_Wr, L0_ffn_Wg, L0_ffn_Wu, L0_ffn_Wd)
    x = x + _L1_xattn_ref(_layernorm(x, axis=-1), ctx_512, L1_xattn_Wq, L1_xattn_Wkv_expand, L1_xattn_Wout)
    x = x + _L1_ffn_ref(_layernorm(x, axis=-1), L1_ffn_norm_w, L1_ffn_gate_w, L1_ffn_w13, L1_ffn_w2, L1_ffn_shared_gate_w, L1_ffn_shared_up_w, L1_ffn_shared_down_w)
    return x

_drawn_inputs = setup_inputs


def setup_inputs(seed=0):
    import zlib

    import numpy as np

    out = dict(_drawn_inputs(seed))
    spreads = {'L1_ffn_norm_w': (1.0, 0.2)}
    factors = {'L0_ffn_Wr': 6.328,
     'L0_ffn_Wg': 4.801,
     'L0_ffn_Wu': 4.666,
     'L0_ffn_Wd': 5.431,
     'L1_xattn_Wq': 64.0,
     'L1_xattn_Wkv_expand': 4.603,
     'L1_xattn_Wout': 4.561}
    for name, (base, spread) in spreads.items():
        noise = np.random.default_rng([zlib.crc32(name.encode()), seed]).standard_normal(out[name].shape)
        drawn = base * np.exp(spread * noise) if base else spread * noise
        out[name] = jnp.asarray(drawn.astype(out[name].dtype))
    for name, factor in factors.items():
        out[name] = (out[name] * factor).astype(out[name].dtype)
    return out
```

```python
from contextlib import ExitStack

import numpy as np

import concourse.bass as bass
from concourse import mybir

F32 = mybir.dt.float32
F32R = mybir.dt.float32r
BF16 = mybir.dt.bfloat16
I32 = mybir.dt.int32
U32 = mybir.dt.uint32
ACT = mybir.ActivationFunctionType
ALU = mybir.AluOpType
AX = mybir.AxisListType

P = 128
B, S, D = 4, 512, 512
SK, DC = 1024, 128
N = B * S
NT = N // P
TB = S // P
KD = D // P
LN_EPS = 1e-5
RMS_EPS = 1e-6

H0, HK, DCQ, R = 16, 128, 384, 64
KQ = DCQ // P
LT = SK // P
H1 = 16
HD = D // H1
GH = P // HD
NG = H1 // GH
NEG = -1e30
E0, K0, I0 = 8, 2, 352
CAP0 = int(1.25 * (N * K0 / E0))
E1, K1, I1 = 32, 4, 256
CAP1 = 2 * N * K1 // E1
NSH = N // CAP1


class Shared:
    pass


class MoeLayer:

    def __init__(self, name, E, K, I, cap, chunks, router, wgu, wd, rms, shared, choice_major, renorm, drop_weight, z_made):
        self.name, self.E, self.K, self.I, self.cap = name, E, K, I, cap
        self.chunks = chunks
        self.router, self.wgu, self.wd = router, wgu, wd
        self.rms = rms
        self.shared = shared
        self.choice_major = choice_major
        self.renorm = renorm
        self.drop_weight = drop_weight
        self.z_made = z_made


class Scope:

    def __init__(self, nc, name):
        self.nc, self.name, self.stack, self.sems = nc, name, ExitStack(), []

    def __enter__(self):
        self.stack.__enter__()
        return self

    def __exit__(self, *a):
        self.stack.__exit__(*a)
        if self.sems:
            self.nc.clear_and_free_semaphores(self.sems)
            self.nc.all_engine_barrier()

    def sb(self, name, shape, dt=F32):
        return self.stack.enter_context(self.nc.sbuf_tensor(f"{self.name}_{name}", shape, dt))

    def ps(self, name, shape=(P, 512), dt=F32):
        return self.stack.enter_context(self.nc.psum_tensor(f"{self.name}_{name}", list(shape), dt))

    def sem(self, name):
        self.sems.append(self.nc.alloc_semaphore(f"{self.name}_{name}"))
        return self.sems[-1]

    def block(self):
        return self.stack.enter_context(self.nc.Block())


def fold_weights(nc, t, g):
    with Scope(nc, "fold") as s:
        kcq = s.sb("kcq", [P, KQ, H0, HK])
        wqr = s.sb("wqr", [P, KQ, H0, R])
        wq = s.sb("wq", [P, H0, D])
        kckv = s.sb("kckv", [P, H0, DC])
        wo = s.sb("wo", [P, H0, D])
        t1 = [s.sb(f"t1_{j}", [P, R]) for j in range(2)]
        ps_t1 = [s.ps(f"ps_t1_{j}") for j in range(2)]
        ps_wa = [s.ps(f"ps_wa_{j}") for j in range(2)]
        ps_mo = [s.ps(f"ps_mo_{j}") for j in range(2)]
        x_in, q_in, v_in = s.sem("x_in"), s.sem("q_in"), s.sem("v_in")
        t1_made, t1_copied, wa_made, wa_copied = (s.sem(n) for n in ("t1_made", "t1_copied", "wa_made", "wa_copied"))
        mo_made, mo_copied, ident_zeroed, consts_made = (s.sem(n) for n in ("mo_made", "mo_copied", "ident_zeroed", "consts_made"))
        block = s.block()

        @block.sync
        def _(sp):
            sp.dma_start(kcq[:], g["w_kc_qT"]).then_inc(q_in, 16)
            sp.dma_start(wqr[:], g["w_qr"]).then_inc(q_in, 16)
            sp.dma_start(wq[:], g["wq0"]).then_inc(q_in, 16)
            sp.dma_start(kckv[:], g["w_kc_kv"]).then_inc(v_in, 16)
            sp.dma_start(wo[:], g["wo0"]).then_inc(v_in, 16)
            sp.dma_start(t.wkr[:], g["w_kr"]).then_inc(x_in, 16)
            sp.dma_start(t.x[:], g["x"].rearrange("(t p) d -> p t d", p=P)).then_inc(x_in, 16)
            sp.wait_ge(x_in, 32)

        @block.gpsimd
        def _(pool):
            pool.memset(t.ident[:], 0.0).then_inc(ident_zeroed, 1)
            pool.wait_ge(ident_zeroed, 1)
            pool.affine_select(out=t.ident[:], in_=t.ident[:], compare_op=ALU.not_equal, fill=1.0, base=0,
                               pattern=[[-1, P]], channel_multiplier=1).then_inc(consts_made, 1)
            pool.memset(t.ones[:], 1.0).then_inc(consts_made, 1)
            pool.memset(t.ln_eps[:], LN_EPS).then_inc(consts_made, 1)
            pool.memset(t.rms_eps[:], RMS_EPS).then_inc(consts_made, 1)
            pool.wait_ge(consts_made, 4)

        @block.tensor
        def _(pe):
            pe.wait_ge(q_in, 48)
            for h in range(H0):
                if h >= 2:
                    pe.wait_ge(t1_copied, h - 1)
                for q in range(KQ):
                    mm = pe.matmul(ps_t1[h % 2][:, 0:R], kcq[:, q, h, :], wqr[:, q, h, :], start=q == 0, stop=q == KQ - 1)
                mm.then_inc(t1_made, 1)
                if h == 0:
                    pe.wait_ge(v_in, 32)
                if h >= 2:
                    pe.wait_ge(mo_copied, h - 1)
                pe.matmul(ps_mo[h % 2][:], kckv[:, h, :], wo[:, h, :], start=True, stop=True).then_inc(mo_made, 1)
                pe.wait_ge(t1_copied, h + 1)
                if h >= 2:
                    pe.wait_ge(wa_copied, h - 1)
                for k in range(KD):
                    mm = pe.matmul(ps_wa[h % 2][:, k * R:(k + 1) * R], wq[:, h, k * P:(k + 1) * P], t1[h % 2][:],
                                   start=True, stop=True)
                mm.then_inc(wa_made, 1)

        @block.vector
        def _(dve):
            for h in range(H0):
                dve.wait_ge(t1_made, h + 1)
                if h >= 2:
                    dve.wait_ge(wa_made, h - 1)
                dve.tensor_copy(t1[h % 2][:], ps_t1[h % 2][:, 0:R]).then_inc(t1_copied, 1)
                dve.wait_ge(wa_made, h + 1)
                dve.tensor_copy(t.wa[:, h, :, :], ps_wa[h % 2][:, 0:KD * R].rearrange("p (k r) -> p k r", r=R)).then_inc(wa_copied, 1)
            dve.wait_ge(wa_copied, H0)

        @block.scalar
        def _(act):
            for h in range(H0):
                act.wait_ge(mo_made, h + 1)
                act.copy(t.mo[:, h, :], ps_mo[h % 2][:]).then_inc(mo_copied, 1)
            act.wait_ge(mo_copied, H0)


def latent_attention(nc, t, g):
    HALF = SK // 2
    with Scope(nc, "la") as s:
        ctx = s.sb("ctx", [P, LT, DC])
        kv = s.sb("kv", [P, LT, DC])
        kvT = s.sb("kvT", [P, SK])
        hqT = s.sb("hqT", [P, KD, S])
        stats, mv = s.sb("stats", [P, TB, 6]), s.sb("mv", [P, TB, 2])
        std, rstd = s.sb("std", [P, TB]), s.sb("rstd", [P, TB])
        was = [s.sb(f"was{j}", [P, KD, 2, R]) for j in range(2)]
        wks = [s.sb(f"wks{j}", [P, 2, R]) for j in range(2)]
        q1 = [s.sb(f"q1_{j}", [P, S], F32R) for j in range(2)]
        q2 = [s.sb(f"q2_{j}", [R + 1, S], F32R) for j in range(2)]
        k1 = [s.sb(f"k1_{j}", [P, SK], F32R) for j in range(2)]
        k2 = [s.sb(f"k2_{j}", [R + 1, SK], F32R) for j in range(2)]
        nmax = [s.sb(f"nmax{j}", [P, TB]) for j in range(2)]
        probs = [s.sb(f"probs{j}", [P, LT, S]) for j in range(2)]
        hq = probs[0][:, 0:TB, :]
        rot = probs[0][:, TB:TB + 2, :].rearrange("p a (c d) -> p (a c) d", d=DC)
        cosT = probs[1][:, 0:2, :].rearrange("p a (c d) -> p (a c) d", d=DC)
        sinT = probs[1][:, 2:4, :].rearrange("p a (c d) -> p (a c) d", d=DC)
        psum_p = [s.sb(f"psum_p{j}", [P, S]) for j in range(2)]
        rsum = [s.sb(f"rsum{j}", [P, TB]) for j in range(2)]
        rsum_row = s.sb("rsum_row", [P, S])
        ctxT = s.sb("ctxT", [P, H0, S])
        misc = s.ps("misc")
        ps_k = s.ps("ps_k")
        ps_max = s.ps("ps_max", [P, 2, HALF])
        ps_s = [s.ps(f"ps_s{j}") for j in range(2)]
        ps_o = [s.ps(f"ps_o{j}") for j in range(2)]
        tab_in, ctx_in, roped, kvT_tr, kvT_made = (s.sem(n) for n in ("tab_in", "ctx_in", "roped", "kvT_tr", "kvT_made"))
        ln_var, ln_std, ln_seq, hq_made, hq_tr, hqT_made = (s.sem(n) for n in ("ln_var", "ln_std", "ln_seq", "hq_made", "hq_tr", "hqT_made"))
        staged, q_made, q_high, q_low = (s.sem(n) for n in ("staged", "q_made", "q_high", "q_low"))
        k_made, k_high, k_low = (s.sem(n) for n in ("k_made", "k_high", "k_low"))
        smax, maxed, nm_row, nm_put = (s.sem(n) for n in ("smax", "maxed", "nm_row", "nm_put"))
        s_made, p_made, p_seq, o_made, sum_made, sum_rec = (s.sem(n) for n in ("s_made", "p_made", "p_seq", "o_made", "sum_made", "sum_rec"))
        row_made, row_put, c_made, y_made, y_added = (s.sem(n) for n in ("row_made", "row_put", "c_made", "y_made", "y_added"))
        ones_made = s.sem("ones_made")
        block = s.block()
        HP = H0 // 2

        @block.sync
        def _(sp):
            sp.dma_start(cosT, g["cos"]).then_inc(tab_in, 16)
            sp.dma_start(sinT, g["sin"]).then_inc(tab_in, 16)
            sp.dma_start(ctx[:], g["ctx"][0:SK, :].rearrange("(l p) d -> p l d", p=P)).then_inc(ctx_in, 16)
            with sp.Fori(1, B) as b:
                sp.wait_ge(roped, b * 5)
                sp.dma_start(ctx[:], g["ctx"][bass.ds(b * SK, SK), :].rearrange("(l p) d -> p l d", p=P)).then_inc(ctx_in, 16)
                sp.wait_ge(c_made, b * H0 + 1)
                sp.dma_start(cosT, g["cos"]).then_inc(tab_in, 16)
                sp.dma_start(sinT, g["sin"]).then_inc(tab_in, 16)

        @block.gpsimd
        def _(pool):
            for j in range(2):
                pool.memset(k2[j][R:R + 1, :].bitcast(F32), 1.0).then_inc(ones_made, 1)
            with pool.Fori(0, B) as b:
                with pool.Fori(0, HP) as hp:
                    it = b * HP + hp
                    for j in range(2):
                        if j == 0:
                            pool.wait_ge(k_made, it * 4 + 1)
                        pool.tensor_copy(was[j][:, :, 0, :], t.wa[:, bass.ds(hp * 2 + j, 1), :, :].rearrange("p o k r -> p (o k) r")).then_inc(staged, 1)
                        pool.tensor_copy(was[j][:, :, 1, :], t.wa[:, bass.ds(hp * 2 + j, 1), :, :].rearrange("p o k r -> p (o k) r")).then_inc(staged, 1)
                        for c in range(2):
                            pool.tensor_copy(wks[j][:, c, :], t.wkr[:, bass.ds(hp * 2 + j, 1), :].rearrange("p o r -> p (o r)")).then_inc(staged, 1)
                    for j in range(2):
                        i = it * 2 + j
                        pool.wait_ge(p_made, i * LT + 2)
                        pool.wait_ge(sum_made, it * 2 + 1)
                        pool.tensor_tensor(psum_p[j][:], probs[j][:, 0, :], probs[j][:, 1, :], ALU.add).then_inc(p_seq, 1)
                        for l in range(2, LT):
                            pool.wait_ge(p_made, i * LT + l + 1)
                            pool.wait_ge(p_seq, i * (LT - 1) + l - 1)
                            pool.tensor_tensor(psum_p[j][:], psum_p[j][:], probs[j][:, l, :], ALU.add).then_inc(p_seq, 1)

        @block.tensor
        def _(pe):
            pe.wait_ge(ones_made, 2)
            pe.sem_inc(k_made, 1)
            pe.sem_inc(row_put, 1)
            pe.sem_inc(c_made, 1)
            pe.sem_inc(y_added, 1)
            pe.sem_inc(sum_made, 1)
            with pe.Fori(0, B) as b:
                for k in range(KD):
                    pe.wait_ge(hq_made, b * TB + TB)
                    if k == 0:
                        pe.wait_ge(y_added, b * TB + 1)
                    if k >= 2:
                        pe.wait_ge(hqT_made, b * KD + k - 1)
                    for tt in range(TB):
                        tr = pe.transpose(ps_s[k % 2][:, tt * P:(tt + 1) * P], hq[:, tt, k * P:(k + 1) * P], t.ident[:])
                    tr.then_inc(hq_tr, 1)
                pe.wait_ge(roped, b * 5 + 5)
                pe.wait_ge(c_made, b * H0 + 1)
                for half in range(2):
                    for l in range(4):
                        tr = pe.transpose(ps_o[half][:, l * P:(l + 1) * P], kv[:, half * 4 + l, :], t.ident[:])
                    tr.then_inc(kvT_tr, 1)
                with pe.Fori(0, HP) as hp:
                    it = b * HP + hp
                    for j in range(2):
                        i = it * 2 + j
                        pe.wait_ge(staged, i * 4 + 4)
                        if j == 0:
                            pe.wait_ge(row_put, it * 2 + 1)
                            pe.wait_ge(hqT_made, b * KD + KD)
                            pe.wait_ge(kvT_made, b * 2 + 2)
                        if j == 1:
                            pe.wait_ge(q_low, i)
                        for k in range(KD):
                            mm = pe.matmul(misc[:], was[j][:, k, :, :].rearrange("p c r -> p (c r)"), hqT[:, k, :], start=k == 0, stop=k == KD - 1)
                        mm.then_inc(q_made, 1)
                        for half in range(2):
                            if j or half:
                                pe.wait_ge(k_low, i * 2 + half)
                            pe.matmul(ps_k[:], wks[j][:].rearrange("p c r -> p (c r)"), kvT[:, half * HALF:(half + 1) * HALF],
                                      start=True, stop=True).then_inc(k_made, 1)
                        pe.wait_ge(q_low, i + 1)
                        pe.wait_ge(k_high, i * 2 + 2)
                        for st in range(TB):
                            if j or st:
                                pe.wait_ge(maxed, i * TB + st)
                            for half in range(2):
                                mm = pe.matmul(ps_max[:, half, :], q1[j][:, st * P:(st + 1) * P], k1[j][:, half * HALF:(half + 1) * HALF],
                                               start=True, stop=True)
                            mm.then_inc(smax, 1)
                    for j in range(2):
                        i = it * 2 + j
                        pe.wait_ge(maxed, i * TB + TB)
                        if j == 1:
                            pe.wait_ge(nm_put, i)
                        for st in range(TB):
                            mm = pe.matmul(misc[0:1, st * P:(st + 1) * P], nmax[j][:, st:st + 1], t.ident[:], start=True, stop=True)
                        mm.then_inc(nm_row, 1)
                    for j in range(2):
                        i = it * 2 + j
                        pe.wait_ge(nm_put, i + 1)
                        if j == 0:
                            pe.wait_ge(c_made, it * 2 + 1)
                        pe.wait_ge(k_low, i * 2 + 2)

                        def scores(l):
                            if j or l >= 2:
                                pe.wait_ge(p_made, i * LT + l - 1)
                            pe.matmul(ps_s[l % 2][:], k1[j][:, l * P:(l + 1) * P], q1[j][:], start=True, stop=False)
                            pe.matmul(ps_s[l % 2][:], k2[j][:, l * P:(l + 1) * P], q2[j][:], start=False, stop=True).then_inc(s_made, 1)

                        scores(0)
                        scores(1)
                        for l in range(LT):
                            pe.wait_ge(p_made, i * LT + l + 1)
                            mm = pe.matmul(ps_o[j][:], kv[:, l, :], probs[j][:, l, :], start=l == 0, stop=l == LT - 1)
                            if l == LT - 1:
                                mm.then_inc(o_made, 1)
                            if l + 2 < LT:
                                scores(l + 2)
                    for j in range(2):
                        i = it * 2 + j
                        pe.wait_ge(p_seq, i * (LT - 1) + LT - 1)
                        if j == 1:
                            pe.wait_ge(row_put, i + 1)
                        for st in range(TB):
                            mm = pe.matmul(misc[:, st:st + 1], psum_p[j][:, st * P:(st + 1) * P], t.ones[:, 0:1], start=True, stop=True)
                        mm.then_inc(sum_made, 1)
                        pe.wait_ge(sum_rec, i + 1)
                        for st in range(TB):
                            mm = pe.matmul(misc[:, st * P:(st + 1) * P], rsum[j][:, st:st + 1].to_broadcast([P, P]), t.ident[:], start=True, stop=True)
                        mm.then_inc(row_made, 1)
                for tt in range(TB):
                    if tt >= 2:
                        pe.wait_ge(y_added, b * TB + tt)
                    pe.wait_ge(c_made, b * H0 + H0 + 1)
                    for h in range(H0):
                        mm = pe.matmul(ps_s[tt % 2][:], ctxT[:, h, tt * P:(tt + 1) * P], t.mo[:, h, :], start=h == 0, stop=h == H0 - 1)
                    mm.then_inc(y_made, 1)

        @block.scalar
        def _(act):
            with act.Fori(0, B) as b:
                act.wait_ge(ln_var, b + 1)
                act.activation(std[:], mv[:, :, 1], ACT.Sqrt, bias=t.ln_eps[:]).then_inc(ln_std, 1)
                for k in range(KD):
                    act.wait_ge(hq_tr, b * KD + k + 1)
                    act.copy(hqT[:, k, :], ps_s[k % 2][:]).then_inc(hqT_made, 1)
                for half in range(2):
                    act.wait_ge(kvT_tr, b * 2 + half + 1)
                    act.copy(kvT[:, half * HALF:(half + 1) * HALF], ps_o[half][:]).then_inc(kvT_made, 1)
                with act.Fori(0, HP) as hp:
                    it = b * HP + hp
                    for j in range(2):
                        i = it * 2 + j
                        act.wait_ge(q_made, i + 1)
                        act.copy(q1[j][:], misc[:])
                        act.copy(q2[j][0:R, :], misc[0:R, :]).then_inc(q_high, 1)
                        for half in range(2):
                            act.wait_ge(k_made, i * 2 + half + 2)
                            act.copy(k1[j][:, half * HALF:(half + 1) * HALF], ps_k[:]).then_inc(k_high, 1)
                    for j in range(2):
                        i = it * 2 + j
                        act.wait_ge(nm_row, i + 1)
                        act.copy(q2[j][R:R + 1, :], misc[0:1, :]).then_inc(nm_put, 1)
                    for j in range(2):
                        i = it * 2 + j
                        for l in range(LT):
                            act.wait_ge(s_made, i * LT + l + 1)
                            act.activation(probs[j][:, l, :], ps_s[l % 2][:], ACT.Exp).then_inc(p_made, 1)
                    for j in range(2):
                        i = it * 2 + j
                        act.wait_ge(row_made, i + 1)
                        if j:
                            act.wait_ge(c_made, i + 1)
                        act.copy(rsum_row[:], misc[:]).then_inc(row_put, 1)

        @block.vector
        def _(dve):
            with dve.Fori(0, B) as b:
                for tt in range(TB):
                    st_ = dve.bn_stats(stats[:, tt, :], t.x[:, bass.ds(b * TB + tt, 1), :].rearrange("p o d -> p (o d)"))
                    st_.then_inc(ln_seq, 1)
                dve.wait_ge(ln_seq, b * (TB + 1) + TB)
                dve.memset(rstd[:], 0.0)
                for tt in range(TB):
                    ag = dve.bn_aggr(mv[:, tt, :], stats[:, tt, :])
                ag.then_inc(ln_var, 1)
                dve.wait_ge(ln_std, b + 1)
                dve.reciprocal(rstd[:], std[:]).then_inc(ln_seq, 1)
                dve.wait_ge(ln_seq, b * (TB + 1) + TB + 1)
                for tt in range(TB):
                    dve.tensor_scalar(hq[:, tt, :], t.x[:, bass.ds(b * TB + tt, 1), :].rearrange("p o d -> p (o d)"), mv[:, tt, 0:1], rstd[:, tt:tt + 1],
                                      ALU.subtract, ALU.mult).then_inc(hq_made, 1)
                dve.wait_ge(tab_in, b * 32 + 32)
                dve.wait_ge(ctx_in, b * 16 + 16)
                dve.tensor_tensor(rot[:, :, 0:DC // 2], ctx[:, :, DC // 2:DC], sinT[:, :, 0:DC // 2], ALU.mult).then_inc(roped, 1)
                dve.tensor_tensor(rot[:, :, DC // 2:DC], ctx[:, :, 0:DC // 2], sinT[:, :, DC // 2:DC], ALU.mult).then_inc(roped, 1)
                dve.tensor_tensor(kv[:], ctx[:], cosT[:], ALU.mult).then_inc(roped, 1)
                dve.wait_ge(roped, b * 5 + 3)
                dve.tensor_tensor(kv[:, :, 0:DC // 2], kv[:, :, 0:DC // 2], rot[:, :, 0:DC // 2], ALU.subtract).then_inc(roped, 1)
                dve.tensor_tensor(kv[:, :, DC // 2:DC], kv[:, :, DC // 2:DC], rot[:, :, DC // 2:DC], ALU.add).then_inc(roped, 1)
                with dve.Fori(0, HP) as hp:
                    it = b * HP + hp
                    for j in range(2):
                        i = it * 2 + j
                        dve.wait_ge(q_high, i + 1)
                        dve.tensor_tensor(q1[j][R:P, :], misc[R:P, :], q1[j][R:P, :].bitcast(F32), ALU.subtract).then_inc(q_low, 1)
                        for half in range(2):
                            dve.wait_ge(k_high, i * 2 + half + 1)
                            hs = slice(half * HALF, (half + 1) * HALF)
                            dve.tensor_tensor(k2[j][0:R, hs], ps_k[0:R, :], k1[j][0:R, hs].bitcast(F32), ALU.subtract).then_inc(k_low, 1)
                        for st in range(TB):
                            dve.wait_ge(smax, i * TB + st + 1)
                            dve.tensor_reduce(nmax[j][:, st:st + 1], ps_max[:], AX.XY, ALU.max, negate=True).then_inc(maxed, 1)
                    for j in range(2):
                        i = it * 2 + j
                        dve.wait_ge(sum_made, i + 2)
                        dve.reciprocal(rsum[j][:], misc[:, 0:TB]).then_inc(sum_rec, 1)
                        dve.wait_ge(row_put, i + 2)
                        dve.wait_ge(o_made, i + 1)
                        dve.tensor_tensor(ctxT[:, bass.ds(hp * 2 + j, 1), :].rearrange("p o s -> p (o s)"), ps_o[j][:], rsum_row[:], ALU.mult).then_inc(c_made, 1)
                for tt in range(TB):
                    dve.wait_ge(y_made, b * TB + tt + 1)
                    xt = t.x[:, bass.ds(b * TB + tt, 1), :].rearrange("p o d -> p (o d)")
                    dve.tensor_tensor(xt, ps_s[tt % 2][:], xt, ALU.add).then_inc(y_added, 1)


def route(nc, t, g, m):
    E, K, cap = m.E, m.K, m.cap
    F = NT * K if m.choice_major else NT
    KT = K * NT
    SLOTS = E * cap
    GT = SLOTS // P
    with Scope(nc, f"rt{m.name}") as s:
        xn = s.sb("xn", [P, NT, D])
        stats, mv = s.sb("stats", [P, NT, 6]), s.sb("mv", [P, NT, 2])
        std, rstd = s.sb("std", [P, NT]), s.sb("rstd", [P, NT])
        wr = s.sb("wr", [P, KD, E])
        xT = [s.sb(f"xT{j}", [P, KD * P]) for j in range(2)]
        lg, ex = s.sb("lg", [P, NT, E]), s.sb("ex", [P, NT, E])
        v8, i8 = s.sb("v8", [P, NT, 8]), s.sb("i8", [P, NT, 8], U32)
        idxf = s.sb("idxf", [P, K, NT])
        dv = s.sb("dv", [P, K, NT])
        den = s.sb("den", [P, NT])
        iota_e = s.sb("iota_e", [P, E])
        tri = s.sb("tri", [P, P])
        masks = s.sb("masks", [P, KT, E])
        queue = masks if m.choice_major else s.sb("queue", [P, NT, E])
        tot = s.sb("tot", [P, F, E])
        pre = [s.sb(f"pre{j}", [P, F, E]) for j in range(2)]
        rank = s.sb("rank", [P, KT])
        sel = s.sb("sel", [P, KT, E])
        keep, base, slotf = s.sb("keep", [P, KT]), s.sb("base", [P, KT]), s.sb("slotf", [P, KT])
        dslot = s.sb("dslot", [P, KT], I32)
        tokid = s.sb("tokid", [P, NT])
        zero = s.sb("zero", [P, P])
        tab = s.sb("tab", [P, P])
        junk = s.sb("junk", [P, 2, D])
        ps_tr = [s.ps(f"ps_tr{j}") for j in range(2)]
        ps_l, ps_tot, ps_rk, ps_tab = (s.ps(n) for n in ("ps_l", "ps_tot", "ps_rk", "ps_tab"))
        w_in, consts, var_ready, std_ready, chain = (s.sem(n) for n in ("w_in", "consts", "var", "std", "chain"))
        xn_made, xn_out, tr_made, xT_made, l_made = (s.sem(n) for n in ("xn_made", "xn_out", "tr_made", "xT_made", "l_made"))
        ex_in, ex_made, q_ready, q_summed, slots_ready = (s.sem(n) for n in ("ex_in", "ex_made", "q_ready", "q_summed", "slots_ready"))
        scattered, tab_in, tab_tr, zeroed = (s.sem(n) for n in ("scattered", "tab_in", "tab_tr", "zeroed"))
        block = s.block()

        @block.sync
        def _(sp):
            sp.dma_start(wr[:], g[m.router]).then_inc(w_in, 16)
            if m.rms:
                sp.dma_start(t.norm_w[:], g["norm_w"]).then_inc(w_in, 16)
            sp.wait_ge(consts, 2)
            sp.dma_start(m.table.rearrange("(n p) o -> n (p o)", p=P), zero[0:GT, :]).then_inc(zeroed, 16)
            for tt in range(NT):
                sp.wait_ge(xn_made, tt + 1)
                sp.dma_start(m.xn_dram[tt * P:(tt + 1) * P, :], xn[:, tt, :]).then_inc(xn_out, 16)
            sp.wait_ge(scattered, 16 * KT)
            sp.dma_start(tab[0:GT, :], m.table.rearrange("(n p) o -> n (p o)", p=P)).then_inc(tab_in, 16)
            sp.wait_ge(xn_out, 16 * NT)
            sp.wait_ge(tab_in, 16)

        @block.gpsimd
        def _(pool):
            pool.memset(t.gidx[:], 0).then_inc(consts, 1)
            pool.memset(zero[:], 0.0).then_inc(consts, 1)
            pool.iota(iota_e[:], pattern=[[1, E]], base=0, channel_multiplier=0, allow_small_or_imprecise_dtypes=True).then_inc(consts, 1)
            pool.iota(tokid[:], pattern=[[P, NT]], base=0, channel_multiplier=1, allow_small_or_imprecise_dtypes=True).then_inc(consts, 1)
            pool.memset(tri[:], 1.0).then_inc(consts, 1)
            pool.wait_ge(consts, 5)
            pool.affine_select(out=tri[:], in_=tri[:], compare_op=ALU.is_gt, fill=0.0, base=0,
                               pattern=[[1, P]], channel_multiplier=-1).then_inc(consts, 1)
            pool.wait_ge(slots_ready, 1)
            pool.wait_ge(zeroed, 16)
            for c in range(KT):
                pool.indirect_dma_start(out=m.table, out_offset=bass.IndirectOffsetOnAxis(ap=dslot[:, c:c + 1], axis=0),
                                        in_=tokid[:, c % NT:c % NT + 1], in_offset=None,
                                        bounds_check=SLOTS - 1, oob_is_err=False).then_inc(scattered, 16)
            pool.wait_ge(scattered, 16 * KT)

        @block.tensor
        def _(pe):
            pe.wait_ge(w_in, 16)
            for tt in range(NT + 1):
                if tt < NT:
                    pe.wait_ge(xn_made, tt + 1)
                    if tt >= 2:
                        pe.wait_ge(xT_made, tt - 1)
                    for k in range(KD):
                        mm = pe.transpose(ps_tr[tt % 2][:, k * P:(k + 1) * P], xn[:, tt, k * P:(k + 1) * P], t.ident[:])
                    mm.then_inc(tr_made, 1)
                if tt >= 1:
                    pe.wait_ge(xT_made, tt)
                    for k in range(KD):
                        mm = pe.matmul(ps_l[:, (tt - 1) * E:tt * E], xT[(tt - 1) % 2][:, k * P:(k + 1) * P], wr[:, k, :], start=k == 0, stop=k == KD - 1)
                    mm.then_inc(l_made, 1)
            pe.wait_ge(q_ready, 1)
            pe.wait_ge(consts, 6)
            pe.matmul(ps_tot[:, 0:F * E], t.ones[:], queue[:, 0:F, :].rearrange("p f e -> p (f e)"), start=True, stop=True).then_inc(q_summed, 1)
            pe.matmul(ps_rk[:, 0:F * E], tri[:], queue[:, 0:F, :].rearrange("p f e -> p (f e)"), start=True, stop=True).then_inc(q_summed, 1)
            pe.wait_ge(tab_in, 16)
            pe.transpose(ps_tab[:, 0:GT], tab[0:GT, :], t.ident[0:GT, 0:GT]).then_inc(tab_tr, 1)

        @block.scalar
        def _(act):
            act.wait_ge(var_ready, 1)
            act.activation(std[:], mv[:, :, 1], ACT.Sqrt, bias=t.ln_eps[:]).then_inc(std_ready, 1)
            if m.rms:
                for tt in range(NT):
                    act.wait_ge(chain, m.z_made + tt)
                    if tt >= 2:
                        act.wait_ge(ex_made, tt - 1)
                    act.activation(junk[:, tt % 2, :], xn[:, tt, :], ACT.Square, accum_out=den[:, tt:tt + 1]).then_inc(ex_made, 1)
                act.wait_ge(ex_made, NT)
                act.activation(std[:], den[:], ACT.Sqrt, bias=t.rms_eps[:], scale=1.0 / D).then_inc(std_ready, 1)
            for tt in range(NT):
                act.wait_ge(tr_made, tt + 1)
                if tt >= 2:
                    act.wait_ge(l_made, tt - 1)
                act.copy(xT[tt % 2][:], ps_tr[tt % 2][:]).then_inc(xT_made, 1)
            act.wait_ge(ex_in, 1)
            act.activation(ex[:], lg[:], ACT.Exp).then_inc(ex_made, 1)
            act.activation(dv[:], dv[:], ACT.Exp).then_inc(ex_made, 1)

        @block.vector
        def _(dve):
            n = [0]

            def link(ins):
                n[0] += 1
                ins.then_inc(chain, 1)
                dve.wait_ge(chain, n[0])

            for tt in range(NT):
                ins = dve.bn_stats(stats[:, tt, :], t.x[:, tt, :])
            link(ins)
            for tt in range(NT):
                ins = dve.bn_aggr(mv[:, tt, :], stats[:, tt, :])
            ins.then_inc(var_ready, 1)
            dve.wait_ge(std_ready, 1)
            link(dve.reciprocal(rstd[:], std[:]))
            assert n[0] == 2
            for tt in range(NT):
                ins = dve.tensor_scalar(xn[:, tt, :], t.x[:, tt, :], mv[:, tt, 0:1], rstd[:, tt:tt + 1], ALU.subtract, ALU.mult)
                if m.rms:
                    n[0] += 1
                    ins.then_inc(chain, 1)
                else:
                    ins.then_inc(xn_made, 1)
            if m.rms:
                dve.wait_ge(chain, n[0])
                link(dve.tensor_tensor(t.x[:], t.x[:], xn[:], ALU.add))
                dve.wait_ge(std_ready, 2)
                link(dve.reciprocal(rstd[:], std[:]))
                dve.wait_ge(w_in, 32)
                for tt in range(NT):
                    dve.scalar_tensor_tensor(out=xn[:, tt, :], in0=xn[:, tt, :], scalar=rstd[:, tt:tt + 1], in1=t.norm_w[:],
                                             op0=ALU.mult, op1=ALU.mult).then_inc(xn_made, 1)
            dve.wait_ge(l_made, NT)
            link(dve.tensor_copy(lg[:], ps_l[:, 0:NT * E].rearrange("p (t e) -> p t e", e=E)))
            for tt in range(NT):
                ins = dve.max(v8[:, tt, :], lg[:, tt, :])
            link(ins)
            for tt in range(NT):
                ins = dve.max_index(i8[:, tt, :], v8[:, tt, :], lg[:, tt, :])
            link(ins)
            link(dve.tensor_copy(idxf[:], i8[:, :, 0:K].rearrange("p t k -> p k t")))
            dve.tensor_tensor(dv[:], v8[:, :, 0:K].rearrange("p t k -> p k t"), v8[:, :, 0:1].rearrange("p t o -> p o t").to_broadcast([P, K, NT]), ALU.subtract)
            dve.tensor_tensor(lg[:], lg[:], v8[:, :, 0:1].to_broadcast([P, NT, E]), ALU.subtract).then_inc(ex_in, 1)
            dve.wait_ge(consts, 4)
            link(dve.tensor_tensor(masks[:], iota_e[:].rearrange("p (o e) -> p o e", o=1).to_broadcast([P, KT, E]),
                                   idxf[:].rearrange("p k (t o) -> p (k t) o", o=1).to_broadcast([P, KT, E]), ALU.is_equal))
            if not m.choice_major:
                link(dve.tensor_tensor(queue[:], masks[:, 0:NT, :], masks[:, NT:2 * NT, :], ALU.add))
                for k in range(2, K):
                    link(dve.tensor_tensor(queue[:], queue[:], masks[:, k * NT:(k + 1) * NT, :], ALU.add))
            dve.sem_inc(q_ready, 1)
            dve.wait_ge(ex_made, 2 + (NT if m.rms else 0))
            if m.renorm:
                link(dve.tensor_reduce(den[:], dv[:].rearrange("p k t -> p t k"), AX.X, ALU.add))
            else:
                link(dve.tensor_reduce(den[:], ex[:], AX.X, ALU.add))
            link(dve.reciprocal(den[:], den[:]))
            link(dve.tensor_tensor(t.gate[:, 0:KT].rearrange("p (k t) -> p k t", t=NT), dv[:], den[:].rearrange("p (o t) -> p o t", o=1).to_broadcast([P, K, NT]), ALU.mult))
            dve.wait_ge(q_summed, 2)
            link(dve.tensor_copy(tot[:], ps_tot[:, 0:F * E].rearrange("p (f e) -> p f e", e=E)))
            src, step, j = tot, 1, 0
            while step < F:
                dve.tensor_copy(pre[j][:, 0:step, :], src[:, 0:step, :])
                link(dve.tensor_tensor(pre[j][:, step:F, :], src[:, step:F, :], src[:, 0:F - step, :], ALU.add))
                src, step, j = pre[j], step * 2, 1 - j
            link(dve.tensor_tensor(tot[:], src[:], tot[:], ALU.subtract))
            link(dve.tensor_tensor(tot[:], ps_rk[:, 0:F * E].rearrange("p (f e) -> p f e", e=E), tot[:], ALU.add))
            if m.choice_major:
                link(dve.tensor_tensor(sel[:], masks[:], tot[:], ALU.mult))
            else:
                for k in range(K):
                    ins = dve.tensor_tensor(sel[:, k * NT:(k + 1) * NT, :], masks[:, k * NT:(k + 1) * NT, :], tot[:], ALU.mult)
                link(ins)
            link(dve.tensor_reduce(rank[:], sel[:], AX.X, ALU.add))
            link(dve.tensor_scalar(base[:], idxf[:].rearrange("p k t -> p (k t)"), float(cap), None, ALU.mult))
            link(dve.tensor_scalar(keep[:], rank[:], float(cap), None, ALU.is_lt))
            link(dve.tensor_scalar(slotf[:], keep[:], -float(2 * SLOTS), float(2 * SLOTS), ALU.mult, ALU.add))
            link(dve.tensor_tensor(slotf[:], slotf[:], rank[:], ALU.add))
            link(dve.tensor_tensor(slotf[:], slotf[:], base[:], ALU.add))
            link(dve.tensor_copy(dslot[:], slotf[:]))
            dve.sem_inc(slots_ready, 1)
            link(dve.tensor_scalar(rank[:], rank[:], float(cap - 1), None, ALU.min))
            link(dve.tensor_tensor(rank[:], rank[:], base[:], ALU.add))
            link(dve.tensor_copy(t.slot[:, 0:KT], rank[:]))
            if m.drop_weight:
                link(dve.tensor_tensor(t.gate[:, 0:KT], t.gate[:, 0:KT], keep[:], ALU.mult))
            dve.wait_ge(tab_tr, 1)
            link(dve.tensor_copy(t.gidx[:, 0:GT], ps_tab[:, 0:GT]))
            if m.shared:
                link(dve.tensor_copy(t.gidx[:, GT:GT + NT], tokid[:]))


def experts(nc, t, g, m):
    NE = m.E + (NSH if m.shared else 0)
    cap, I = m.cap, m.I
    CT = cap // P
    CH = cap // m.chunks
    IS = [min(P, I - i) for i in range(0, I, P)]
    IT = len(IS)
    NGU = IT * m.chunks
    with Scope(nc, f"ex{m.name}") as s:
        wgu = [s.sb(f"wgu{j}", [P, KD, 2 * I]) for j in range(2)]
        wd = [s.sb(f"wd{j}", [P, IT, D]) for j in range(2)]
        idx = [s.sb(f"idx{j}", [P, CT], I32) for j in range(2)]
        xg = [s.sb(f"xg{j}", [P, CT, D]) for j in range(2)]
        xgT = [s.sb(f"xgT{j}", [P, KD, cap]) for j in range(2)]
        sg = [s.sb(f"sg{j}", [P, CH]) for j in range(2)]
        hT = [s.sb(f"hT{j}", [P, IT, cap]) for j in range(2)]
        y = [s.sb(f"y{c}", [P, D]) for c in range(CT)]
        ps_tr = [s.ps(f"ps_tr{j}") for j in range(2)]
        ps_g = [s.ps(f"ps_g{j}") for j in range(2)]
        ps_u = [s.ps(f"ps_u{j}") for j in range(2)]
        ps_y = [s.ps(f"ps_y{j}") for j in range(2)]
        turn, turned = s.sb("turn", [P, 2]), s.sem("turned")
        w_in = [s.sem(f"w_in{j}") for j in range(2)]
        x_in = [s.sem(f"x_in{j}") for j in range(2)]
        idx_made, tr_made, xT_made, gu_made, sg_made, h_made = (s.sem(n) for n in ("idx_made", "tr_made", "xT_made", "gu_made", "sg_made", "h_made"))
        y_made, y_put = s.sem("y_made"), s.sem("y_put")
        y_out = [s.sem(f"y_out{c}") for c in range(CT)]
        block = s.block()
        WD = 16 * (2 if IS[-1] == P else 3)

        @block.sync
        def _(sp):
            def load_weights(e, j):
                sp.dma_start(wgu[j][:], g[m.wgu][bass.ds(e, 1), :, :, :].rearrange("o p k i -> (o p) k i")).then_inc(w_in[j], 16)
                full = I // P * P
                sp.dma_start(wd[j][:, 0:I // P, :], g[m.wd][bass.ds(e, 1), 0:full, :].rearrange("o (i p) d -> (o p) i d", p=P)).then_inc(w_in[j], 16)
                if full < I:
                    sp.dma_start(wd[j][0:I - full, IT - 1, :], g[m.wd][bass.ds(e, 1), full:I, :].rearrange("o p d -> (o p) d")).then_inc(w_in[j], 16)

            def store(e, j):
                for c in range(CT):
                    sp.wait_ge(y_put, e * CT + c + 3)
                    sp.dma_start(m.y_dram[bass.ds((e * CT + c) * P, P), :], y[c][:]).then_inc(y_out[c], 16)

            sp.sem_inc(y_made, 1)
            for c in range(CT):
                sp.sem_inc(y_out[c], 16)
            load_weights(0, 0)
            with sp.Fori(0, NE // 2 - 1) as ep:
                sp.wait_ge(y_made, ep * (2 * CT) + 1)
                load_weights(ep * 2 + 1, 1)
                store(ep * 2, 0)
                sp.wait_ge(y_made, ep * (2 * CT) + CT + 1)
                load_weights(ep * 2 + 2, 0)
                store(ep * 2 + 1, 1)
            sp.wait_ge(y_made, (NE - 2) * CT + 1)
            load_weights(NE - 1, 1)
            store(NE - 2, 0)
            store(NE - 1, 1)
            for c in range(CT):
                sp.wait_ge(y_out[c], 16 * NE + 16)

        @block.gpsimd
        def _(pool):
            last_token = pool.to_reg(N - 1)
            pool.memset(turn[:], 0.0).then_inc(turned, 1)
            pool.wait_ge(turned, 1)
            with pool.Fori(0, NE // 2) as ep:
                for j in range(2):
                    e = ep * 2 + j
                    pool.wait_ge(idx_made, e + 1)
                    pool.wait_ge(turned, e + 1)
                    pool.tensor_tensor(turn[:, 1:2], turn[:, 0:1], turn[:, 0:1], ALU.add).then_inc(turned, 1)
                    for c in range(CT):
                        pool.indirect_dma_start(out=xg[j][:, c, :], out_offset=None, in_=m.xn_dram,
                                                in_offset=bass.IndirectOffsetOnAxis(ap=idx[j][:, c:c + 1], axis=0),
                                                bounds_check=last_token, oob_is_err=False).then_inc(x_in[j], 16)

        @block.tensor
        def _(pe):
            def transposes(ep, j):
                e = ep * 2 + j
                pe.wait_ge(x_in[j], ep * (16 * CT) + 16 * CT)
                for c in range(CT):
                    i = e * CT + c
                    pe.wait_ge(xT_made, i + 1)
                    for k in range(KD):
                        mm = pe.transpose(ps_tr[(j * CT + c) % 2][:, k * P:(k + 1) * P], xg[j][:, c, k * P:(k + 1) * P], t.ident[:])
                    mm.then_inc(tr_made, 1)

            def gate_up(ep, j):
                e = ep * 2 + j
                pe.wait_ge(w_in[j], ep * WD + WD)
                pe.wait_ge(xT_made, e * CT + CT + 2)
                for a in range(NGU):
                    it, ch = a // m.chunks, a % m.chunks
                    cols = slice(ch * CH, (ch + 1) * CH)
                    pe.wait_ge(h_made, e * NGU + a + 1)
                    for base, ps in ((0, ps_g), (I, ps_u)):
                        for k in range(KD):
                            mm = pe.matmul(ps[a % 2][0:IS[it], 0:CH], wgu[j][:, k, base + it * P:base + it * P + IS[it]], xgT[j][:, k, cols],
                                           start=k == 0, stop=k == KD - 1)
                    mm.then_inc(gu_made, 1)

            def down(ep, j):
                e = ep * 2 + j
                pe.wait_ge(h_made, e * NGU + NGU + 2)
                for c in range(CT):
                    pe.wait_ge(y_put, e * CT + c + 1)
                    for it in range(IT):
                        mm = pe.matmul(ps_y[(j * CT + c) % 2][:], hT[j][0:IS[it], it, c * P:(c + 1) * P], wd[j][0:IS[it], it, :],
                                       start=it == 0, stop=it == IT - 1)
                    mm.then_inc(y_made, 1)

            pe.sem_inc(xT_made, 2)
            pe.sem_inc(h_made, 2)
            pe.sem_inc(y_put, 2)
            with pe.Fori(0, NE // 2) as ep:
                transposes(ep, 0)
                gate_up(ep, 0)
                transposes(ep, 1)
                down(ep, 0)
                gate_up(ep, 1)
                down(ep, 1)

        @block.scalar
        def _(act):
            def evacuate(ep, j):
                for c in range(CT):
                    i = (ep * 2 + j) * CT + c
                    act.wait_ge(tr_made, i + 1)
                    act.copy(xgT[j][:, :, c * P:(c + 1) * P], ps_tr[(j * CT + c) % 2][:].rearrange("p (k c) -> p k c", c=P)).then_inc(xT_made, 1)

            def silu(ep, j):
                for a in range(NGU):
                    i = (ep * 2 + j) * NGU + a
                    r = IS[a // m.chunks]
                    act.wait_ge(gu_made, i + 1)
                    act.wait_ge(h_made, i + 1)
                    act.activation(sg[a % 2][0:r, :], ps_g[a % 2][0:r, 0:CH], ACT.Silu).then_inc(sg_made, 1)

            with act.Fori(0, NE // 2) as ep:
                evacuate(ep, 0)
                silu(ep, 0)
                evacuate(ep, 1)
                silu(ep, 1)

        @block.vector
        def _(dve):
            def stage_idx(e, j):
                dve.tensor_copy(idx[j][:], t.gidx[:, bass.ds(e * CT, CT)]).then_inc(idx_made, 1)

            def hidden(ep, j):
                for a in range(NGU):
                    i = (ep * 2 + j) * NGU + a
                    it, ch = a // m.chunks, a % m.chunks
                    r = IS[it]
                    dve.wait_ge(sg_made, i + 1)
                    dve.tensor_tensor(hT[j][0:r, it, ch * CH:(ch + 1) * CH], ps_u[a % 2][0:r, 0:CH], sg[a % 2][0:r, :], ALU.mult).then_inc(h_made, 1)

            def put(ep, j):
                for c in range(CT):
                    i = (ep * 2 + j) * CT + c
                    dve.wait_ge(y_made, i + 2)
                    dve.wait_ge(y_out[c], (ep * 2 + j) * 16 + 16)
                    dve.tensor_copy(y[c][:], ps_y[(j * CT + c) % 2][:]).then_inc(y_put, 1)

            for j in range(2):
                stage_idx(j, j)
            with dve.Fori(0, NE // 2) as ep:
                for j in range(2):
                    hidden(ep, j)
                    stage_idx(ep * 2 + j + 2, j)
                    put(ep, j)


def combine(nc, t, g, m):
    K = m.K
    RING = 8
    with Scope(nc, f"co{m.name}") as s:
        row = [s.sb(f"row{r}", [P, D]) for r in range(RING)]
        row_in = [s.sem(f"row_in{r}") for r in range(RING)]
        added = s.sem("added")
        sh, sh_in = (s.sb("sh", [P, NT, D]), s.sem("sh_in")) if m.shared else (None, None)
        block = s.block()
        todo = [(tt, k) for tt in range(NT) for k in range(K)]

        @block.sync
        def _(sp):
            if m.shared:
                first = m.E * m.cap
                sp.dma_start(sh[:], m.y_dram[first:first + N, :].rearrange("(t p) d -> p t d", p=P)).then_inc(sh_in, 16)

        @block.gpsimd
        def _(pool):
            for n, (tt, k) in enumerate(todo):
                if n >= RING:
                    pool.wait_ge(added, n - RING + 1 + m.shared)
                c = k * NT + tt
                pool.indirect_dma_start(out=row[n % RING][:], out_offset=None, in_=m.y_dram,
                                        in_offset=bass.IndirectOffsetOnAxis(ap=t.slot[:, c:c + 1], axis=0),
                                        bounds_check=m.y_rows - 1, oob_is_err=False).then_inc(row_in[n % RING], 16)

        @block.vector
        def _(dve):
            if m.shared:
                dve.wait_ge(sh_in, 16)
                dve.tensor_tensor(t.x[:], t.x[:], sh[:], ALU.add).then_inc(added, 0 + 1)
            for n, (tt, k) in enumerate(todo):
                c = k * NT + tt
                dve.wait_ge(row_in[n % RING], 16 * (n // RING + 1))
                if n or m.shared:
                    dve.wait_ge(added, n + m.shared)
                dve.scalar_tensor_tensor(out=t.x[:, tt, :], in0=row[n % RING][:], scalar=t.gate[:, c:c + 1], in1=t.x[:, tt, :],
                                         op0=ALU.mult, op1=ALU.add).then_inc(added, 1)
            dve.wait_ge(added, len(todo) + m.shared)


def causal_attention(nc, t, g):
    SC = float(np.float32(1.0) / np.sqrt(np.float32(HD)))
    R3 = 3 * HD
    with Scope(nc, "ca") as s:
        wq, wk, wv, wo = s.sb("wq", [P, KD, D]), s.sb("wk", [P, D]), s.sb("wv", [P, D]), s.sb("wo", [P, KD, D])
        ctxT = s.sb("ctxT", [P, S])
        stats, mv = s.sb("stats", [P, TB, 6]), s.sb("mv", [P, TB, 2])
        std, rstd = s.sb("std", [P, TB]), s.sb("rstd", [P, TB])
        hq, hqT = s.sb("hq", [P, TB, D]), s.sb("hqT", [P, KD, S])
        v = s.sb("v", [P, TB, D])
        wqs, wks = s.sb("wqs", [P, KD, P]), s.sb("wks", [P, P])
        vp = [s.sb(f"vp{j}", [P, TB, P]) for j in range(GH)]
        onep = [s.sb(f"onep{j}", [P, P]) for j in range(GH)]
        pick = s.sb("pick", [P, 2, 2, GH, P], F32R)
        pickf = s.sb("pickf", [P, 2, 2, GH, P])
        negf, neg = s.sb("negf", [P, 2, P]), s.sb("neg", [P, 2, P], F32R)
        identr = s.sb("identr", [P, P], F32R)
        qh, ql = s.sb("qh", [P, S], F32R), s.sb("ql", [P, S], F32R)
        kh, kl = s.sb("kh", [P, S], F32R), s.sb("kl", [P, S], F32R)
        qs = [s.sb(f"qs{j}", [R3 + 1, S], F32R) for j in range(GH)]
        ks = [s.sb(f"ks{j}", [R3 + 1, S], F32R) for j in range(GH)]
        nmax = [s.sb(f"nmax{j}", [P, TB]) for j in range(GH)]
        probs = [s.sb(f"probs{j}", [P, TB, S]) for j in range(GH)]
        psum_p = [s.sb(f"psum_p{j}", [P, S]) for j in range(GH)]
        rec = s.sb("rec", [P, S])
        oT = s.sb("oT", [P, NG, S])
        pa, pb, pm, pn = (s.ps(n) for n in ("pa", "pb", "pm", "pn"))
        ps_s = [s.ps(f"ps_s{j}") for j in range(2)]
        ps_o, ps_sum = s.ps("ps_o"), s.ps("ps_sum")
        w_in, ctx_in, consts, made = (s.sem(n) for n in ("w_in", "ctx_in", "consts", "made"))
        ln_seq, ln_var, ln_std, hq_made, hq_tr, hqT_made = (s.sem(n) for n in ("ln_seq", "ln_var", "ln_std", "hq_made", "hq_tr", "hqT_made"))
        v_made, v_put, staged, proj, high, low = (s.sem(n) for n in ("v_made", "v_put", "staged", "proj", "high", "low"))
        stacked, q_put, k_put, smax, maxed, nm_row, nm_put = (s.sem(n) for n in ("stacked", "q_put", "k_put", "smax", "maxed", "nm_row", "nm_put"))
        s_made, p_made, p_seq, o_made, rec_made, o_put, y_made, y_added = (s.sem(n) for n in ("s_made", "p_made", "p_seq", "o_made", "rec_made", "o_put", "y_made", "y_added"))
        block = s.block()

        @block.sync
        def _(sp):
            sp.dma_start(wq[:], g["wq1"]).then_inc(w_in, 16)
            sp.dma_start(wk[:], g["wk1"]).then_inc(w_in, 16)
            sp.dma_start(wv[:], g["wv1"]).then_inc(w_in, 16)
            sp.dma_start(wo[:], g["wo1"]).then_inc(w_in, 16)
            sp.sem_inc(o_put, 1)
            with sp.Fori(0, B) as b:
                sp.wait_ge(o_put, b * NG + 1)
                sp.dma_start(ctxT[:], g["ctxT"][:, bass.ds(b * S, S)]).then_inc(ctx_in, 16)

        @block.gpsimd
        def _(pool):
            pool.memset(pickf[:], 0.0).then_inc(consts, 1)
            pool.memset(negf[:], 0.0).then_inc(consts, 1)
            for j in range(GH):
                pool.memset(vp[j][:], 0.0).then_inc(consts, 1)
                pool.memset(onep[j][:], 0.0).then_inc(consts, 1)
            pool.wait_ge(consts, 2 + 2 * GH)
            for j in range(GH):
                head = slice(j * HD, (j + 1) * HD)
                pool.memset(onep[j][:, head], 1.0).then_inc(consts, 1)
                for x, part, blk in ((0, 0, 0), (0, 1, 1), (0, 0, 2), (1, 0, 0), (1, 0, 1), (1, 1, 2)):
                    pool.tensor_copy(pickf[:, x, part, j, blk * HD:(blk + 1) * HD], t.ident[:, head]).then_inc(consts, 1)
            pool.affine_select(out=negf[:, 0, :], in_=negf[:, 0, :], compare_op=ALU.is_ge, fill=NEG, base=0,
                               pattern=[[-1, P]], channel_multiplier=1).then_inc(consts, 1)
            pool.affine_select(out=negf[:, 1, :], in_=negf[:, 1, :], compare_op=ALU.is_ge, fill=NEG, base=0,
                               pattern=[[1, P]], channel_multiplier=-1).then_inc(consts, 1)
            pool.wait_ge(w_in, 64)
            pool.sem_inc(proj, 1)
            with pool.Fori(0, B) as b:
                with pool.Fori(0, NG) as gr:
                    it = b * NG + gr
                    pool.wait_ge(proj, it * 2 + 1)
                    pool.tensor_copy(wqs[:], wq[:, :, bass.ds(gr * P, P)]).then_inc(staged, 1)
                    pool.tensor_copy(wks[:], wk[:, bass.ds(gr * P, P)]).then_inc(staged, 1)
                    pool.wait_ge(o_put, it + 1)
                    pool.wait_ge(v_put, b * TB + TB)
                    for j in range(GH):
                        pool.tensor_copy(vp[j][:, :, j * HD:(j + 1) * HD], v[:, :, bass.ds(gr * P + j * HD, HD)]).then_inc(staged, 1)
                    for j in range(GH):
                        i = it * GH + j
                        pool.wait_ge(p_made, i * TB + 2)
                        pool.tensor_tensor(psum_p[j][:, 0:P], probs[j][:, 0, 0:P], t.ones[:], ALU.mult).then_inc(p_seq, 1)
                        pool.tensor_tensor(psum_p[j][:, P:S], probs[j][:, 0, P:S], probs[j][:, 1, P:S], ALU.add).then_inc(p_seq, 1)
                        for l in range(2, TB):
                            pool.wait_ge(p_made, i * TB + l + 1)
                            pool.wait_ge(p_seq, i * TB + l)
                            pool.tensor_tensor(psum_p[j][:, l * P:S], psum_p[j][:, l * P:S], probs[j][:, l, l * P:S], ALU.add).then_inc(p_seq, 1)

        @block.tensor
        def _(pe):
            pe.sem_inc(y_added, 2)
            pe.wait_ge(w_in, 64)
            pe.wait_ge(made, 3 + GH)
            with pe.Fori(0, B) as b:
                for k in range(KD):
                    pe.wait_ge(hq_made, b * TB + TB)
                    if k == 0:
                        pe.wait_ge(y_added, b * TB + 2)
                    if k >= 2:
                        pe.wait_ge(hqT_made, b * KD + k - 1)
                    for tt in range(TB):
                        tr = pe.transpose(ps_s[k % 2][:, tt * P:(tt + 1) * P], hq[:, tt, k * P:(k + 1) * P], t.ident[:])
                    tr.then_inc(hq_tr, 1)
                for tt in range(TB):
                    pe.wait_ge(ctx_in, b * 16 + 16)
                    if tt:
                        pe.wait_ge(v_put, b * TB + tt)
                    pe.matmul(pm[:], ctxT[:, tt * P:(tt + 1) * P], wv[:], start=True, stop=True).then_inc(v_made, 1)
                with pe.Fori(0, NG) as gr:
                    it = b * NG + gr

                    def stack(j):
                        i = it * GH + j
                        pe.wait_ge(low, it * 2 + 2)
                        if j:
                            pe.wait_ge(q_put, i)
                            pe.wait_ge(k_put, i)
                        pe.matmul(pa[0:R3, :], pick[:, 0, 0, j, 0:R3], qh[:], start=True, stop=False)
                        pe.matmul(pa[0:R3, :], pick[:, 0, 1, j, 0:R3], ql[:], start=False, stop=True).then_inc(stacked, 1)
                        pe.matmul(pb[0:R3, :], pick[:, 1, 0, j, 0:R3], kh[:], start=True, stop=False)
                        pe.matmul(pb[0:R3, :], pick[:, 1, 1, j, 0:R3], kl[:], start=False, stop=True).then_inc(stacked, 1)
                        pe.wait_ge(q_put, i + 1)
                        pe.wait_ge(k_put, i + 1)
                        for st in range(TB):
                            if j or st:
                                pe.wait_ge(maxed, i * TB + st)
                            w = (st + 1) * P
                            pe.matmul(pm[:, 0:w], qs[j][0:R3, st * P:w], ks[j][0:R3, 0:w], start=True, stop=False)
                            pe.matmul(pm[:, st * P:w], identr[:], neg[:, 0, :], start=False, stop=True).then_inc(smax, 1)

                    def max_row(j):
                        i = it * GH + j
                        pe.wait_ge(maxed, i * TB + TB)
                        if j:
                            pe.wait_ge(nm_put, i)
                        for st in range(TB):
                            mm = pe.matmul(pn[0:1, st * P:(st + 1) * P], nmax[j][:, st:st + 1], t.ident[:], start=True, stop=True)
                        mm.then_inc(nm_row, 1)

                    def scores(j):
                        i = it * GH + j
                        pe.wait_ge(nm_put, i + 1)
                        for l in range(TB):
                            if j or l >= 2:
                                pe.wait_ge(p_made, i * TB + l - 1)
                            pe.matmul(ps_s[l % 2][:, 0:S - l * P], ks[j][:, l * P:(l + 1) * P], qs[j][:, l * P:S], start=True, stop=False)
                            pe.matmul(ps_s[l % 2][:, 0:P], identr[:], neg[:, 1, :], start=False, stop=True).then_inc(s_made, 1)

                    def values(j):
                        i = it * GH + j
                        pe.wait_ge(p_made, i * TB + TB)
                        if j == 0:
                            pe.wait_ge(staged, it * (2 + GH) + 2 + GH)
                        for l in range(TB):
                            pe.matmul(ps_o[:, l * P:S], vp[j][:, l, :], probs[j][:, l, l * P:S], start=j == 0 and l == 0, stop=j == GH - 1 and l == TB - 1)
                        pe.wait_ge(p_seq, i * TB + TB)
                        mm = pe.matmul(ps_sum[:], onep[j][:], psum_p[j][:], start=j == 0, stop=j == GH - 1)
                        if j == GH - 1:
                            mm.then_inc(o_made, 1)

                    pe.wait_ge(staged, it * (2 + GH) + 2)
                    pe.wait_ge(hqT_made, b * KD + KD)
                    for k in range(KD):
                        mm = pe.matmul(pa[:], wqs[:, k, :], hqT[:, k, :], start=k == 0, stop=k == KD - 1)
                    mm.then_inc(proj, 1)
                    pe.matmul(pb[:], wks[:], ctxT[:], start=True, stop=True).then_inc(proj, 1)
                    pe.wait_ge(v_put, b * TB + TB)
                    stack(0)
                    stack(1)
                    max_row(0)
                    scores(0)
                    stack(2)
                    max_row(1)
                    scores(1)
                    pe.wait_ge(o_put, it + 1)
                    values(0)
                    stack(3)
                    max_row(2)
                    scores(2)
                    values(1)
                    max_row(3)
                    scores(3)
                    values(2)
                    values(3)
                for tt in range(TB):
                    pe.wait_ge(o_put, b * NG + NG + 1)
                    pe.wait_ge(y_added, b * TB + tt + 1)
                    for k in range(NG):
                        mm = pe.matmul(ps_s[tt % 2][:], oT[:, k, tt * P:(tt + 1) * P], wo[:, k, :], start=k == 0, stop=k == NG - 1)
                    mm.then_inc(y_made, 1)

        @block.scalar
        def _(act):
            with act.Fori(0, B) as b:
                act.wait_ge(ln_var, b + 1)
                act.activation(std[:], mv[:, :, 1], ACT.Sqrt, bias=t.ln_eps[:]).then_inc(ln_std, 1)
                for k in range(KD):
                    act.wait_ge(hq_tr, b * KD + k + 1)
                    act.copy(hqT[:, k, :], ps_s[k % 2][:]).then_inc(hqT_made, 1)
                for tt in range(TB):
                    act.wait_ge(v_made, b * TB + tt + 1)
                    act.copy(v[:, tt, :], pm[:]).then_inc(v_put, 1)
                with act.Fori(0, NG) as gr:
                    it = b * NG + gr

                    def put_q(j):
                        act.wait_ge(stacked, (it * GH + j) * 2 + 1)
                        act.copy(qs[j][0:R3, :], pa[0:R3, :]).then_inc(q_put, 1)

                    def put_max(j):
                        act.wait_ge(nm_row, it * GH + j + 1)
                        act.copy(qs[j][R3:R3 + 1, :], pn[0:1, :]).then_inc(nm_put, 1)

                    def exps(j):
                        for l in range(TB):
                            act.wait_ge(s_made, (it * GH + j) * TB + l + 1)
                            act.activation(probs[j][:, l, l * P:S], ps_s[l % 2][:, 0:S - l * P], ACT.Exp).then_inc(p_made, 1)

                    act.wait_ge(proj, it * 2 + 2)
                    act.activation(qh[:], pa[:], ACT.Copy, scale=SC).then_inc(high, 1)
                    act.wait_ge(proj, it * 2 + 3)
                    act.copy(kh[:], pb[:]).then_inc(high, 1)
                    put_q(0)
                    put_q(1)
                    put_max(0)
                    exps(0)
                    put_q(2)
                    put_max(1)
                    exps(1)
                    put_q(3)
                    put_max(2)
                    exps(2)
                    put_max(3)
                    exps(3)

        @block.vector
        def _(dve):
            for j in range(GH):
                dve.memset(ks[j][R3:R3 + 1, :].bitcast(F32), 1.0).then_inc(made, 1)
            dve.wait_ge(consts, 4 + 9 * GH)
            dve.tensor_copy(pick[:], pickf[:]).then_inc(made, 1)
            dve.tensor_copy(neg[:], negf[:]).then_inc(made, 1)
            dve.tensor_copy(identr[:], t.ident[:]).then_inc(made, 1)
            with dve.Fori(0, B) as b:
                for tt in range(TB):
                    dve.bn_stats(stats[:, tt, :], t.x[:, bass.ds(b * TB + tt, 1), :].rearrange("p o d -> p (o d)")).then_inc(ln_seq, 1)
                dve.wait_ge(ln_seq, b * (TB + 1) + TB)
                dve.memset(rstd[:], 0.0)
                for tt in range(TB):
                    ag = dve.bn_aggr(mv[:, tt, :], stats[:, tt, :])
                ag.then_inc(ln_var, 1)
                dve.wait_ge(ln_std, b + 1)
                dve.reciprocal(rstd[:], std[:]).then_inc(ln_seq, 1)
                dve.wait_ge(ln_seq, b * (TB + 1) + TB + 1)
                for tt in range(TB):
                    dve.tensor_scalar(hq[:, tt, :], t.x[:, bass.ds(b * TB + tt, 1), :].rearrange("p o d -> p (o d)"), mv[:, tt, 0:1], rstd[:, tt:tt + 1],
                                      ALU.subtract, ALU.mult).then_inc(hq_made, 1)
                with dve.Fori(0, NG) as gr:
                    it = b * NG + gr
                    dve.wait_ge(high, it * 2 + 1)
                    dve.scalar_tensor_tensor(out=ql[:], in0=pa[:], scalar=SC, in1=qh[:].bitcast(F32), op0=ALU.mult, op1=ALU.subtract).then_inc(low, 1)
                    dve.wait_ge(high, it * 2 + 2)
                    dve.tensor_tensor(kl[:], pb[:], kh[:].bitcast(F32), ALU.subtract).then_inc(low, 1)
                    for j in range(GH):
                        i = it * GH + j
                        dve.wait_ge(stacked, i * 2 + 2)
                        dve.tensor_copy(ks[j][0:R3, :], pb[0:R3, :]).then_inc(k_put, 1)
                        for st in range(TB):
                            dve.wait_ge(smax, i * TB + st + 1)
                            dve.tensor_reduce(nmax[j][:, st:st + 1], pm[:, 0:(st + 1) * P], AX.X, ALU.max, negate=True).then_inc(maxed, 1)
                    dve.wait_ge(o_made, it + 1)
                    dve.reciprocal(rec[:], ps_sum[:]).then_inc(rec_made, 1)
                    dve.wait_ge(rec_made, it + 1)
                    dve.tensor_tensor(oT[:, bass.ds(gr, 1), :].rearrange("p o s -> p (o s)"), ps_o[:], rec[:], ALU.mult).then_inc(o_put, 1)
                for tt in range(TB):
                    dve.wait_ge(y_made, b * TB + tt + 1)
                    xt = t.x[:, bass.ds(b * TB + tt, 1), :].rearrange("p o d -> p (o d)")
                    dve.tensor_tensor(xt, ps_s[tt % 2][:], xt, ALU.add).then_inc(y_added, 1)


def build_program(nc, g, out):
    with Scope(nc, "all") as s:
        t = Shared()
        t.x = s.sb("x", [P, NT, D])
        t.ident, t.ones = s.sb("ident", [P, P]), s.sb("ones", [P, P])
        t.ln_eps, t.rms_eps = s.sb("ln_eps", [P, 1]), s.sb("rms_eps", [P, 1])
        with Scope(nc, "l0w") as w:
            t.wa, t.mo, t.wkr = w.sb("wa", [P, H0, KD, R]), w.sb("mo", [P, H0, D]), w.sb("wkr", [P, H0, R])
            fold_weights(nc, t, g)
            latent_attention(nc, t, g)
        moe_layer(nc, t, g, LAYER0_MOE)
        causal_attention(nc, t, g)
        moe_layer(nc, t, g, LAYER1_MOE)
        store_x(nc, t, out)


def moe_layer(nc, t, g, m):
    NE = m.E + (NSH if m.shared else 0)
    CT = m.cap // P
    m.y_rows = NE * m.cap
    m.xn_dram = nc.dram_tensor(f"xn_{m.name}", (N, D), F32).ap()
    m.y_dram = nc.dram_tensor(f"y_{m.name}", (m.y_rows, D), F32).ap()
    m.table = nc.dram_tensor(f"table_{m.name}", (m.E * m.cap, 1), F32).ap()
    with Scope(nc, f"moe{m.name}") as s:
        t.gate = s.sb("gate", [P, m.K * NT])
        t.slot = s.sb("slot", [P, m.K * NT], I32)
        t.gidx = s.sb("gidx", [P, (NE + 2) * CT], I32)
        if m.rms:
            t.norm_w = s.sb("norm_w", [P, D])
        route(nc, t, g, m)
        experts(nc, t, g, m)
        combine(nc, t, g, m)


LAYER0_MOE = MoeLayer(name="0", E=E0, K=K0, I=I0, cap=CAP0, chunks=2, router="wr0", wgu="wgu0", wd="wd0", rms=False,
                  shared=False, choice_major=True, renorm=False, drop_weight=True, z_made=None)
LAYER1_MOE = MoeLayer(name="1", E=E1, K=K1, I=I1, cap=CAP1, chunks=1, router="wr1", wgu="wgu1", wd="wd1", rms=True,
                  shared=True, choice_major=False, renorm=True, drop_weight=False, z_made=3)


def store_x(nc, t, out):
    with Scope(nc, "st") as s:
        stored = s.sem("stored")
        block = s.block()

        @block.sync
        def _(sp):
            sp.dma_start(out.rearrange("(t p) d -> p t d", p=P), t.x[:]).then_inc(stored, 16)
            sp.wait_ge(stored, 16)


def _rope_tables():
    inv = (np.float32(1.0) / np.float32(10000.0) ** (np.arange(0, DC, 2, dtype=np.float32) / np.float32(DC))).astype(np.float32)
    ang = np.arange(SK, dtype=np.float32)[:, None] * inv[None, :]
    def lay(a):
        a = np.repeat(a, 2, axis=-1).astype(np.float32)
        return np.ascontiguousarray(a.reshape(LT, P, DC).transpose(1, 0, 2))
    return lay(np.cos(ang)), lay(np.sin(ang))


def kernel(x, ctx_512, L0_xattn_Wq, L0_xattn_w_kc_q, L0_xattn_w_kc_kv, L0_xattn_W_qr, L0_xattn_W_kr, L0_xattn_Wo,
           L0_ffn_Wr, L0_ffn_Wg, L0_ffn_Wu, L0_ffn_Wd, L1_xattn_Wq, L1_xattn_Wkv_expand, L1_xattn_Wout,
           L1_ffn_norm_w, L1_ffn_gate_w, L1_ffn_w13, L1_ffn_w2, L1_ffn_shared_gate_w, L1_ffn_shared_up_w,
           L1_ffn_shared_down_w):
    import concourse.bacc as _bacc
    from concourse.bass_utils import run_bass_kernel_spmd as _run

    def rows(a, r, p=P):
        return np.asarray(a).reshape(r // p, p, -1).transpose(1, 0, 2)

    cos, sin = _rope_tables()
    lay = {
        "x": np.asarray(x).reshape(N, D),
        "ctx": np.asarray(ctx_512).reshape(B * SK, DC),
        "cos": cos, "sin": sin,
        "w_kc_qT": np.asarray(L0_xattn_w_kc_q).transpose(2, 0, 1).reshape(KQ, P, H0, HK).transpose(1, 0, 2, 3),
        "w_qr": np.asarray(L0_xattn_W_qr).transpose(1, 0, 2).reshape(KQ, P, H0, R).transpose(1, 0, 2, 3),
        "wq0": rows(L0_xattn_Wq, H0 * HK),
        "w_kc_kv": np.asarray(L0_xattn_w_kc_kv).transpose(1, 0, 2),
        "wo0": rows(np.asarray(L0_xattn_Wo).T, H0 * HK),
        "w_kr": np.asarray(L0_xattn_W_kr).transpose(1, 0, 2),
        "wr0": rows(np.asarray(L0_ffn_Wr).T, D),
        "wgu0": np.concatenate([np.asarray(L0_ffn_Wg), np.asarray(L0_ffn_Wu)], axis=1).transpose(0, 2, 1).reshape(E0, KD, P, 2 * I0).transpose(0, 2, 1, 3),
        "wd0": np.asarray(L0_ffn_Wd).transpose(0, 2, 1),
        "ctxT": np.asarray(ctx_512)[:, 0:S, :].transpose(2, 0, 1).reshape(DC, B * S),
        "wq1": rows(np.asarray(L1_xattn_Wq).T, D),
        "wk1": np.asarray(L1_xattn_Wkv_expand)[0:D].T,
        "wv1": np.asarray(L1_xattn_Wkv_expand)[D:2 * D].T,
        "wo1": rows(np.asarray(L1_xattn_Wout).T, D),
        "norm_w": np.tile(np.asarray(L1_ffn_norm_w)[None], (P, 1)),
        "wr1": rows(np.asarray(L1_ffn_gate_w).T, D),
        "wgu1": np.concatenate([np.asarray(L1_ffn_w13)] + [np.concatenate([np.asarray(L1_ffn_shared_gate_w), np.asarray(L1_ffn_shared_up_w)], axis=1)[None]] * NSH)
                .reshape(E1 + NSH, KD, P, 2 * I1).transpose(0, 2, 1, 3),
        "wd1": np.concatenate([np.asarray(L1_ffn_w2)] + [np.asarray(L1_ffn_shared_down_w)[None]] * NSH),
    }
    nc = _bacc.Bacc("TRN2", target_bir_lowering=False, num_devices=1)
    arrays, g = {}, {}
    for name, a in lay.items():
        a = np.ascontiguousarray(a)
        arrays[f"in_{name}"] = a
        g[name] = nc.dram_tensor(f"in_{name}", a.shape, mybir.dt.from_np(a.dtype), kind="ExternalInput").ap()
    out = nc.dram_tensor("out_x", (N, D), F32, kind="ExternalOutput").ap()
    build_program(nc, g, out)
    r = _run(nc, [arrays], core_ids=[0])
    return r.results[0]["out_x"].reshape(B, S, D)
```

```python
from contextlib import ExitStack

import numpy as np

import concourse.bass as bass
from concourse import mybir

F32 = mybir.dt.float32
F32R = mybir.dt.float32r
BF16 = mybir.dt.bfloat16
I32 = mybir.dt.int32
U32 = mybir.dt.uint32
ACT = mybir.ActivationFunctionType
ALU = mybir.AluOpType
AX = mybir.AxisListType

P = 128
B, S, D = 4, 512, 512
SK, DC = 1024, 128
N = B * S
NT = N // P
TB = S // P
KD = D // P
LN_EPS = 1e-5
RMS_EPS = 1e-6

H0, HK, DCQ, R = 16, 128, 384, 64
KQ = DCQ // P
LT = SK // P
H1 = 16
HD = D // H1
GH = P // HD
NG = H1 // GH
NEG = -1e30
E0, K0, I0 = 8, 2, 352
CAP0 = int(1.25 * (N * K0 / E0))
E1, K1, I1 = 32, 4, 256
CAP1 = 2 * N * K1 // E1
NSH = N // CAP1


class Shared:
    pass


class MoeLayer:

    def __init__(self, name, E, K, I, cap, chunks, router, wgu, wd, rms, shared, choice_major, renorm, drop_weight, z_made):
        self.name, self.E, self.K, self.I, self.cap = name, E, K, I, cap
        self.chunks = chunks
        self.router, self.wgu, self.wd = router, wgu, wd
        self.rms = rms
        self.shared = shared
        self.choice_major = choice_major
        self.renorm = renorm
        self.drop_weight = drop_weight
        self.z_made = z_made


class Scope:

    def __init__(self, nc, name):
        self.nc, self.name, self.stack, self.sems = nc, name, ExitStack(), []

    def __enter__(self):
        self.stack.__enter__()
        return self

    def __exit__(self, *a):
        self.stack.__exit__(*a)
        if self.sems:
            self.nc.clear_and_free_semaphores(self.sems)
            self.nc.all_engine_barrier()

    def sb(self, name, shape, dt=F32):
        return self.stack.enter_context(self.nc.sbuf_tensor(f"{self.name}_{name}", shape, dt))

    def ps(self, name, shape=(P, 512), dt=F32):
        return self.stack.enter_context(self.nc.psum_tensor(f"{self.name}_{name}", list(shape), dt))

    def sem(self, name):
        self.sems.append(self.nc.alloc_semaphore(f"{self.name}_{name}"))
        return self.sems[-1]

    def block(self):
        return self.stack.enter_context(self.nc.Block())


def fold_weights(nc, t, g):
    with Scope(nc, "fold") as s:
        kcq = s.sb("kcq", [P, KQ, H0, HK])
        wqr = s.sb("wqr", [P, KQ, H0, R])
        wq = s.sb("wq", [P, H0, D])
        kckv = s.sb("kckv", [P, H0, DC])
        wo = s.sb("wo", [P, H0, D])
        t1 = [s.sb(f"t1_{j}", [P, R]) for j in range(2)]
        ps_t1 = [s.ps(f"ps_t1_{j}") for j in range(2)]
        ps_wa = [s.ps(f"ps_wa_{j}") for j in range(2)]
        ps_mo = [s.ps(f"ps_mo_{j}") for j in range(2)]
        x_in, q_in, v_in = s.sem("x_in"), s.sem("q_in"), s.sem("v_in")
        t1_made, t1_copied, wa_made, wa_copied = (s.sem(n) for n in ("t1_made", "t1_copied", "wa_made", "wa_copied"))
        mo_made, mo_copied, ident_zeroed, consts_made = (s.sem(n) for n in ("mo_made", "mo_copied", "ident_zeroed", "consts_made"))
        block = s.block()

        @block.sync
        def _(sp):
            sp.dma_start(kcq[:], g["w_kc_qT"]).then_inc(q_in, 16)
            sp.dma_start(wqr[:], g["w_qr"]).then_inc(q_in, 16)
            sp.dma_start(wq[:], g["wq0"]).then_inc(q_in, 16)
            sp.dma_start(kckv[:], g["w_kc_kv"]).then_inc(v_in, 16)
            sp.dma_start(wo[:], g["wo0"]).then_inc(v_in, 16)
            sp.dma_start(t.wkr[:], g["w_kr"]).then_inc(x_in, 16)
            sp.dma_start(t.x[:], g["x"].rearrange("(t p) d -> p t d", p=P)).then_inc(x_in, 16)
            sp.wait_ge(x_in, 32)

        @block.gpsimd
        def _(pool):
            pool.memset(t.ident[:], 0.0).then_inc(ident_zeroed, 1)
            pool.wait_ge(ident_zeroed, 1)
            pool.affine_select(out=t.ident[:], in_=t.ident[:], compare_op=ALU.not_equal, fill=1.0, base=0,
                               pattern=[[-1, P]], channel_multiplier=1).then_inc(consts_made, 1)
            pool.memset(t.ones[:], 1.0).then_inc(consts_made, 1)
            pool.memset(t.ln_eps[:], LN_EPS).then_inc(consts_made, 1)
            pool.memset(t.rms_eps[:], RMS_EPS).then_inc(consts_made, 1)
            pool.wait_ge(consts_made, 4)

        @block.tensor
        def _(pe):
            pe.wait_ge(q_in, 48)
            for h in range(H0):
                if h >= 2:
                    pe.wait_ge(t1_copied, h - 1)
                for q in range(KQ):
                    mm = pe.matmul(ps_t1[h % 2][:, 0:R], kcq[:, q, h, :], wqr[:, q, h, :], start=q == 0, stop=q == KQ - 1)
                mm.then_inc(t1_made, 1)
                if h == 0:
                    pe.wait_ge(v_in, 32)
                if h >= 2:
                    pe.wait_ge(mo_copied, h - 1)
                pe.matmul(ps_mo[h % 2][:], kckv[:, h, :], wo[:, h, :], start=True, stop=True).then_inc(mo_made, 1)
                pe.wait_ge(t1_copied, h + 1)
                if h >= 2:
                    pe.wait_ge(wa_copied, h - 1)
                for k in range(KD):
                    mm = pe.matmul(ps_wa[h % 2][:, k * R:(k + 1) * R], wq[:, h, k * P:(k + 1) * P], t1[h % 2][:],
                                   start=True, stop=True)
                mm.then_inc(wa_made, 1)

        @block.vector
        def _(dve):
            for h in range(H0):
                dve.wait_ge(t1_made, h + 1)
                if h >= 2:
                    dve.wait_ge(wa_made, h - 1)
                dve.tensor_copy(t1[h % 2][:], ps_t1[h % 2][:, 0:R]).then_inc(t1_copied, 1)
                dve.wait_ge(wa_made, h + 1)
                dve.tensor_copy(t.wa[:, h, :, :], ps_wa[h % 2][:, 0:KD * R].rearrange("p (k r) -> p k r", r=R)).then_inc(wa_copied, 1)
            dve.wait_ge(wa_copied, H0)

        @block.scalar
        def _(act):
            for h in range(H0):
                act.wait_ge(mo_made, h + 1)
                act.copy(t.mo[:, h, :], ps_mo[h % 2][:]).then_inc(mo_copied, 1)
            act.wait_ge(mo_copied, H0)


def latent_attention(nc, t, g):
    HALF = SK // 2
    NM = 2 * TB
    with Scope(nc, "la") as s:
        ctx = s.sb("ctx", [P, LT, DC])
        kv = s.sb("kv", [P, LT, DC])
        kvT = s.sb("kvT", [P, SK])
        hqT = s.sb("hqT", [P, KD, S])
        stats, mv = s.sb("stats", [P, TB, 6]), s.sb("mv", [P, TB, 2])
        std, rstd = s.sb("std", [P, TB]), s.sb("rstd", [P, TB])
        was = [s.sb(f"was{j}", [P, KD, 2, R]) for j in range(2)]
        wks = [s.sb(f"wks{j}", [P, 2, R]) for j in range(2)]
        q1 = [s.sb(f"q1_{j}", [P, S], F32R) for j in range(2)]
        q2 = [s.sb(f"q2_{j}", [R + 1, S], F32R) for j in range(2)]
        k1 = [s.sb(f"k1_{j}", [P, SK], F32R) for j in range(2)]
        k2 = [s.sb(f"k2_{j}", [R + 1, SK], F32R) for j in range(2)]
        pmax = s.sb("pmax", [P, TB, 2])
        nmax = [s.sb(f"nmax{j}", [P, TB], F32R) for j in range(2)]
        identr = s.sb("identr", [P, P], F32R)
        probs = [s.sb(f"probs{j}", [P, LT, S]) for j in range(2)]
        hq = probs[0][:, 0:TB, :]
        rot = probs[0][:, TB:TB + 2, :].rearrange("p a (c d) -> p (a c) d", d=DC)
        cosT = probs[1][:, 0:2, :].rearrange("p a (c d) -> p (a c) d", d=DC)
        sinT = probs[1][:, 2:4, :].rearrange("p a (c d) -> p (a c) d", d=DC)
        psum_p = [s.sb(f"psum_p{j}", [P, S]) for j in range(2)]
        rsum = [s.sb(f"rsum{j}", [P, TB]) for j in range(2)]
        rsum_row = s.sb("rsum_row", [P, S])
        spare = s.sb("spare", [P, 2])
        ctxT = s.sb("ctxT", [P, H0, S])
        misc = s.ps("misc")
        ps_k = s.ps("ps_k")
        ps_max = [s.ps(f"ps_max{j}") for j in range(2)]
        ps_s = [s.ps(f"ps_s{j}") for j in range(2)]
        ps_o = [s.ps(f"ps_o{j}") for j in range(2)]
        tab_in, ctx_in, roped, kvT_tr, kvT_made = (s.sem(n) for n in ("tab_in", "ctx_in", "roped", "kvT_tr", "kvT_made"))
        ln_var, ln_std, ln_seq, hq_made, hq_tr, hqT_made = (s.sem(n) for n in ("ln_var", "ln_std", "ln_seq", "hq_made", "hq_tr", "hqT_made"))
        staged, q_made, q_high, q_low = (s.sem(n) for n in ("staged", "q_made", "q_high", "q_low"))
        k_made, k_high, k_low = (s.sem(n) for n in ("k_made", "k_high", "k_low"))
        smax, part_max, maxed, nm_row, nm_put = (s.sem(n) for n in ("smax", "part_max", "maxed", "nm_row", "nm_put"))
        s_made, p_made, p_seq, o_made, sum_made, sum_rec = (s.sem(n) for n in ("s_made", "p_made", "p_seq", "o_made", "sum_made", "sum_rec"))
        row_made, row_put, c_made, y_made, y_added = (s.sem(n) for n in ("row_made", "row_put", "c_made", "y_made", "y_added"))
        consts = s.sem("consts")
        block = s.block()

        def heads(eng, b, before, step, after):
            before((b * H0, 0, 0))
            step((b * H0, 0, 0), first=True, last=False)
            with eng.Fori(0, (H0 - 2) // 2) as hp:
                step((b * H0 + hp * 2 + 1, hp * 2 + 1, 1), first=False, last=False)
                step((b * H0 + hp * 2 + 2, hp * 2 + 2, 0), first=False, last=False)
            step((b * H0 + H0 - 1, H0 - 1, 1), first=False, last=True)
            after((b * H0 + H0 - 1, H0 - 1, 1))

        def following(head, d=1):
            i, h, j = head
            return i + d, h + d, (j + d) % 2

        @block.sync
        def _(sp):
            sp.dma_start(cosT, g["cos"]).then_inc(tab_in, 16)
            sp.dma_start(sinT, g["sin"]).then_inc(tab_in, 16)
            sp.dma_start(ctx[:], g["ctx"][0:SK, :].rearrange("(l p) d -> p l d", p=P)).then_inc(ctx_in, 16)
            with sp.Fori(1, B) as b:
                sp.wait_ge(roped, b * 5)
                sp.dma_start(ctx[:], g["ctx"][bass.ds(b * SK, SK), :].rearrange("(l p) d -> p l d", p=P)).then_inc(ctx_in, 16)
                sp.wait_ge(c_made, b * H0 + 2)
                sp.dma_start(cosT, g["cos"]).then_inc(tab_in, 16)
                sp.dma_start(sinT, g["sin"]).then_inc(tab_in, 16)

        @block.gpsimd
        def _(pool):
            for j in range(2):
                pool.memset(k2[j][R:R + 1, :].bitcast(F32), 1.0).then_inc(consts, 1)

            def stage(head):
                i, h, j = head
                pool.tensor_tensor(spare[:, j:j + 1], t.ln_eps[:], t.ln_eps[:], ALU.add)
                for c in range(2):
                    pool.tensor_copy(was[j][:, :, c, :], t.wa[:, bass.ds(h, 1), :, :].rearrange("p o k r -> p (o k) r")).then_inc(staged, 1)
                for c in range(2):
                    pool.tensor_copy(wks[j][:, c, :], t.wkr[:, bass.ds(h, 1), :].rearrange("p o r -> p (o r)")).then_inc(staged, 1)

            def before(head):
                pool.wait_ge(k_made, head[0] * 2 + 2)
                stage(head)
                stage(following(head))

            def step(head, first, last):
                i, h, j = head
                pool.wait_ge(p_made, i * LT + 2)
                pool.wait_ge(sum_made, i + 1)
                pool.tensor_tensor(psum_p[j][:], probs[j][:, 0, :], probs[j][:, 1, :], ALU.add).then_inc(p_seq, 1)
                for l in range(2, LT):
                    pool.wait_ge(p_made, i * LT + l + 1)
                    pool.wait_ge(p_seq, i * (LT - 1) + l - 1)
                    pool.tensor_tensor(psum_p[j][:], psum_p[j][:], probs[j][:, l, :], ALU.add).then_inc(p_seq, 1)

            with pool.Fori(0, B) as b:
                before((b * H0, 0, 0))
                step((b * H0, 0, 0), True, False)
                pool.wait_ge(k_made, b * (2 * H0) + 4)
                stage((b * H0 + 2, 2, 0))
                with pool.Fori(0, (H0 - 4) // 2) as hp:
                    for d, j in ((1, 1), (2, 0)):
                        step((b * H0 + hp * 2 + d, hp * 2 + d, j), False, False)
                        pool.wait_ge(k_made, b * (2 * H0) + hp * 4 + 2 * d + 4)
                        stage((b * H0 + hp * 2 + d + 2, hp * 2 + d + 2, j))
                step((b * H0 + H0 - 3, H0 - 3, 1), False, False)
                pool.wait_ge(k_made, b * (2 * H0) + 2 * (H0 - 3) + 4)
                stage((b * H0 + H0 - 1, H0 - 1, 1))
                step((b * H0 + H0 - 2, H0 - 2, 0), False, False)
                step((b * H0 + H0 - 1, H0 - 1, 1), False, True)

        @block.tensor
        def _(pe):
            def project_q(head, k):
                i, h, j = head
                if k == 0:
                    pe.wait_ge(staged, i * 4 + 4)
                mm = pe.matmul(misc[:], was[j][:, k, :, :].rearrange("p c r -> p (c r)"), hqT[:, k, :], start=k == 0, stop=k == KD - 1)
                if k == KD - 1:
                    mm.then_inc(q_made, 1)

            def project_k(head, half):
                i, h, j = head
                if half:
                    pe.wait_ge(k_low, i * 2 + 1)
                pe.matmul(ps_k[:], wks[j][:].rearrange("p c r -> p (c r)"), kvT[:, half * HALF:(half + 1) * HALF],
                          start=True, stop=True).then_inc(k_made, 1)

            def for_max(head, n):
                i, h, j = head
                st, half = n // 2, n % 2
                if n == 0:
                    pe.wait_ge(q_low, i + 1)
                    pe.wait_ge(k_high, i * 2 + 2)
                if n >= 2:
                    pe.wait_ge(part_max, i * NM + n - 1)
                pe.matmul(ps_max[n % 2][:], q1[j][:, st * P:(st + 1) * P], k1[j][:, half * HALF:(half + 1) * HALF],
                          start=True, stop=True).then_inc(smax, 1)

            def max_row(head, first_of_batch):
                i, h, j = head
                pe.wait_ge(maxed, i + 1)
                if not first_of_batch:
                    pe.wait_ge(row_put, i)
                for st in range(TB):
                    mm = pe.matmul(misc[0:1, st * P:(st + 1) * P], nmax[j][:, st:st + 1], identr[:], start=True, stop=True)
                mm.then_inc(nm_row, 1)

            def scores(head, l):
                i, h, j = head
                if l == 0:
                    pe.wait_ge(nm_put, i + 1)
                    pe.wait_ge(k_low, i * 2 + 2)
                if l >= 2:
                    pe.wait_ge(p_made, i * LT + l - 1)
                pe.matmul(ps_s[l % 2][:], k1[j][:, l * P:(l + 1) * P], q1[j][:], start=True, stop=False)
                pe.matmul(ps_s[l % 2][:], k2[j][:, l * P:(l + 1) * P], q2[j][:], start=False, stop=True).then_inc(s_made, 1)

            def weigh(head, l):
                i, h, j = head
                if l == 0:
                    pe.wait_ge(c_made, i + 1)
                pe.wait_ge(p_made, i * LT + l + 1)
                mm = pe.matmul(ps_o[j][:], kv[:, l, :], probs[j][:, l, :], start=l == 0, stop=l == LT - 1)
                if l == LT - 1:
                    mm.then_inc(o_made, 1)

            def sums(head, after_q):
                i, h, j = head
                pe.wait_ge(p_seq, i * (LT - 1) + LT - 1)
                if after_q:
                    pe.wait_ge(q_low, i + 3)
                else:
                    pe.wait_ge(row_put, i + 1)
                for st in range(TB):
                    mm = pe.matmul(misc[:, st:st + 1], psum_p[j][:, st * P:(st + 1) * P], t.ones[:, 0:1], start=True, stop=True)
                mm.then_inc(sum_made, 1)

            def sum_row(head):
                i, h, j = head
                pe.wait_ge(sum_rec, i + 1)
                for st in range(TB):
                    mm = pe.matmul(misc[:, st * P:(st + 1) * P], rsum[j][:, st:st + 1].to_broadcast([P, P]), t.ident[:], start=True, stop=True)
                mm.then_inc(row_made, 1)

            def before(head):
                pe.wait_ge(row_put, head[0] + 1)
                for k in range(KD):
                    project_q(head, k)
                for half in range(2):
                    project_k(head, half)
                for n in range(NM):
                    for_max(head, n)
                max_row(head, True)

            def step(head, first, last):
                nxt = following(head)
                prev = following(head, -1)
                scores(head, 0)
                scores(head, 1)
                for l in range(LT):
                    if not last:
                        if l == 0:
                            for k in range(KD):
                                project_q(nxt, k)
                        if l == 1:
                            project_k(nxt, 0)
                        if l == 2:
                            project_k(nxt, 1)
                        if 3 <= l < 7:
                            for_max(nxt, 2 * (l - 3))
                    weigh(head, l)
                    if not last and 3 <= l < 7:
                        for_max(nxt, 2 * (l - 3) + 1)
                    if not first:
                        if l == 3:
                            sums(prev, not last)
                        if l == 5:
                            sum_row(prev)
                    if l + 2 < LT:
                        scores(head, l + 2)
                if not last:
                    max_row(nxt, False)

            def after(head):
                sums(head, False)
                sum_row(head)

            pe.wait_ge(consts, 3)
            pe.sem_inc(row_put, 1)
            pe.sem_inc(c_made, 2)
            pe.sem_inc(y_added, 1)
            pe.sem_inc(k_made, 2)
            pe.sem_inc(sum_made, 2)
            with pe.Fori(0, B) as b:
                for k in range(KD):
                    pe.wait_ge(hq_made, b * TB + TB)
                    if k == 0:
                        pe.wait_ge(y_added, b * TB + 1)
                    if k >= 2:
                        pe.wait_ge(hqT_made, b * KD + k - 1)
                    for tt in range(TB):
                        tr = pe.transpose(ps_s[k % 2][:, tt * P:(tt + 1) * P], hq[:, tt, k * P:(k + 1) * P], t.ident[:])
                    tr.then_inc(hq_tr, 1)
                pe.wait_ge(roped, b * 5 + 5)
                pe.wait_ge(c_made, b * H0 + 2)
                for half in range(2):
                    for l in range(4):
                        tr = pe.transpose(ps_o[half][:, l * P:(l + 1) * P], kv[:, half * 4 + l, :], t.ident[:])
                    tr.then_inc(kvT_tr, 1)
                pe.wait_ge(hqT_made, b * KD + KD)
                pe.wait_ge(kvT_made, b * 2 + 2)
                heads(pe, b, before, step, after)
                for tt in range(TB):
                    if tt >= 2:
                        pe.wait_ge(y_added, b * TB + tt)
                    pe.wait_ge(c_made, b * H0 + H0 + 2)
                    for h in range(H0):
                        mm = pe.matmul(ps_s[tt % 2][:], ctxT[:, h, tt * P:(tt + 1) * P], t.mo[:, h, :], start=h == 0, stop=h == H0 - 1)
                    mm.then_inc(y_made, 1)

        @block.scalar
        def _(act):
            def high_q(head):
                i, h, j = head
                act.wait_ge(q_made, i + 1)
                act.copy(q1[j][:], misc[:])
                act.copy(q2[j][0:R, :], misc[0:R, :]).then_inc(q_high, 1)

            def high_k(head, half):
                i, h, j = head
                act.wait_ge(k_made, i * 2 + half + 3)
                act.copy(k1[j][:, half * HALF:(half + 1) * HALF], ps_k[:]).then_inc(k_high, 1)

            def put_max(head):
                i, h, j = head
                act.wait_ge(nm_row, i + 1)
                act.copy(q2[j][R:R + 1, :], misc[0:1, :]).then_inc(nm_put, 1)

            def put_row(head):
                i, h, j = head
                act.wait_ge(row_made, i + 1)
                act.wait_ge(c_made, i + 2)
                act.copy(rsum_row[:], misc[:]).then_inc(row_put, 1)

            def before(head):
                high_q(head)
                high_k(head, 0)
                high_k(head, 1)
                put_max(head)

            def step(head, first, last):
                i, h, j = head
                nxt, prev = following(head), following(head, -1)
                for l in range(LT):
                    act.wait_ge(s_made, i * LT + l + 1)
                    act.activation(probs[j][:, l, :], ps_s[l % 2][:], ACT.Exp).then_inc(p_made, 1)
                    if not last:
                        if l == 0:
                            high_q(nxt)
                        if l == 1:
                            high_k(nxt, 0)
                        if l == 2:
                            high_k(nxt, 1)
                    if not first and l == 6:
                        put_row(prev)
                if not last:
                    put_max(nxt)

            with act.Fori(0, B) as b:
                act.wait_ge(ln_var, b + 1)
                act.activation(std[:], mv[:, :, 1], ACT.Sqrt, bias=t.ln_eps[:]).then_inc(ln_std, 1)
                for k in range(KD):
                    act.wait_ge(hq_tr, b * KD + k + 1)
                    act.copy(hqT[:, k, :], ps_s[k % 2][:]).then_inc(hqT_made, 1)
                for half in range(2):
                    act.wait_ge(kvT_tr, b * 2 + half + 1)
                    act.copy(kvT[:, half * HALF:(half + 1) * HALF], ps_o[half][:]).then_inc(kvT_made, 1)
                heads(act, b, before, step, put_row)

        @block.vector
        def _(dve):
            def low_q(head):
                i, h, j = head
                dve.wait_ge(q_high, i + 1)
                dve.tensor_tensor(q1[j][R:P, :], misc[R:P, :], q1[j][R:P, :].bitcast(F32), ALU.subtract).then_inc(q_low, 1)

            def low_k(head, half):
                i, h, j = head
                dve.wait_ge(k_high, i * 2 + half + 1)
                hs = slice(half * HALF, (half + 1) * HALF)
                dve.tensor_tensor(k2[j][0:R, hs], ps_k[0:R, :], k1[j][0:R, hs].bitcast(F32), ALU.subtract).then_inc(k_low, 1)

            def maximum(head, n):
                i, h, j = head
                dve.wait_ge(smax, i * NM + n + 1)
                dve.tensor_reduce(pmax[:, n // 2, n % 2:n % 2 + 1], ps_max[n % 2][:], AX.X, ALU.max).then_inc(part_max, 1)
                if n == NM - 1:
                    dve.wait_ge(part_max, i * NM + NM)
                    dve.tensor_reduce(nmax[j][:], pmax[:], AX.X, ALU.max, negate=True).then_inc(maxed, 1)

            def reciprocal(head):
                i, h, j = head
                dve.wait_ge(sum_made, i + 3)
                dve.reciprocal(rsum[j][:], misc[:, 0:TB]).then_inc(sum_rec, 1)

            def normalize(head):
                i, h, j = head
                dve.wait_ge(row_put, i + 2)
                dve.wait_ge(o_made, i + 1)
                dve.tensor_tensor(ctxT[:, bass.ds(h, 1), :].rearrange("p o s -> p (o s)"), ps_o[j][:], rsum_row[:], ALU.mult).then_inc(c_made, 1)

            def before(head):
                low_q(head)
                low_k(head, 0)
                low_k(head, 1)
                for n in range(NM):
                    maximum(head, n)

            def step(head, first, last):
                nxt, prev = following(head), following(head, -1)
                if not last:
                    low_q(nxt)
                    low_k(nxt, 0)
                    low_k(nxt, 1)
                    maximum(nxt, 0)
                    maximum(nxt, 1)
                if not first:
                    reciprocal(prev)
                if not last:
                    for n in range(2, NM):
                        maximum(nxt, n)
                if not first:
                    normalize(prev)

            def after(head):
                reciprocal(head)
                normalize(head)

            dve.tensor_copy(identr[:], t.ident[:]).then_inc(consts, 1)
            with dve.Fori(0, B) as b:
                for tt in range(TB):
                    dve.bn_stats(stats[:, tt, :], t.x[:, bass.ds(b * TB + tt, 1), :].rearrange("p o d -> p (o d)")).then_inc(ln_seq, 1)
                dve.wait_ge(ln_seq, b * (TB + 1) + TB)
                dve.memset(rstd[:], 0.0)
                for tt in range(TB):
                    ag = dve.bn_aggr(mv[:, tt, :], stats[:, tt, :])
                ag.then_inc(ln_var, 1)
                dve.wait_ge(ln_std, b + 1)
                dve.reciprocal(rstd[:], std[:]).then_inc(ln_seq, 1)
                dve.wait_ge(ln_seq, b * (TB + 1) + TB + 1)
                for tt in range(TB):
                    dve.tensor_scalar(hq[:, tt, :], t.x[:, bass.ds(b * TB + tt, 1), :].rearrange("p o d -> p (o d)"), mv[:, tt, 0:1], rstd[:, tt:tt + 1],
                                      ALU.subtract, ALU.mult).then_inc(hq_made, 1)
                dve.wait_ge(tab_in, b * 32 + 32)
                dve.wait_ge(ctx_in, b * 16 + 16)
                dve.tensor_tensor(rot[:, :, 0:DC // 2], ctx[:, :, DC // 2:DC], sinT[:, :, 0:DC // 2], ALU.mult).then_inc(roped, 1)
                dve.tensor_tensor(rot[:, :, DC // 2:DC], ctx[:, :, 0:DC // 2], sinT[:, :, DC // 2:DC], ALU.mult).then_inc(roped, 1)
                dve.tensor_tensor(kv[:], ctx[:], cosT[:], ALU.mult).then_inc(roped, 1)
                dve.wait_ge(roped, b * 5 + 3)
                dve.tensor_tensor(kv[:, :, 0:DC // 2], kv[:, :, 0:DC // 2], rot[:, :, 0:DC // 2], ALU.subtract).then_inc(roped, 1)
                dve.tensor_tensor(kv[:, :, DC // 2:DC], kv[:, :, DC // 2:DC], rot[:, :, DC // 2:DC], ALU.add).then_inc(roped, 1)
                heads(dve, b, before, step, after)
                for tt in range(TB):
                    dve.wait_ge(y_made, b * TB + tt + 1)
                    xt = t.x[:, bass.ds(b * TB + tt, 1), :].rearrange("p o d -> p (o d)")
                    dve.tensor_tensor(xt, ps_s[tt % 2][:], xt, ALU.add).then_inc(y_added, 1)


def route(nc, t, g, m):
    E, K, cap = m.E, m.K, m.cap
    F = NT * K if m.choice_major else NT
    KT = K * NT
    SLOTS = E * cap
    GT = SLOTS // P
    with Scope(nc, f"rt{m.name}") as s:
        xn = s.sb("xn", [P, NT, D])
        stats, mv = s.sb("stats", [P, NT, 6]), s.sb("mv", [P, NT, 2])
        std, rstd = s.sb("std", [P, NT]), s.sb("rstd", [P, NT])
        wr = s.sb("wr", [P, KD, E])
        xT = [s.sb(f"xT{j}", [P, KD * P]) for j in range(2)]
        lg, ex = s.sb("lg", [P, NT, E]), s.sb("ex", [P, NT, E])
        v8, i8 = s.sb("v8", [P, NT, 8]), s.sb("i8", [P, NT, 8], U32)
        idxf = s.sb("idxf", [P, K, NT])
        dv = s.sb("dv", [P, K, NT])
        den = s.sb("den", [P, NT])
        iota_e = s.sb("iota_e", [P, E])
        tri = s.sb("tri", [P, P])
        masks = s.sb("masks", [P, KT, E])
        queue = masks if m.choice_major else s.sb("queue", [P, NT, E])
        tot = s.sb("tot", [P, F, E])
        pre = [s.sb(f"pre{j}", [P, F, E]) for j in range(2)]
        rank = s.sb("rank", [P, KT])
        sel = s.sb("sel", [P, KT, E])
        keep, base, slotf = s.sb("keep", [P, KT]), s.sb("base", [P, KT]), s.sb("slotf", [P, KT])
        dslot = s.sb("dslot", [P, KT], I32)
        tokid = s.sb("tokid", [P, NT])
        zero = s.sb("zero", [P, P])
        tab = s.sb("tab", [P, P])
        junk = s.sb("junk", [P, 2, D])
        ps_tr = [s.ps(f"ps_tr{j}") for j in range(2)]
        ps_l, ps_tot, ps_rk, ps_tab = (s.ps(n) for n in ("ps_l", "ps_tot", "ps_rk", "ps_tab"))
        w_in, consts, var_ready, std_ready, chain = (s.sem(n) for n in ("w_in", "consts", "var", "std", "chain"))
        xn_made, xn_out, tr_made, xT_made, l_made = (s.sem(n) for n in ("xn_made", "xn_out", "tr_made", "xT_made", "l_made"))
        ex_in, ex_made, q_ready, q_summed, slots_ready = (s.sem(n) for n in ("ex_in", "ex_made", "q_ready", "q_summed", "slots_ready"))
        scattered, tab_in, tab_tr, zeroed = (s.sem(n) for n in ("scattered", "tab_in", "tab_tr", "zeroed"))
        block = s.block()

        @block.sync
        def _(sp):
            sp.dma_start(wr[:], g[m.router]).then_inc(w_in, 16)
            if m.rms:
                sp.dma_start(t.norm_w[:], g["norm_w"]).then_inc(w_in, 16)
            sp.wait_ge(consts, 2)
            sp.dma_start(m.table.rearrange("(n p) o -> n (p o)", p=P), zero[0:GT, :]).then_inc(zeroed, 16)
            for tt in range(NT):
                sp.wait_ge(xn_made, tt + 1)
                sp.dma_start(m.xn_dram[tt * P:(tt + 1) * P, :], xn[:, tt, :]).then_inc(xn_out, 16)
            sp.wait_ge(scattered, 16 * KT)
            sp.dma_start(tab[0:GT, :], m.table.rearrange("(n p) o -> n (p o)", p=P)).then_inc(tab_in, 16)
            sp.wait_ge(xn_out, 16 * NT)
            sp.wait_ge(tab_in, 16)

        @block.gpsimd
        def _(pool):
            pool.memset(t.gidx[:], 0).then_inc(consts, 1)
            pool.memset(zero[:], 0.0).then_inc(consts, 1)
            pool.iota(iota_e[:], pattern=[[1, E]], base=0, channel_multiplier=0, allow_small_or_imprecise_dtypes=True).then_inc(consts, 1)
            pool.iota(tokid[:], pattern=[[P, NT]], base=0, channel_multiplier=1, allow_small_or_imprecise_dtypes=True).then_inc(consts, 1)
            pool.memset(tri[:], 1.0).then_inc(consts, 1)
            pool.wait_ge(consts, 5)
            pool.affine_select(out=tri[:], in_=tri[:], compare_op=ALU.is_gt, fill=0.0, base=0,
                               pattern=[[1, P]], channel_multiplier=-1).then_inc(consts, 1)
            pool.wait_ge(slots_ready, 1)
            pool.wait_ge(zeroed, 16)
            for c in range(KT):
                pool.indirect_dma_start(out=m.table, out_offset=bass.IndirectOffsetOnAxis(ap=dslot[:, c:c + 1], axis=0),
                                        in_=tokid[:, c % NT:c % NT + 1], in_offset=None,
                                        bounds_check=SLOTS - 1, oob_is_err=False).then_inc(scattered, 16)
            pool.wait_ge(scattered, 16 * KT)

        @block.tensor
        def _(pe):
            pe.wait_ge(w_in, 16)
            for tt in range(NT + 1):
                if tt < NT:
                    pe.wait_ge(xn_made, tt + 1)
                    if tt >= 2:
                        pe.wait_ge(xT_made, tt - 1)
                    for k in range(KD):
                        mm = pe.transpose(ps_tr[tt % 2][:, k * P:(k + 1) * P], xn[:, tt, k * P:(k + 1) * P], t.ident[:])
                    mm.then_inc(tr_made, 1)
                if tt >= 1:
                    pe.wait_ge(xT_made, tt)
                    for k in range(KD):
                        mm = pe.matmul(ps_l[:, (tt - 1) * E:tt * E], xT[(tt - 1) % 2][:, k * P:(k + 1) * P], wr[:, k, :], start=k == 0, stop=k == KD - 1)
                    mm.then_inc(l_made, 1)
            pe.wait_ge(q_ready, 1)
            pe.wait_ge(consts, 6)
            pe.matmul(ps_tot[:, 0:F * E], t.ones[:], queue[:, 0:F, :].rearrange("p f e -> p (f e)"), start=True, stop=True).then_inc(q_summed, 1)
            pe.matmul(ps_rk[:, 0:F * E], tri[:], queue[:, 0:F, :].rearrange("p f e -> p (f e)"), start=True, stop=True).then_inc(q_summed, 1)
            pe.wait_ge(tab_in, 16)
            pe.transpose(ps_tab[:, 0:GT], tab[0:GT, :], t.ident[0:GT, 0:GT]).then_inc(tab_tr, 1)

        @block.scalar
        def _(act):
            act.wait_ge(var_ready, 1)
            act.activation(std[:], mv[:, :, 1], ACT.Sqrt, bias=t.ln_eps[:]).then_inc(std_ready, 1)
            if m.rms:
                for tt in range(NT):
                    act.wait_ge(chain, m.z_made + tt)
                    if tt >= 2:
                        act.wait_ge(ex_made, tt - 1)
                    act.activation(junk[:, tt % 2, :], xn[:, tt, :], ACT.Square, accum_out=den[:, tt:tt + 1]).then_inc(ex_made, 1)
                act.wait_ge(ex_made, NT)
                act.activation(std[:], den[:], ACT.Sqrt, bias=t.rms_eps[:], scale=1.0 / D).then_inc(std_ready, 1)
            for tt in range(NT):
                act.wait_ge(tr_made, tt + 1)
                if tt >= 2:
                    act.wait_ge(l_made, tt - 1)
                act.copy(xT[tt % 2][:], ps_tr[tt % 2][:]).then_inc(xT_made, 1)
            act.wait_ge(ex_in, 1)
            act.activation(ex[:], lg[:], ACT.Exp).then_inc(ex_made, 1)
            act.activation(dv[:], dv[:], ACT.Exp).then_inc(ex_made, 1)

        @block.vector
        def _(dve):
            n = [0]

            def link(ins):
                n[0] += 1
                ins.then_inc(chain, 1)
                dve.wait_ge(chain, n[0])

            for tt in range(NT):
                ins = dve.bn_stats(stats[:, tt, :], t.x[:, tt, :])
            link(ins)
            for tt in range(NT):
                ins = dve.bn_aggr(mv[:, tt, :], stats[:, tt, :])
            ins.then_inc(var_ready, 1)
            dve.wait_ge(std_ready, 1)
            link(dve.reciprocal(rstd[:], std[:]))
            assert n[0] == 2
            for tt in range(NT):
                ins = dve.tensor_scalar(xn[:, tt, :], t.x[:, tt, :], mv[:, tt, 0:1], rstd[:, tt:tt + 1], ALU.subtract, ALU.mult)
                if m.rms:
                    n[0] += 1
                    ins.then_inc(chain, 1)
                else:
                    ins.then_inc(xn_made, 1)
            if m.rms:
                dve.wait_ge(chain, n[0])
                link(dve.tensor_tensor(t.x[:], t.x[:], xn[:], ALU.add))
                dve.wait_ge(std_ready, 2)
                link(dve.reciprocal(rstd[:], std[:]))
                dve.wait_ge(w_in, 32)
                for tt in range(NT):
                    dve.scalar_tensor_tensor(out=xn[:, tt, :], in0=xn[:, tt, :], scalar=rstd[:, tt:tt + 1], in1=t.norm_w[:],
                                             op0=ALU.mult, op1=ALU.mult).then_inc(xn_made, 1)
            dve.wait_ge(l_made, NT)
            link(dve.tensor_copy(lg[:], ps_l[:, 0:NT * E].rearrange("p (t e) -> p t e", e=E)))
            for tt in range(NT):
                ins = dve.max(v8[:, tt, :], lg[:, tt, :])
            link(ins)
            for tt in range(NT):
                ins = dve.max_index(i8[:, tt, :], v8[:, tt, :], lg[:, tt, :])
            link(ins)
            link(dve.tensor_copy(idxf[:], i8[:, :, 0:K].rearrange("p t k -> p k t")))
            dve.tensor_tensor(dv[:], v8[:, :, 0:K].rearrange("p t k -> p k t"), v8[:, :, 0:1].rearrange("p t o -> p o t").to_broadcast([P, K, NT]), ALU.subtract)
            dve.tensor_tensor(lg[:], lg[:], v8[:, :, 0:1].to_broadcast([P, NT, E]), ALU.subtract).then_inc(ex_in, 1)
            dve.wait_ge(consts, 4)
            link(dve.tensor_tensor(masks[:], iota_e[:].rearrange("p (o e) -> p o e", o=1).to_broadcast([P, KT, E]),
                                   idxf[:].rearrange("p k (t o) -> p (k t) o", o=1).to_broadcast([P, KT, E]), ALU.is_equal))
            if not m.choice_major:
                link(dve.tensor_tensor(queue[:], masks[:, 0:NT, :], masks[:, NT:2 * NT, :], ALU.add))
                for k in range(2, K):
                    link(dve.tensor_tensor(queue[:], queue[:], masks[:, k * NT:(k + 1) * NT, :], ALU.add))
            dve.sem_inc(q_ready, 1)
            dve.wait_ge(ex_made, 2 + (NT if m.rms else 0))
            if m.renorm:
                link(dve.tensor_reduce(den[:], dv[:].rearrange("p k t -> p t k"), AX.X, ALU.add))
            else:
                link(dve.tensor_reduce(den[:], ex[:], AX.X, ALU.add))
            link(dve.reciprocal(den[:], den[:]))
            link(dve.tensor_tensor(t.gate[:, 0:KT].rearrange("p (k t) -> p k t", t=NT), dv[:], den[:].rearrange("p (o t) -> p o t", o=1).to_broadcast([P, K, NT]), ALU.mult))
            dve.wait_ge(q_summed, 2)
            link(dve.tensor_copy(tot[:], ps_tot[:, 0:F * E].rearrange("p (f e) -> p f e", e=E)))
            src, step, j = tot, 1, 0
            while step < F:
                dve.tensor_copy(pre[j][:, 0:step, :], src[:, 0:step, :])
                link(dve.tensor_tensor(pre[j][:, step:F, :], src[:, step:F, :], src[:, 0:F - step, :], ALU.add))
                src, step, j = pre[j], step * 2, 1 - j
            link(dve.tensor_tensor(tot[:], src[:], tot[:], ALU.subtract))
            link(dve.tensor_tensor(tot[:], ps_rk[:, 0:F * E].rearrange("p (f e) -> p f e", e=E), tot[:], ALU.add))
            if m.choice_major:
                link(dve.tensor_tensor(sel[:], masks[:], tot[:], ALU.mult))
            else:
                for k in range(K):
                    ins = dve.tensor_tensor(sel[:, k * NT:(k + 1) * NT, :], masks[:, k * NT:(k + 1) * NT, :], tot[:], ALU.mult)
                link(ins)
            link(dve.tensor_reduce(rank[:], sel[:], AX.X, ALU.add))
            link(dve.tensor_scalar(base[:], idxf[:].rearrange("p k t -> p (k t)"), float(cap), None, ALU.mult))
            link(dve.tensor_scalar(keep[:], rank[:], float(cap), None, ALU.is_lt))
            link(dve.tensor_scalar(slotf[:], keep[:], -float(2 * SLOTS), float(2 * SLOTS), ALU.mult, ALU.add))
            link(dve.tensor_tensor(slotf[:], slotf[:], rank[:], ALU.add))
            link(dve.tensor_tensor(slotf[:], slotf[:], base[:], ALU.add))
            link(dve.tensor_copy(dslot[:], slotf[:]))
            dve.sem_inc(slots_ready, 1)
            link(dve.tensor_scalar(rank[:], rank[:], float(cap - 1), None, ALU.min))
            link(dve.tensor_tensor(rank[:], rank[:], base[:], ALU.add))
            link(dve.tensor_copy(t.slot[:, 0:KT], rank[:]))
            if m.drop_weight:
                link(dve.tensor_tensor(t.gate[:, 0:KT], t.gate[:, 0:KT], keep[:], ALU.mult))
            dve.wait_ge(tab_tr, 1)
            link(dve.tensor_copy(t.gidx[:, 0:GT], ps_tab[:, 0:GT]))
            if m.shared:
                link(dve.tensor_copy(t.gidx[:, GT:GT + NT], tokid[:]))


def experts(nc, t, g, m):
    NE = m.E + (NSH if m.shared else 0)
    cap, I = m.cap, m.I
    CT = cap // P
    CH = cap // m.chunks
    IS = [min(P, I - i) for i in range(0, I, P)]
    IT = len(IS)
    NGU = IT * m.chunks
    with Scope(nc, f"ex{m.name}") as s:
        wgu = [s.sb(f"wgu{j}", [P, KD, 2 * I]) for j in range(2)]
        wd = [s.sb(f"wd{j}", [P, IT, D]) for j in range(2)]
        idx = [s.sb(f"idx{j}", [P, CT], I32) for j in range(2)]
        xg = [s.sb(f"xg{j}", [P, CT, D]) for j in range(2)]
        xgT = [s.sb(f"xgT{j}", [P, KD, cap]) for j in range(2)]
        sg = [s.sb(f"sg{j}", [P, CH]) for j in range(2)]
        hT = [s.sb(f"hT{j}", [P, IT, cap]) for j in range(2)]
        y = [s.sb(f"y{c}", [P, D]) for c in range(CT)]
        ps_tr = [s.ps(f"ps_tr{j}") for j in range(2)]
        ps_g = [s.ps(f"ps_g{j}") for j in range(2)]
        ps_u = [s.ps(f"ps_u{j}") for j in range(2)]
        ps_y = [s.ps(f"ps_y{j}") for j in range(2)]
        turn, turned = s.sb("turn", [P, 2]), s.sem("turned")
        w_in = [s.sem(f"w_in{j}") for j in range(2)]
        x_in = [s.sem(f"x_in{j}") for j in range(2)]
        idx_made, tr_made, xT_made, gu_made, sg_made, h_made = (s.sem(n) for n in ("idx_made", "tr_made", "xT_made", "gu_made", "sg_made", "h_made"))
        y_made, y_put = s.sem("y_made"), s.sem("y_put")
        y_out = [s.sem(f"y_out{c}") for c in range(CT)]
        block = s.block()
        WD = 16 * (2 if IS[-1] == P else 3)

        @block.sync
        def _(sp):
            def load_weights(e, j):
                sp.dma_start(wgu[j][:], g[m.wgu][bass.ds(e, 1), :, :, :].rearrange("o p k i -> (o p) k i")).then_inc(w_in[j], 16)
                full = I // P * P
                sp.dma_start(wd[j][:, 0:I // P, :], g[m.wd][bass.ds(e, 1), 0:full, :].rearrange("o (i p) d -> (o p) i d", p=P)).then_inc(w_in[j], 16)
                if full < I:
                    sp.dma_start(wd[j][0:I - full, IT - 1, :], g[m.wd][bass.ds(e, 1), full:I, :].rearrange("o p d -> (o p) d")).then_inc(w_in[j], 16)

            def store(e, j):
                for c in range(CT):
                    sp.wait_ge(y_put, e * CT + c + 3)
                    sp.dma_start(m.y_dram[bass.ds((e * CT + c) * P, P), :], y[c][:]).then_inc(y_out[c], 16)

            sp.sem_inc(y_made, 1)
            for c in range(CT):
                sp.sem_inc(y_out[c], 16)
            load_weights(0, 0)
            with sp.Fori(0, NE // 2 - 1) as ep:
                sp.wait_ge(y_made, ep * (2 * CT) + 1)
                load_weights(ep * 2 + 1, 1)
                store(ep * 2, 0)
                sp.wait_ge(y_made, ep * (2 * CT) + CT + 1)
                load_weights(ep * 2 + 2, 0)
                store(ep * 2 + 1, 1)
            sp.wait_ge(y_made, (NE - 2) * CT + 1)
            load_weights(NE - 1, 1)
            store(NE - 2, 0)
            store(NE - 1, 1)
            for c in range(CT):
                sp.wait_ge(y_out[c], 16 * NE + 16)

        @block.gpsimd
        def _(pool):
            last_token = pool.to_reg(N - 1)
            pool.memset(turn[:], 0.0).then_inc(turned, 1)
            pool.wait_ge(turned, 1)
            with pool.Fori(0, NE // 2) as ep:
                for j in range(2):
                    e = ep * 2 + j
                    pool.wait_ge(idx_made, e + 1)
                    pool.wait_ge(turned, e + 1)
                    pool.tensor_tensor(turn[:, 1:2], turn[:, 0:1], turn[:, 0:1], ALU.add).then_inc(turned, 1)
                    for c in range(CT):
                        pool.indirect_dma_start(out=xg[j][:, c, :], out_offset=None, in_=m.xn_dram,
                                                in_offset=bass.IndirectOffsetOnAxis(ap=idx[j][:, c:c + 1], axis=0),
                                                bounds_check=last_token, oob_is_err=False).then_inc(x_in[j], 16)

        @block.tensor
        def _(pe):
            def transposes(ep, j):
                e = ep * 2 + j
                pe.wait_ge(x_in[j], ep * (16 * CT) + 16 * CT)
                for c in range(CT):
                    i = e * CT + c
                    pe.wait_ge(xT_made, i + 1)
                    for k in range(KD):
                        mm = pe.transpose(ps_tr[(j * CT + c) % 2][:, k * P:(k + 1) * P], xg[j][:, c, k * P:(k + 1) * P], t.ident[:])
                    mm.then_inc(tr_made, 1)

            def gate_up(ep, j):
                e = ep * 2 + j
                pe.wait_ge(w_in[j], ep * WD + WD)
                pe.wait_ge(xT_made, e * CT + CT + 2)
                for a in range(NGU):
                    it, ch = a // m.chunks, a % m.chunks
                    cols = slice(ch * CH, (ch + 1) * CH)
                    pe.wait_ge(h_made, e * NGU + a + 1)
                    for base, ps in ((0, ps_g), (I, ps_u)):
                        for k in range(KD):
                            mm = pe.matmul(ps[a % 2][0:IS[it], 0:CH], wgu[j][:, k, base + it * P:base + it * P + IS[it]], xgT[j][:, k, cols],
                                           start=k == 0, stop=k == KD - 1)
                    mm.then_inc(gu_made, 1)

            def down(ep, j):
                e = ep * 2 + j
                pe.wait_ge(h_made, e * NGU + NGU + 2)
                for c in range(CT):
                    pe.wait_ge(y_put, e * CT + c + 1)
                    for it in range(IT):
                        mm = pe.matmul(ps_y[(j * CT + c) % 2][:], hT[j][0:IS[it], it, c * P:(c + 1) * P], wd[j][0:IS[it], it, :],
                                       start=it == 0, stop=it == IT - 1)
                    mm.then_inc(y_made, 1)

            pe.sem_inc(xT_made, 2)
            pe.sem_inc(h_made, 2)
            pe.sem_inc(y_put, 2)
            with pe.Fori(0, NE // 2) as ep:
                transposes(ep, 0)
                gate_up(ep, 0)
                transposes(ep, 1)
                down(ep, 0)
                gate_up(ep, 1)
                down(ep, 1)

        @block.scalar
        def _(act):
            def evacuate(ep, j):
                for c in range(CT):
                    i = (ep * 2 + j) * CT + c
                    act.wait_ge(tr_made, i + 1)
                    act.copy(xgT[j][:, :, c * P:(c + 1) * P], ps_tr[(j * CT + c) % 2][:].rearrange("p (k c) -> p k c", c=P)).then_inc(xT_made, 1)

            def silu(ep, j):
                for a in range(NGU):
                    i = (ep * 2 + j) * NGU + a
                    r = IS[a // m.chunks]
                    act.wait_ge(gu_made, i + 1)
                    act.wait_ge(h_made, i + 1)
                    act.activation(sg[a % 2][0:r, :], ps_g[a % 2][0:r, 0:CH], ACT.Silu).then_inc(sg_made, 1)

            with act.Fori(0, NE // 2) as ep:
                evacuate(ep, 0)
                silu(ep, 0)
                evacuate(ep, 1)
                silu(ep, 1)

        @block.vector
        def _(dve):
            def stage_idx(e, j):
                dve.tensor_copy(idx[j][:], t.gidx[:, bass.ds(e * CT, CT)]).then_inc(idx_made, 1)

            def hidden(ep, j):
                for a in range(NGU):
                    i = (ep * 2 + j) * NGU + a
                    it, ch = a // m.chunks, a % m.chunks
                    r = IS[it]
                    dve.wait_ge(sg_made, i + 1)
                    dve.tensor_tensor(hT[j][0:r, it, ch * CH:(ch + 1) * CH], ps_u[a % 2][0:r, 0:CH], sg[a % 2][0:r, :], ALU.mult).then_inc(h_made, 1)

            def put(ep, j):
                for c in range(CT):
                    i = (ep * 2 + j) * CT + c
                    dve.wait_ge(y_made, i + 2)
                    dve.wait_ge(y_out[c], (ep * 2 + j) * 16 + 16)
                    dve.tensor_copy(y[c][:], ps_y[(j * CT + c) % 2][:]).then_inc(y_put, 1)

            for j in range(2):
                stage_idx(j, j)
            with dve.Fori(0, NE // 2) as ep:
                for j in range(2):
                    hidden(ep, j)
                    stage_idx(ep * 2 + j + 2, j)
                    put(ep, j)


def combine(nc, t, g, m):
    K = m.K
    RING = 8
    with Scope(nc, f"co{m.name}") as s:
        row = [s.sb(f"row{r}", [P, D]) for r in range(RING)]
        row_in = [s.sem(f"row_in{r}") for r in range(RING)]
        added = s.sem("added")
        sh, sh_in = (s.sb("sh", [P, NT, D]), s.sem("sh_in")) if m.shared else (None, None)
        block = s.block()
        todo = [(tt, k) for tt in range(NT) for k in range(K)]

        @block.sync
        def _(sp):
            if m.shared:
                first = m.E * m.cap
                sp.dma_start(sh[:], m.y_dram[first:first + N, :].rearrange("(t p) d -> p t d", p=P)).then_inc(sh_in, 16)

        @block.gpsimd
        def _(pool):
            for n, (tt, k) in enumerate(todo):
                if n >= RING:
                    pool.wait_ge(added, n - RING + 1 + m.shared)
                c = k * NT + tt
                pool.indirect_dma_start(out=row[n % RING][:], out_offset=None, in_=m.y_dram,
                                        in_offset=bass.IndirectOffsetOnAxis(ap=t.slot[:, c:c + 1], axis=0),
                                        bounds_check=m.y_rows - 1, oob_is_err=False).then_inc(row_in[n % RING], 16)

        @block.vector
        def _(dve):
            if m.shared:
                dve.wait_ge(sh_in, 16)
                dve.tensor_tensor(t.x[:], t.x[:], sh[:], ALU.add).then_inc(added, 0 + 1)
            for n, (tt, k) in enumerate(todo):
                c = k * NT + tt
                dve.wait_ge(row_in[n % RING], 16 * (n // RING + 1))
                if n or m.shared:
                    dve.wait_ge(added, n + m.shared)
                dve.scalar_tensor_tensor(out=t.x[:, tt, :], in0=row[n % RING][:], scalar=t.gate[:, c:c + 1], in1=t.x[:, tt, :],
                                         op0=ALU.mult, op1=ALU.add).then_inc(added, 1)
            dve.wait_ge(added, len(todo) + m.shared)


def causal_attention(nc, t, g):
    SC = float(np.float32(1.0) / np.sqrt(np.float32(HD)))
    R3 = 3 * HD
    with Scope(nc, "ca") as s:
        wq, wk, wv, wo = s.sb("wq", [P, KD, D]), s.sb("wk", [P, D]), s.sb("wv", [P, D]), s.sb("wo", [P, KD, D])
        ctxT = s.sb("ctxT", [P, S])
        stats, mv = s.sb("stats", [P, TB, 6]), s.sb("mv", [P, TB, 2])
        std, rstd = s.sb("std", [P, TB]), s.sb("rstd", [P, TB])
        hq, hqT = s.sb("hq", [P, TB, D]), s.sb("hqT", [P, KD, S])
        v = s.sb("v", [P, TB, D])
        wqs, wks = s.sb("wqs", [P, KD, P]), s.sb("wks", [P, P])
        vp = [s.sb(f"vp{j}", [P, TB, P]) for j in range(GH)]
        onep = [s.sb(f"onep{j}", [P, P]) for j in range(GH)]
        pick = s.sb("pick", [P, 2, 2, GH, P], F32R)
        pickf = s.sb("pickf", [P, 2, 2, GH, P])
        negf, neg = s.sb("negf", [P, 2, P]), s.sb("neg", [P, 2, P], F32R)
        identr = s.sb("identr", [P, P], F32R)
        qh, ql = s.sb("qh", [P, S], F32R), s.sb("ql", [P, S], F32R)
        kh, kl = s.sb("kh", [P, S], F32R), s.sb("kl", [P, S], F32R)
        qs = [s.sb(f"qs{j}", [R3 + 1, S], F32R) for j in range(GH)]
        ks = [s.sb(f"ks{j}", [R3 + 1, S], F32R) for j in range(GH)]
        nmax = [s.sb(f"nmax{j}", [P, TB]) for j in range(GH)]
        probs = [s.sb(f"probs{j}", [P, TB, S]) for j in range(GH)]
        psum_p = [s.sb(f"psum_p{j}", [P, S]) for j in range(GH)]
        rec = s.sb("rec", [P, S])
        oT = s.sb("oT", [P, NG, S])
        pa, pb, pm, pn = (s.ps(n) for n in ("pa", "pb", "pm", "pn"))
        ps_s = [s.ps(f"ps_s{j}") for j in range(2)]
        ps_o, ps_sum = s.ps("ps_o"), s.ps("ps_sum")
        w_in, ctx_in, consts, made = (s.sem(n) for n in ("w_in", "ctx_in", "consts", "made"))
        ln_seq, ln_var, ln_std, hq_made, hq_tr, hqT_made = (s.sem(n) for n in ("ln_seq", "ln_var", "ln_std", "hq_made", "hq_tr", "hqT_made"))
        v_made, v_put, staged, proj, high, low = (s.sem(n) for n in ("v_made", "v_put", "staged", "proj", "high", "low"))
        stacked, q_put, k_put, smax, maxed, nm_row, nm_put = (s.sem(n) for n in ("stacked", "q_put", "k_put", "smax", "maxed", "nm_row", "nm_put"))
        s_made, p_made, p_seq, o_made, rec_made, o_put, y_made, y_added = (s.sem(n) for n in ("s_made", "p_made", "p_seq", "o_made", "rec_made", "o_put", "y_made", "y_added"))
        block = s.block()

        @block.sync
        def _(sp):
            sp.dma_start(wq[:], g["wq1"]).then_inc(w_in, 16)
            sp.dma_start(wk[:], g["wk1"]).then_inc(w_in, 16)
            sp.dma_start(wv[:], g["wv1"]).then_inc(w_in, 16)
            sp.dma_start(wo[:], g["wo1"]).then_inc(w_in, 16)
            sp.sem_inc(o_put, 1)
            with sp.Fori(0, B) as b:
                sp.wait_ge(o_put, b * NG + 1)
                sp.dma_start(ctxT[:], g["ctxT"][:, bass.ds(b * S, S)]).then_inc(ctx_in, 16)

        @block.gpsimd
        def _(pool):
            pool.memset(pickf[:], 0.0).then_inc(consts, 1)
            pool.memset(negf[:], 0.0).then_inc(consts, 1)
            for j in range(GH):
                pool.memset(vp[j][:], 0.0).then_inc(consts, 1)
                pool.memset(onep[j][:], 0.0).then_inc(consts, 1)
            pool.wait_ge(consts, 2 + 2 * GH)
            for j in range(GH):
                head = slice(j * HD, (j + 1) * HD)
                pool.memset(onep[j][:, head], 1.0).then_inc(consts, 1)
                for x, part, blk in ((0, 0, 0), (0, 1, 1), (0, 0, 2), (1, 0, 0), (1, 0, 1), (1, 1, 2)):
                    pool.tensor_copy(pickf[:, x, part, j, blk * HD:(blk + 1) * HD], t.ident[:, head]).then_inc(consts, 1)
            pool.affine_select(out=negf[:, 0, :], in_=negf[:, 0, :], compare_op=ALU.is_ge, fill=NEG, base=0,
                               pattern=[[-1, P]], channel_multiplier=1).then_inc(consts, 1)
            pool.affine_select(out=negf[:, 1, :], in_=negf[:, 1, :], compare_op=ALU.is_ge, fill=NEG, base=0,
                               pattern=[[1, P]], channel_multiplier=-1).then_inc(consts, 1)
            pool.wait_ge(w_in, 64)
            pool.sem_inc(proj, 1)
            with pool.Fori(0, B) as b:
                with pool.Fori(0, NG) as gr:
                    it = b * NG + gr
                    pool.wait_ge(proj, it * 2 + 1)
                    pool.tensor_copy(wqs[:], wq[:, :, bass.ds(gr * P, P)]).then_inc(staged, 1)
                    pool.tensor_copy(wks[:], wk[:, bass.ds(gr * P, P)]).then_inc(staged, 1)
                    pool.wait_ge(o_put, it + 1)
                    pool.wait_ge(v_put, b * TB + TB)
                    for j in range(GH):
                        pool.tensor_copy(vp[j][:, :, j * HD:(j + 1) * HD], v[:, :, bass.ds(gr * P + j * HD, HD)]).then_inc(staged, 1)
                    for j in range(GH):
                        i = it * GH + j
                        pool.wait_ge(p_made, i * TB + 2)
                        pool.tensor_tensor(psum_p[j][:, 0:P], probs[j][:, 0, 0:P], t.ones[:], ALU.mult).then_inc(p_seq, 1)
                        pool.tensor_tensor(psum_p[j][:, P:S], probs[j][:, 0, P:S], probs[j][:, 1, P:S], ALU.add).then_inc(p_seq, 1)
                        for l in range(2, TB):
                            pool.wait_ge(p_made, i * TB + l + 1)
                            pool.wait_ge(p_seq, i * TB + l)
                            pool.tensor_tensor(psum_p[j][:, l * P:S], psum_p[j][:, l * P:S], probs[j][:, l, l * P:S], ALU.add).then_inc(p_seq, 1)

        @block.tensor
        def _(pe):
            pe.sem_inc(y_added, 2)
            pe.wait_ge(w_in, 64)
            pe.wait_ge(made, 3 + GH)
            with pe.Fori(0, B) as b:
                for k in range(KD):
                    pe.wait_ge(hq_made, b * TB + TB)
                    if k == 0:
                        pe.wait_ge(y_added, b * TB + 2)
                    if k >= 2:
                        pe.wait_ge(hqT_made, b * KD + k - 1)
                    for tt in range(TB):
                        tr = pe.transpose(ps_s[k % 2][:, tt * P:(tt + 1) * P], hq[:, tt, k * P:(k + 1) * P], t.ident[:])
                    tr.then_inc(hq_tr, 1)
                for tt in range(TB):
                    pe.wait_ge(ctx_in, b * 16 + 16)
                    if tt:
                        pe.wait_ge(v_put, b * TB + tt)
                    pe.matmul(pm[:], ctxT[:, tt * P:(tt + 1) * P], wv[:], start=True, stop=True).then_inc(v_made, 1)
                with pe.Fori(0, NG) as gr:
                    it = b * NG + gr

                    def stack(j):
                        i = it * GH + j
                        pe.wait_ge(low, it * 2 + 2)
                        if j:
                            pe.wait_ge(q_put, i)
                            pe.wait_ge(k_put, i)
                        pe.matmul(pa[0:R3, :], pick[:, 0, 0, j, 0:R3], qh[:], start=True, stop=False)
                        pe.matmul(pa[0:R3, :], pick[:, 0, 1, j, 0:R3], ql[:], start=False, stop=True).then_inc(stacked, 1)
                        pe.matmul(pb[0:R3, :], pick[:, 1, 0, j, 0:R3], kh[:], start=True, stop=False)
                        pe.matmul(pb[0:R3, :], pick[:, 1, 1, j, 0:R3], kl[:], start=False, stop=True).then_inc(stacked, 1)
                        pe.wait_ge(q_put, i + 1)
                        pe.wait_ge(k_put, i + 1)
                        for st in range(TB):
                            if j or st:
                                pe.wait_ge(maxed, i * TB + st)
                            w = (st + 1) * P
                            pe.matmul(pm[:, 0:w], qs[j][0:R3, st * P:w], ks[j][0:R3, 0:w], start=True, stop=False)
                            pe.matmul(pm[:, st * P:w], identr[:], neg[:, 0, :], start=False, stop=True).then_inc(smax, 1)

                    def max_row(j):
                        i = it * GH + j
                        pe.wait_ge(maxed, i * TB + TB)
                        if j:
                            pe.wait_ge(nm_put, i)
                        for st in range(TB):
                            mm = pe.matmul(pn[0:1, st * P:(st + 1) * P], nmax[j][:, st:st + 1], t.ident[:], start=True, stop=True)
                        mm.then_inc(nm_row, 1)

                    def scores(j):
                        i = it * GH + j
                        pe.wait_ge(nm_put, i + 1)
                        for l in range(TB):
                            if j or l >= 2:
                                pe.wait_ge(p_made, i * TB + l - 1)
                            pe.matmul(ps_s[l % 2][:, 0:S - l * P], ks[j][:, l * P:(l + 1) * P], qs[j][:, l * P:S], start=True, stop=False)
                            pe.matmul(ps_s[l % 2][:, 0:P], identr[:], neg[:, 1, :], start=False, stop=True).then_inc(s_made, 1)

                    def values(j):
                        i = it * GH + j
                        pe.wait_ge(p_made, i * TB + TB)
                        if j == 0:
                            pe.wait_ge(staged, it * (2 + GH) + 2 + GH)
                        for l in range(TB):
                            pe.matmul(ps_o[:, l * P:S], vp[j][:, l, :], probs[j][:, l, l * P:S], start=j == 0 and l == 0, stop=j == GH - 1 and l == TB - 1)
                        pe.wait_ge(p_seq, i * TB + TB)
                        mm = pe.matmul(ps_sum[:], onep[j][:], psum_p[j][:], start=j == 0, stop=j == GH - 1)
                        if j == GH - 1:
                            mm.then_inc(o_made, 1)

                    pe.wait_ge(staged, it * (2 + GH) + 2)
                    pe.wait_ge(hqT_made, b * KD + KD)
                    for k in range(KD):
                        mm = pe.matmul(pa[:], wqs[:, k, :], hqT[:, k, :], start=k == 0, stop=k == KD - 1)
                    mm.then_inc(proj, 1)
                    pe.matmul(pb[:], wks[:], ctxT[:], start=True, stop=True).then_inc(proj, 1)
                    pe.wait_ge(v_put, b * TB + TB)
                    stack(0)
                    stack(1)
                    max_row(0)
                    scores(0)
                    stack(2)
                    max_row(1)
                    scores(1)
                    pe.wait_ge(o_put, it + 1)
                    values(0)
                    stack(3)
                    max_row(2)
                    scores(2)
                    values(1)
                    max_row(3)
                    scores(3)
                    values(2)
                    values(3)
                for tt in range(TB):
                    pe.wait_ge(o_put, b * NG + NG + 1)
                    pe.wait_ge(y_added, b * TB + tt + 1)
                    for k in range(NG):
                        mm = pe.matmul(ps_s[tt % 2][:], oT[:, k, tt * P:(tt + 1) * P], wo[:, k, :], start=k == 0, stop=k == NG - 1)
                    mm.then_inc(y_made, 1)

        @block.scalar
        def _(act):
            with act.Fori(0, B) as b:
                act.wait_ge(ln_var, b + 1)
                act.activation(std[:], mv[:, :, 1], ACT.Sqrt, bias=t.ln_eps[:]).then_inc(ln_std, 1)
                for k in range(KD):
                    act.wait_ge(hq_tr, b * KD + k + 1)
                    act.copy(hqT[:, k, :], ps_s[k % 2][:]).then_inc(hqT_made, 1)
                for tt in range(TB):
                    act.wait_ge(v_made, b * TB + tt + 1)
                    act.copy(v[:, tt, :], pm[:]).then_inc(v_put, 1)
                with act.Fori(0, NG) as gr:
                    it = b * NG + gr

                    def put_q(j):
                        act.wait_ge(stacked, (it * GH + j) * 2 + 1)
                        act.copy(qs[j][0:R3, :], pa[0:R3, :]).then_inc(q_put, 1)

                    def put_max(j):
                        act.wait_ge(nm_row, it * GH + j + 1)
                        act.copy(qs[j][R3:R3 + 1, :], pn[0:1, :]).then_inc(nm_put, 1)

                    def exps(j):
                        for l in range(TB):
                            act.wait_ge(s_made, (it * GH + j) * TB + l + 1)
                            act.activation(probs[j][:, l, l * P:S], ps_s[l % 2][:, 0:S - l * P], ACT.Exp).then_inc(p_made, 1)

                    act.wait_ge(proj, it * 2 + 2)
                    act.activation(qh[:], pa[:], ACT.Copy, scale=SC).then_inc(high, 1)
                    act.wait_ge(proj, it * 2 + 3)
                    act.copy(kh[:], pb[:]).then_inc(high, 1)
                    put_q(0)
                    put_q(1)
                    put_max(0)
                    exps(0)
                    put_q(2)
                    put_max(1)
                    exps(1)
                    put_q(3)
                    put_max(2)
                    exps(2)
                    put_max(3)
                    exps(3)

        @block.vector
        def _(dve):
            for j in range(GH):
                dve.memset(ks[j][R3:R3 + 1, :].bitcast(F32), 1.0).then_inc(made, 1)
            dve.wait_ge(consts, 4 + 9 * GH)
            dve.tensor_copy(pick[:], pickf[:]).then_inc(made, 1)
            dve.tensor_copy(neg[:], negf[:]).then_inc(made, 1)
            dve.tensor_copy(identr[:], t.ident[:]).then_inc(made, 1)
            with dve.Fori(0, B) as b:
                for tt in range(TB):
                    dve.bn_stats(stats[:, tt, :], t.x[:, bass.ds(b * TB + tt, 1), :].rearrange("p o d -> p (o d)")).then_inc(ln_seq, 1)
                dve.wait_ge(ln_seq, b * (TB + 1) + TB)
                dve.memset(rstd[:], 0.0)
                for tt in range(TB):
                    ag = dve.bn_aggr(mv[:, tt, :], stats[:, tt, :])
                ag.then_inc(ln_var, 1)
                dve.wait_ge(ln_std, b + 1)
                dve.reciprocal(rstd[:], std[:]).then_inc(ln_seq, 1)
                dve.wait_ge(ln_seq, b * (TB + 1) + TB + 1)
                for tt in range(TB):
                    dve.tensor_scalar(hq[:, tt, :], t.x[:, bass.ds(b * TB + tt, 1), :].rearrange("p o d -> p (o d)"), mv[:, tt, 0:1], rstd[:, tt:tt + 1],
                                      ALU.subtract, ALU.mult).then_inc(hq_made, 1)
                with dve.Fori(0, NG) as gr:
                    it = b * NG + gr
                    dve.wait_ge(high, it * 2 + 1)
                    dve.scalar_tensor_tensor(out=ql[:], in0=pa[:], scalar=SC, in1=qh[:].bitcast(F32), op0=ALU.mult, op1=ALU.subtract).then_inc(low, 1)
                    dve.wait_ge(high, it * 2 + 2)
                    dve.tensor_tensor(kl[:], pb[:], kh[:].bitcast(F32), ALU.subtract).then_inc(low, 1)
                    for j in range(GH):
                        i = it * GH + j
                        dve.wait_ge(stacked, i * 2 + 2)
                        dve.tensor_copy(ks[j][0:R3, :], pb[0:R3, :]).then_inc(k_put, 1)
                        for st in range(TB):
                            dve.wait_ge(smax, i * TB + st + 1)
                            dve.tensor_reduce(nmax[j][:, st:st + 1], pm[:, 0:(st + 1) * P], AX.X, ALU.max, negate=True).then_inc(maxed, 1)
                    dve.wait_ge(o_made, it + 1)
                    dve.reciprocal(rec[:], ps_sum[:]).then_inc(rec_made, 1)
                    dve.wait_ge(rec_made, it + 1)
                    dve.tensor_tensor(oT[:, bass.ds(gr, 1), :].rearrange("p o s -> p (o s)"), ps_o[:], rec[:], ALU.mult).then_inc(o_put, 1)
                for tt in range(TB):
                    dve.wait_ge(y_made, b * TB + tt + 1)
                    xt = t.x[:, bass.ds(b * TB + tt, 1), :].rearrange("p o d -> p (o d)")
                    dve.tensor_tensor(xt, ps_s[tt % 2][:], xt, ALU.add).then_inc(y_added, 1)


def build_program(nc, g, out):
    with Scope(nc, "all") as s:
        t = Shared()
        t.x = s.sb("x", [P, NT, D])
        t.ident, t.ones = s.sb("ident", [P, P]), s.sb("ones", [P, P])
        t.ln_eps, t.rms_eps = s.sb("ln_eps", [P, 1]), s.sb("rms_eps", [P, 1])
        with Scope(nc, "l0w") as w:
            t.wa, t.mo, t.wkr = w.sb("wa", [P, H0, KD, R]), w.sb("mo", [P, H0, D]), w.sb("wkr", [P, H0, R])
            fold_weights(nc, t, g)
            latent_attention(nc, t, g)
        moe_layer(nc, t, g, LAYER0_MOE)
        causal_attention(nc, t, g)
        moe_layer(nc, t, g, LAYER1_MOE)
        store_x(nc, t, out)


def moe_layer(nc, t, g, m):
    NE = m.E + (NSH if m.shared else 0)
    CT = m.cap // P
    m.y_rows = NE * m.cap
    m.xn_dram = nc.dram_tensor(f"xn_{m.name}", (N, D), F32).ap()
    m.y_dram = nc.dram_tensor(f"y_{m.name}", (m.y_rows, D), F32).ap()
    m.table = nc.dram_tensor(f"table_{m.name}", (m.E * m.cap, 1), F32).ap()
    with Scope(nc, f"moe{m.name}") as s:
        t.gate = s.sb("gate", [P, m.K * NT])
        t.slot = s.sb("slot", [P, m.K * NT], I32)
        t.gidx = s.sb("gidx", [P, (NE + 2) * CT], I32)
        if m.rms:
            t.norm_w = s.sb("norm_w", [P, D])
        route(nc, t, g, m)
        experts(nc, t, g, m)
        combine(nc, t, g, m)


LAYER0_MOE = MoeLayer(name="0", E=E0, K=K0, I=I0, cap=CAP0, chunks=2, router="wr0", wgu="wgu0", wd="wd0", rms=False,
                  shared=False, choice_major=True, renorm=False, drop_weight=True, z_made=None)
LAYER1_MOE = MoeLayer(name="1", E=E1, K=K1, I=I1, cap=CAP1, chunks=1, router="wr1", wgu="wgu1", wd="wd1", rms=True,
                  shared=True, choice_major=False, renorm=True, drop_weight=False, z_made=3)


def store_x(nc, t, out):
    with Scope(nc, "st") as s:
        stored = s.sem("stored")
        block = s.block()

        @block.sync
        def _(sp):
            sp.dma_start(out.rearrange("(t p) d -> p t d", p=P), t.x[:]).then_inc(stored, 16)
            sp.wait_ge(stored, 16)


def _rope_tables():
    inv = (np.float32(1.0) / np.float32(10000.0) ** (np.arange(0, DC, 2, dtype=np.float32) / np.float32(DC))).astype(np.float32)
    ang = np.arange(SK, dtype=np.float32)[:, None] * inv[None, :]
    def lay(a):
        a = np.repeat(a, 2, axis=-1).astype(np.float32)
        return np.ascontiguousarray(a.reshape(LT, P, DC).transpose(1, 0, 2))
    return lay(np.cos(ang)), lay(np.sin(ang))


def kernel(x, ctx_512, L0_xattn_Wq, L0_xattn_w_kc_q, L0_xattn_w_kc_kv, L0_xattn_W_qr, L0_xattn_W_kr, L0_xattn_Wo,
           L0_ffn_Wr, L0_ffn_Wg, L0_ffn_Wu, L0_ffn_Wd, L1_xattn_Wq, L1_xattn_Wkv_expand, L1_xattn_Wout,
           L1_ffn_norm_w, L1_ffn_gate_w, L1_ffn_w13, L1_ffn_w2, L1_ffn_shared_gate_w, L1_ffn_shared_up_w,
           L1_ffn_shared_down_w):
    import concourse.bacc as _bacc
    from concourse.bass_utils import run_bass_kernel_spmd as _run

    def rows(a, r, p=P):
        return np.asarray(a).reshape(r // p, p, -1).transpose(1, 0, 2)

    cos, sin = _rope_tables()
    lay = {
        "x": np.asarray(x).reshape(N, D),
        "ctx": np.asarray(ctx_512).reshape(B * SK, DC),
        "cos": cos, "sin": sin,
        "w_kc_qT": np.asarray(L0_xattn_w_kc_q).transpose(2, 0, 1).reshape(KQ, P, H0, HK).transpose(1, 0, 2, 3),
        "w_qr": np.asarray(L0_xattn_W_qr).transpose(1, 0, 2).reshape(KQ, P, H0, R).transpose(1, 0, 2, 3),
        "wq0": rows(L0_xattn_Wq, H0 * HK),
        "w_kc_kv": np.asarray(L0_xattn_w_kc_kv).transpose(1, 0, 2),
        "wo0": rows(np.asarray(L0_xattn_Wo).T, H0 * HK),
        "w_kr": np.asarray(L0_xattn_W_kr).transpose(1, 0, 2),
        "wr0": rows(np.asarray(L0_ffn_Wr).T, D),
        "wgu0": np.concatenate([np.asarray(L0_ffn_Wg), np.asarray(L0_ffn_Wu)], axis=1).transpose(0, 2, 1).reshape(E0, KD, P, 2 * I0).transpose(0, 2, 1, 3),
        "wd0": np.asarray(L0_ffn_Wd).transpose(0, 2, 1),
        "ctxT": np.asarray(ctx_512)[:, 0:S, :].transpose(2, 0, 1).reshape(DC, B * S),
        "wq1": rows(np.asarray(L1_xattn_Wq).T, D),
        "wk1": np.asarray(L1_xattn_Wkv_expand)[0:D].T,
        "wv1": np.asarray(L1_xattn_Wkv_expand)[D:2 * D].T,
        "wo1": rows(np.asarray(L1_xattn_Wout).T, D),
        "norm_w": np.tile(np.asarray(L1_ffn_norm_w)[None], (P, 1)),
        "wr1": rows(np.asarray(L1_ffn_gate_w).T, D),
        "wgu1": np.concatenate([np.asarray(L1_ffn_w13)] + [np.concatenate([np.asarray(L1_ffn_shared_gate_w), np.asarray(L1_ffn_shared_up_w)], axis=1)[None]] * NSH)
                .reshape(E1 + NSH, KD, P, 2 * I1).transpose(0, 2, 1, 3),
        "wd1": np.concatenate([np.asarray(L1_ffn_w2)] + [np.asarray(L1_ffn_shared_down_w)[None]] * NSH),
    }
    nc = _bacc.Bacc("TRN2", target_bir_lowering=False, num_devices=1)
    arrays, g = {}, {}
    for name, a in lay.items():
        a = np.ascontiguousarray(a)
        arrays[f"in_{name}"] = a
        g[name] = nc.dram_tensor(f"in_{name}", a.shape, mybir.dt.from_np(a.dtype), kind="ExternalInput").ap()
    out = nc.dram_tensor("out_x", (N, D), F32, kind="ExternalOutput").ap()
    build_program(nc, g, out)
    r = _run(nc, [arrays], core_ids=[0])
    return r.results[0]["out_x"].reshape(B, S, D)
```

```python
from contextlib import ExitStack

import numpy as np

import concourse.bass as bass
from concourse import mybir

F32 = mybir.dt.float32
F32R = mybir.dt.float32r
BF16 = mybir.dt.bfloat16
I32 = mybir.dt.int32
U32 = mybir.dt.uint32
ACT = mybir.ActivationFunctionType
ALU = mybir.AluOpType
AX = mybir.AxisListType

P = 128
B, S, D = 4, 512, 512
SK, DC = 1024, 128
N = B * S
NT = N // P
TB = S // P
KD = D // P
LN_EPS = 1e-5
RMS_EPS = 1e-6

H0, HK, DCQ, R = 16, 128, 384, 64
KQ = DCQ // P
LT = SK // P
H1 = 16
HD = D // H1
GH = P // HD
NG = H1 // GH
NEG = -1e30
E0, K0, I0 = 8, 2, 352
CAP0 = int(1.25 * (N * K0 / E0))
E1, K1, I1 = 32, 4, 256
CAP1 = 2 * N * K1 // E1
NSH = N // CAP1


class Shared:
    pass


class MoeLayer:

    def __init__(self, name, E, K, I, cap, chunks, router, wgu, wd, rms, shared, choice_major, renorm, drop_weight, z_made):
        self.name, self.E, self.K, self.I, self.cap = name, E, K, I, cap
        self.chunks = chunks
        self.router, self.wgu, self.wd = router, wgu, wd
        self.rms = rms
        self.shared = shared
        self.choice_major = choice_major
        self.renorm = renorm
        self.drop_weight = drop_weight
        self.z_made = z_made


class Scope:

    def __init__(self, nc, name):
        self.nc, self.name, self.stack, self.sems = nc, name, ExitStack(), []

    def __enter__(self):
        self.stack.__enter__()
        return self

    def __exit__(self, *a):
        self.stack.__exit__(*a)
        if self.sems:
            self.nc.clear_and_free_semaphores(self.sems)
            self.nc.all_engine_barrier()

    def sb(self, name, shape, dt=F32):
        return self.stack.enter_context(self.nc.sbuf_tensor(f"{self.name}_{name}", shape, dt))

    def ps(self, name, shape=(P, 512), dt=F32):
        return self.stack.enter_context(self.nc.psum_tensor(f"{self.name}_{name}", list(shape), dt))

    def sem(self, name):
        self.sems.append(self.nc.alloc_semaphore(f"{self.name}_{name}"))
        return self.sems[-1]

    def block(self):
        return self.stack.enter_context(self.nc.Block())


def fold_weights(nc, t, g):
    HG = 4
    with Scope(nc, "fold") as s:
        kcq = s.sb("kcq", [P, KQ, H0, HK])
        wqr = s.sb("wqr", [P, KQ, H0, R])
        wq = s.sb("wq", [P, H0, D])
        kckv = s.sb("kckv", [P, H0, DC])
        wo = s.sb("wo", [P, H0, D])
        t1 = [s.sb(f"t1_{j}", [P, R]) for j in range(2)]
        ps_t1 = [s.ps(f"ps_t1_{j}") for j in range(2)]
        ps_wa = [s.ps(f"ps_wa_{j}") for j in range(2)]
        ps_mo = [s.ps(f"ps_mo_{j}") for j in range(2)]
        x_in = s.sem("x_in")
        q_in = [s.sem(f"q_in{j}") for j in range(H0 // HG)]
        v_in = [s.sem(f"v_in{j}") for j in range(H0 // HG)]
        t1_made, t1_copied, wa_made, wa_copied = (s.sem(n) for n in ("t1_made", "t1_copied", "wa_made", "wa_copied"))
        mo_made, mo_copied, ident_zeroed, consts_made = (s.sem(n) for n in ("mo_made", "mo_copied", "ident_zeroed", "consts_made"))
        block = s.block()

        @block.sync
        def _(sp):
            for h in range(0, H0, HG):
                hs = slice(h, h + HG)
                sp.dma_start(kcq[:, :, hs, :], g["w_kc_qT"][:, :, hs, :]).then_inc(q_in[h // HG], 16)
                sp.dma_start(wqr[:, :, hs, :], g["w_qr"][:, :, hs, :]).then_inc(q_in[h // HG], 16)
                sp.dma_start(kckv[:, hs, :], g["w_kc_kv"][:, hs, :]).then_inc(v_in[h // HG], 16)
                sp.dma_start(wo[:, hs, :], g["wo0"][:, hs, :]).then_inc(v_in[h // HG], 16)
                sp.dma_start(wq[:, hs, :], g["wq0"][:, hs, :]).then_inc(v_in[h // HG], 16)
            sp.dma_start(t.wkr[:], g["w_kr"]).then_inc(x_in, 16)
            sp.dma_start(t.x[:], g["x"].rearrange("(t p) d -> p t d", p=P)).then_inc(x_in, 16)
            sp.wait_ge(x_in, 32)

        @block.gpsimd
        def _(pool):
            pool.memset(t.ident[:], 0.0).then_inc(ident_zeroed, 1)
            pool.wait_ge(ident_zeroed, 1)
            pool.affine_select(out=t.ident[:], in_=t.ident[:], compare_op=ALU.not_equal, fill=1.0, base=0,
                               pattern=[[-1, P]], channel_multiplier=1).then_inc(consts_made, 1)
            pool.memset(t.ones[:], 1.0).then_inc(consts_made, 1)
            pool.memset(t.ln_eps[:], LN_EPS).then_inc(consts_made, 1)
            pool.memset(t.rms_eps[:], RMS_EPS).then_inc(consts_made, 1)
            pool.wait_ge(consts_made, 4)

        @block.tensor
        def _(pe):
            def first_product(h):
                pe.wait_ge(q_in[h // HG], 32)
                if h >= 2:
                    pe.wait_ge(t1_copied, h - 1)
                for q in range(KQ):
                    mm = pe.matmul(ps_t1[h % 2][:, 0:R], kcq[:, q, h, :], wqr[:, q, h, :], start=q == 0, stop=q == KQ - 1)
                mm.then_inc(t1_made, 1)

            first_product(0)
            for h in range(H0):
                if h + 1 < H0:
                    first_product(h + 1)
                pe.wait_ge(v_in[h // HG], 48)
                if h >= 2:
                    pe.wait_ge(mo_copied, h - 1)
                pe.matmul(ps_mo[h % 2][:], kckv[:, h, :], wo[:, h, :], start=True, stop=True).then_inc(mo_made, 1)
                pe.wait_ge(t1_copied, h + 1)
                if h >= 2:
                    pe.wait_ge(wa_copied, h - 1)
                for k in range(KD):
                    mm = pe.matmul(ps_wa[h % 2][:, k * R:(k + 1) * R], wq[:, h, k * P:(k + 1) * P], t1[h % 2][:],
                                   start=True, stop=True)
                mm.then_inc(wa_made, 1)

        @block.vector
        def _(dve):
            def copy_first(h):
                dve.wait_ge(t1_made, h + 1)
                if h >= 2:
                    dve.wait_ge(wa_made, h - 1)
                dve.tensor_copy(t1[h % 2][:], ps_t1[h % 2][:, 0:R]).then_inc(t1_copied, 1)

            copy_first(0)
            for h in range(H0):
                if h + 1 < H0:
                    copy_first(h + 1)
                dve.wait_ge(wa_made, h + 1)
                dve.tensor_copy(t.wa[:, h, :, :], ps_wa[h % 2][:, 0:KD * R].rearrange("p (k r) -> p k r", r=R)).then_inc(wa_copied, 1)
            dve.wait_ge(wa_copied, H0)

        @block.scalar
        def _(act):
            for h in range(H0):
                act.wait_ge(mo_made, h + 1)
                act.copy(t.mo[:, h, :], ps_mo[h % 2][:]).then_inc(mo_copied, 1)
            act.wait_ge(mo_copied, H0)


def latent_attention(nc, t, g):
    HALF = SK // 2
    PR = 4
    MAXIMA_AT = {2: (0,), 3: (1, 2), 4: (3, 4), 5: (5, 6), 6: (7,)}
    NM = 2 * TB
    with Scope(nc, "la") as s:
        ctx = s.sb("ctx", [P, LT, DC])
        kv = s.sb("kv", [P, LT, DC])
        kvT = s.sb("kvT", [P, SK])
        hqT = s.sb("hqT", [P, KD, S])
        stats, mv = s.sb("stats", [P, TB, 6]), s.sb("mv", [P, TB, 2])
        std, rstd = s.sb("std", [P, TB]), s.sb("rstd", [P, TB])
        was = [s.sb(f"was{j}", [P, KD, 2, R]) for j in range(2)]
        wks = [s.sb(f"wks{j}", [P, 2, R]) for j in range(2)]
        q1 = [s.sb(f"q1_{j}", [P, S], F32R) for j in range(2)]
        q2 = [s.sb(f"q2_{j}", [R + 1, S], F32R) for j in range(2)]
        k1 = [s.sb(f"k1_{j}", [P, SK], F32R) for j in range(2)]
        k2 = [s.sb(f"k2_{j}", [R + 1, SK], F32R) for j in range(2)]
        pmax = s.sb("pmax", [P, TB, 2])
        nmax = [s.sb(f"nmax{j}", [P, TB], F32R) for j in range(2)]
        identr = s.sb("identr", [P, P], F32R)
        kv_h, kv_l = (s.sb(f"kv_{part}", [P, LT, DC], F32R) for part in "hl")
        ring = s.sb("ring", [P, PR, S])
        probs = [ring[:, n, :] for n in range(PR)]
        probs_h, probs_l = ([s.sb(f"probs_{part}{n}", [P, S], F32R) for n in range(PR)] for part in "hl")
        summed = s.sb("summed", [P, 2, S])
        psum_p = [summed[:, j, :] for j in range(2)]
        hq = ring[:]
        rot = summed[:].rearrange("p a (c d) -> p (a c) d", d=DC)
        cosT = kvT[:].rearrange("p (c d) -> p c d", d=DC)
        sinT = hqT[:, 2:4, :].rearrange("p a (c d) -> p (a c) d", d=DC)
        rsum = [s.sb(f"rsum{j}", [P, TB]) for j in range(2)]
        rsum_row = s.sb("rsum_row", [P, S])
        spare = s.sb("spare", [P, 2])
        ctxT = s.sb("ctxT", [P, H0, S])
        misc = s.ps("misc")
        ps_k = s.ps("ps_k")
        ps_max = [s.ps(f"ps_max{j}") for j in range(2)]
        ps_k = [ps_k, ps_max[1]]
        ps_s = [s.ps(f"ps_s{j}") for j in range(2)]
        ps_o = [s.ps(f"ps_o{j}") for j in range(2)]
        tab_in, ctx_in, roped, kvT_tr, kvT_made = (s.sem(n) for n in ("tab_in", "ctx_in", "roped", "kvT_tr", "kvT_made"))
        ln_var, ln_std, ln_seq, hq_made, hq_tr, hqT_made = (s.sem(n) for n in ("ln_var", "ln_std", "ln_seq", "hq_made", "hq_tr", "hqT_made"))
        staged, q_made, q_high, q_low = (s.sem(n) for n in ("staged", "q_made", "q_high", "q_low"))
        k_made, k_high, k_low = (s.sem(n) for n in ("k_made", "k_high", "k_low"))
        smax, part_max, maxed, nm_row, nm_put = (s.sem(n) for n in ("smax", "part_max", "maxed", "nm_row", "nm_put"))
        s_made, p_made, p_seq, o_made, sum_made, sum_rec = (s.sem(n) for n in ("s_made", "p_made", "p_seq", "o_made", "sum_made", "sum_rec"))
        row_made, row_put, c_made, y_made, y_added = (s.sem(n) for n in ("row_made", "row_put", "c_made", "y_made", "y_added"))
        consts, p_high, p_low, kv_high, kv_low = (s.sem(n) for n in ("consts", "p_high", "p_low", "kv_high", "kv_low"))
        block = s.block()

        def heads(eng, b, before, step, after):
            before((b * H0, 0, 0))
            step((b * H0, 0, 0), first=True, last=False)
            with eng.Fori(0, (H0 - 2) // 2) as hp:
                step((b * H0 + hp * 2 + 1, hp * 2 + 1, 1), first=False, last=False)
                step((b * H0 + hp * 2 + 2, hp * 2 + 2, 0), first=False, last=False)
            step((b * H0 + H0 - 1, H0 - 1, 1), first=False, last=True)
            after((b * H0 + H0 - 1, H0 - 1, 1))

        def following(head, d=1):
            i, h, j = head
            return i + d, h + d, (j + d) % 2

        @block.sync
        def _(sp):
            sp.dma_start(cosT, g["cos"]).then_inc(tab_in, 16)
            sp.dma_start(sinT, g["sin"]).then_inc(tab_in, 16)
            sp.dma_start(ctx[:], g["ctx"][0:SK, :].rearrange("(l p) d -> p l d", p=P)).then_inc(ctx_in, 16)
            with sp.Fori(1, B) as b:
                sp.wait_ge(roped, b * 5)
                sp.dma_start(ctx[:], g["ctx"][bass.ds(b * SK, SK), :].rearrange("(l p) d -> p l d", p=P)).then_inc(ctx_in, 16)
                sp.wait_ge(q_made, b * H0)
                sp.dma_start(cosT, g["cos"]).then_inc(tab_in, 16)
                sp.dma_start(sinT, g["sin"]).then_inc(tab_in, 16)

        @block.gpsimd
        def _(pool):
            for j in range(2):
                pool.memset(k2[j][R:R + 1, :].bitcast(F32), 1.0).then_inc(consts, 1)

            def stage(head):
                i, h, j = head
                pool.tensor_tensor(spare[:, j:j + 1], t.ln_eps[:], t.ln_eps[:], ALU.add)
                for c in range(2):
                    pool.tensor_copy(was[j][:, :, c, :], t.wa[:, bass.ds(h, 1), :, :].rearrange("p o k r -> p (o k) r")).then_inc(staged, 1)
                for c in range(2):
                    pool.tensor_copy(wks[j][:, c, :], t.wkr[:, bass.ds(h, 1), :].rearrange("p o r -> p (o r)")).then_inc(staged, 1)

            def before(head):
                pool.wait_ge(sum_made, head[0] + 1)
                stage(head)
                stage(following(head))

            def step(head, first, last):
                i, h, j = head
                pool.wait_ge(p_made, i * LT + 2)
                pool.wait_ge(sum_made, i + 1)
                pool.tensor_tensor(psum_p[j], probs[0], probs[1], ALU.add).then_inc(p_seq, 1)
                for l in range(2, LT):
                    pool.wait_ge(p_made, i * LT + l + 1)
                    pool.wait_ge(p_seq, i * (LT - 1) + l - 1)
                    pool.tensor_tensor(psum_p[j], psum_p[j], probs[l % PR], ALU.add).then_inc(p_seq, 1)

            with pool.Fori(0, B) as b:
                before((b * H0, 0, 0))
                step((b * H0, 0, 0), True, False)
                pool.wait_ge(k_made, b * (2 * H0) + 4)
                stage((b * H0 + 2, 2, 0))
                with pool.Fori(0, (H0 - 4) // 2) as hp:
                    for d, j in ((1, 1), (2, 0)):
                        step((b * H0 + hp * 2 + d, hp * 2 + d, j), False, False)
                        pool.wait_ge(q_made, b * H0 + hp * 2 + d + 1)
                        stage((b * H0 + hp * 2 + d + 2, hp * 2 + d + 2, j))
                step((b * H0 + H0 - 3, H0 - 3, 1), False, False)
                pool.wait_ge(q_made, b * H0 + H0 - 2)
                stage((b * H0 + H0 - 1, H0 - 1, 1))
                step((b * H0 + H0 - 2, H0 - 2, 0), False, False)
                step((b * H0 + H0 - 1, H0 - 1, 1), False, True)

        @block.tensor
        def _(pe):
            def project_q(head, k):
                i, h, j = head
                if k == 0:
                    pe.wait_ge(staged, i * 4 + 4)
                mm = pe.matmul(misc[:], was[j][:, k, :, :].rearrange("p c r -> p (c r)"), hqT[:, k, :], start=k == 0, stop=k == KD - 1)
                if k == KD - 1:
                    mm.then_inc(q_made, 1)

            def project_k(head, half):
                i, h, j = head
                if half == 0:
                    pe.wait_ge(staged, i * 4 + 4)
                pe.matmul(ps_k[half][:], wks[j][:].rearrange("p c r -> p (c r)"), kvT[:, half * HALF:(half + 1) * HALF],
                          start=True, stop=True).then_inc(k_made, 1)

            def for_max(head, n):
                i, h, j = head
                st, half = n // 2, n % 2
                if n == 0:
                    pe.wait_ge(q_low, i + 1)
                    pe.wait_ge(k_high, i * 2 + 2)
                if n == 1:
                    pe.wait_ge(k_low, i * 2 + 2)
                if n >= 2:
                    pe.wait_ge(part_max, i * NM + n - 1)
                pe.matmul(ps_max[n % 2][:], q1[j][:, st * P:(st + 1) * P], k1[j][:, half * HALF:(half + 1) * HALF],
                          start=True, stop=True).then_inc(smax, 1)

            def max_row(head, first_of_batch):
                i, h, j = head
                pe.wait_ge(maxed, i + 1)
                if not first_of_batch:
                    pe.wait_ge(row_put, i)
                for st in range(TB):
                    mm = pe.matmul(misc[0:1, st * P:(st + 1) * P], nmax[j][:, st:st + 1], identr[:], start=True, stop=True)
                mm.then_inc(nm_row, 1)

            def scores(head, l):
                i, h, j = head
                if l == 0:
                    pe.wait_ge(nm_put, i + 1)
                    pe.wait_ge(k_low, i * 2 + 2)
                if l >= 2:
                    pe.wait_ge(p_made, i * LT + l - 1)
                pe.matmul(ps_s[l % 2][:], k1[j][:, l * P:(l + 1) * P], q1[j][:], start=True, stop=False)
                pe.matmul(ps_s[l % 2][:], k2[j][:, l * P:(l + 1) * P], q2[j][:], start=False, stop=True).then_inc(s_made, 1)

            def weigh(head, l):
                i, h, j = head
                if l == 0:
                    pe.wait_ge(c_made, i + 1)
                pe.wait_ge(p_low, i * LT + l + 1)
                pe.matmul(ps_o[j][:], kv_h[:, l, :], probs_h[l % PR][:], start=l == 0, stop=False)
                pe.matmul(ps_o[j][:], kv_h[:, l, :], probs_l[l % PR][:], start=False, stop=False)
                mm = pe.matmul(ps_o[j][:], kv_l[:, l, :], probs_h[l % PR][:], start=False, stop=l == LT - 1)
                if l == LT - 1:
                    mm.then_inc(o_made, 1)

            def sums(head, after_q):
                i, h, j = head
                pe.wait_ge(p_seq, i * (LT - 1) + LT - 1)
                if after_q:
                    pe.wait_ge(q_low, i + 3)
                else:
                    pe.wait_ge(row_put, i + 1)
                for st in range(TB):
                    mm = pe.matmul(misc[:, st:st + 1], psum_p[j][:, st * P:(st + 1) * P], t.ones[:, 0:1], start=True, stop=True)
                mm.then_inc(sum_made, 1)

            def sum_row(head):
                i, h, j = head
                pe.wait_ge(sum_rec, i + 1)
                for st in range(TB):
                    mm = pe.matmul(misc[:, st * P:(st + 1) * P], rsum[j][:, st:st + 1].to_broadcast([P, P]), t.ident[:], start=True, stop=True)
                mm.then_inc(row_made, 1)

            def before(head):
                pe.wait_ge(row_put, head[0] + 1)
                for k in range(KD):
                    project_q(head, k)
                for half in range(2):
                    project_k(head, half)
                for n in range(NM):
                    for_max(head, n)
                max_row(head, True)

            def step(head, first, last):
                nxt, prev = following(head), following(head, -1)
                scores(head, 0)
                scores(head, 1)
                for l in range(LT):
                    if not last:
                        if l == 0:
                            project_k(nxt, 0)
                            project_k(nxt, 1)
                        for n in MAXIMA_AT.get(l, ())[:1]:
                            for_max(nxt, n)
                    if not first and l == 5:
                        sum_row(prev)
                    if l + 2 < LT:
                        scores(head, l + 2)
                    if not last and l == 0:
                        for k in range(KD):
                            project_q(nxt, k)
                    if l:
                        weigh(head, l - 1)
                    if not last:
                        for n in MAXIMA_AT.get(l, ())[1:]:
                            for_max(nxt, n)
                    if not first and l == 3:
                        sums(prev, not last)
                if not last:
                    max_row(nxt, False)
                weigh(head, LT - 1)

            def after(head):
                sums(head, False)
                sum_row(head)

            pe.wait_ge(consts, 3)
            pe.sem_inc(row_put, 1)
            pe.sem_inc(c_made, 2)
            pe.sem_inc(y_added, 1)
            pe.sem_inc(k_made, 2)
            pe.sem_inc(sum_made, 2)
            with pe.Fori(0, B) as b:
                for k in range(KD):
                    pe.wait_ge(hq_made, b * TB + TB)
                    if k == 0:
                        pe.wait_ge(y_added, b * TB + 1)
                    if k >= 2:
                        pe.wait_ge(hqT_made, b * KD + k - 1)
                    for tt in range(TB):
                        tr = pe.transpose(ps_s[k % 2][:, tt * P:(tt + 1) * P], hq[:, tt, k * P:(k + 1) * P], t.ident[:])
                    tr.then_inc(hq_tr, 1)
                pe.wait_ge(roped, b * 5 + 5)
                pe.wait_ge(c_made, b * H0 + 2)
                for half in range(2):
                    for l in range(4):
                        tr = pe.transpose(ps_o[half][:, l * P:(l + 1) * P], kv[:, half * 4 + l, :], t.ident[:])
                    tr.then_inc(kvT_tr, 1)
                pe.wait_ge(hqT_made, b * KD + KD)
                pe.wait_ge(kvT_made, b * 2 + 2)
                pe.wait_ge(kv_low, b + 1)
                heads(pe, b, before, step, after)
                for tt in range(TB):
                    if tt >= 2:
                        pe.wait_ge(y_added, b * TB + tt)
                    pe.wait_ge(c_made, b * H0 + H0 + 2)
                    for h in range(H0):
                        mm = pe.matmul(ps_s[tt % 2][:], ctxT[:, h, tt * P:(tt + 1) * P], t.mo[:, h, :], start=h == 0, stop=h == H0 - 1)
                    mm.then_inc(y_made, 1)

        @block.scalar
        def _(act):
            def high_q(head):
                i, h, j = head
                act.wait_ge(q_made, i + 1)
                act.copy(q1[j][:], misc[:])
                act.copy(q2[j][0:R, :], misc[0:R, :]).then_inc(q_high, 1)

            def high_k(head, half):
                i, h, j = head
                act.wait_ge(k_made, i * 2 + half + 3)
                act.copy(k1[j][:, half * HALF:(half + 1) * HALF], ps_k[half][:]).then_inc(k_high, 1)

            def put_max(head):
                i, h, j = head
                act.wait_ge(nm_row, i + 1)
                act.copy(q2[j][R:R + 1, :], misc[0:1, :]).then_inc(nm_put, 1)

            def put_row(head):
                i, h, j = head
                act.wait_ge(row_made, i + 1)
                act.wait_ge(c_made, i + 2)
                act.copy(rsum_row[:], misc[:]).then_inc(row_put, 1)

            def before(head):
                high_q(head)
                high_k(head, 0)
                high_k(head, 1)
                put_max(head)

            def step(head, first, last):
                i, h, j = head
                nxt, prev = following(head), following(head, -1)
                for l in range(LT):
                    if l >= PR or not first:
                        act.wait_ge(p_low, i * LT + l - PR + 1)
                        act.wait_ge(p_seq, i * (LT - 1) + (max(l - PR, 1) if l >= PR else l - (LT - 1 - PR)))
                    act.wait_ge(s_made, i * LT + l + 1)
                    act.activation(probs[l % PR], ps_s[l % 2][:], ACT.Exp).then_inc(p_made, 1)
                    act.wait_ge(p_made, i * LT + l + 1)
                    act.copy(probs_h[l % PR][:], probs[l % PR]).then_inc(p_high, 1)
                    if not last:
                        if l == 1:
                            high_k(nxt, 0)
                            high_k(nxt, 1)
                        if l == 2:
                            high_q(nxt)
                    if not first and l == 6:
                        put_row(prev)
                if not last:
                    put_max(nxt)

            with act.Fori(0, B) as b:
                act.wait_ge(ln_var, b + 1)
                act.activation(std[:], mv[:, :, 1], ACT.Sqrt, bias=t.ln_eps[:]).then_inc(ln_std, 1)
                for k in range(KD):
                    if k == 2:
                        act.wait_ge(roped, b * 5 + 2)
                    act.wait_ge(hq_tr, b * KD + k + 1)
                    act.copy(hqT[:, k, :], ps_s[k % 2][:]).then_inc(hqT_made, 1)
                for half in range(2):
                    act.wait_ge(kvT_tr, b * 2 + half + 1)
                    act.copy(kvT[:, half * HALF:(half + 1) * HALF], ps_o[half][:]).then_inc(kvT_made, 1)
                heads(act, b, before, step, put_row)

        @block.vector
        def _(dve):
            def low_q(head):
                i, h, j = head
                dve.wait_ge(q_high, i + 1)
                dve.tensor_tensor(q1[j][R:P, :], misc[R:P, :], q1[j][R:P, :].bitcast(F32), ALU.subtract).then_inc(q_low, 1)

            def low_k(head, half):
                i, h, j = head
                dve.wait_ge(k_high, i * 2 + half + 1)
                hs = slice(half * HALF, (half + 1) * HALF)
                dve.tensor_tensor(k2[j][0:R, hs], ps_k[half][0:R, :], k1[j][0:R, hs].bitcast(F32), ALU.subtract).then_inc(k_low, 1)

            def maximum(head, n):
                i, h, j = head
                dve.wait_ge(smax, i * NM + n + 1)
                dve.tensor_reduce(pmax[:, n // 2, n % 2:n % 2 + 1], ps_max[n % 2][:], AX.X, ALU.max).then_inc(part_max, 1)
                if n == NM - 1:
                    dve.wait_ge(part_max, i * NM + NM)
                    dve.tensor_reduce(nmax[j][:], pmax[:], AX.X, ALU.max, negate=True).then_inc(maxed, 1)

            def reciprocal(head):
                i, h, j = head
                dve.wait_ge(sum_made, i + 3)
                dve.reciprocal(rsum[j][:], misc[:, 0:TB]).then_inc(sum_rec, 1)

            def normalize(head):
                i, h, j = head
                dve.wait_ge(row_put, i + 2)
                dve.wait_ge(o_made, i + 1)
                dve.tensor_tensor(ctxT[:, bass.ds(h, 1), :].rearrange("p o s -> p (o s)"), ps_o[j][:], rsum_row[:], ALU.mult).then_inc(c_made, 1)

            def before(head):
                low_q(head)
                low_k(head, 0)
                low_k(head, 1)
                for n in range(NM):
                    maximum(head, n)

            def step(head, first, last):
                i, h, j = head
                nxt, prev = following(head), following(head, -1)
                for l in range(LT):
                    dve.wait_ge(p_high, i * LT + l + 1)
                    dve.tensor_tensor(probs_l[l % PR][:], probs[l % PR], probs_h[l % PR][:].bitcast(F32), ALU.subtract).then_inc(p_low, 1)
                    if not last:
                        if l == 1:
                            low_k(nxt, 0)
                            low_k(nxt, 1)
                        if l == 2:
                            low_q(nxt)
                        for n in MAXIMA_AT.get(l - 1, ()):
                            maximum(nxt, n)
                    if not first and l == 4:
                        reciprocal(prev)
                if not first:
                    normalize(prev)

            def after(head):
                reciprocal(head)
                normalize(head)

            dve.tensor_copy(identr[:], t.ident[:]).then_inc(consts, 1)
            with dve.Fori(0, B) as b:
                for tt in range(TB):
                    dve.bn_stats(stats[:, tt, :], t.x[:, bass.ds(b * TB + tt, 1), :].rearrange("p o d -> p (o d)")).then_inc(ln_seq, 1)
                dve.wait_ge(ln_seq, b * (TB + 1) + TB)
                dve.memset(rstd[:], 0.0)
                for tt in range(TB):
                    ag = dve.bn_aggr(mv[:, tt, :], stats[:, tt, :])
                ag.then_inc(ln_var, 1)
                dve.wait_ge(ln_std, b + 1)
                dve.reciprocal(rstd[:], std[:]).then_inc(ln_seq, 1)
                dve.wait_ge(ln_seq, b * (TB + 1) + TB + 1)
                for tt in range(TB):
                    dve.tensor_scalar(hq[:, tt, :], t.x[:, bass.ds(b * TB + tt, 1), :].rearrange("p o d -> p (o d)"), mv[:, tt, 0:1], rstd[:, tt:tt + 1],
                                      ALU.subtract, ALU.mult).then_inc(hq_made, 1)
                dve.wait_ge(tab_in, b * 32 + 32)
                dve.wait_ge(ctx_in, b * 16 + 16)
                dve.tensor_tensor(rot[:, :, 0:DC // 2], ctx[:, :, DC // 2:DC], sinT[:, :, 0:DC // 2], ALU.mult).then_inc(roped, 1)
                dve.tensor_tensor(rot[:, :, DC // 2:DC], ctx[:, :, 0:DC // 2], sinT[:, :, DC // 2:DC], ALU.mult).then_inc(roped, 1)
                dve.tensor_tensor(kv[:], ctx[:], cosT[:], ALU.mult).then_inc(roped, 1)
                dve.wait_ge(roped, b * 5 + 3)
                dve.tensor_tensor(kv[:, :, 0:DC // 2], kv[:, :, 0:DC // 2], rot[:, :, 0:DC // 2], ALU.subtract).then_inc(roped, 1)
                dve.tensor_tensor(kv[:, :, DC // 2:DC], kv[:, :, DC // 2:DC], rot[:, :, DC // 2:DC], ALU.add).then_inc(roped, 1)
                dve.wait_ge(roped, b * 5 + 5)
                dve.tensor_copy(kv_h[:], kv[:]).then_inc(kv_high, 1)
                dve.wait_ge(kv_high, b + 1)
                dve.tensor_tensor(kv_l[:], kv[:], kv_h[:].bitcast(F32), ALU.subtract).then_inc(kv_low, 1)
                heads(dve, b, before, step, after)
                for tt in range(TB):
                    dve.wait_ge(y_made, b * TB + tt + 1)
                    xt = t.x[:, bass.ds(b * TB + tt, 1), :].rearrange("p o d -> p (o d)")
                    dve.tensor_tensor(xt, ps_s[tt % 2][:], xt, ALU.add).then_inc(y_added, 1)


def route(nc, t, g, m):
    E, K, cap = m.E, m.K, m.cap
    F = NT * K if m.choice_major else NT
    KT = K * NT
    SLOTS = E * cap
    GT = SLOTS // P
    with Scope(nc, f"rt{m.name}") as s:
        xn = s.sb("xn", [P, NT, D])
        stats, mv = s.sb("stats", [P, NT, 6]), s.sb("mv", [P, NT, 2])
        std, rstd = s.sb("std", [P, NT]), s.sb("rstd", [P, NT])
        wr = s.sb("wr", [P, KD, E])
        xT = [s.sb(f"xT{j}", [P, KD * P]) for j in range(2)]
        lg, ex = s.sb("lg", [P, NT, E]), s.sb("ex", [P, NT, E])
        v8, i8 = s.sb("v8", [P, NT, 8]), s.sb("i8", [P, NT, 8], U32)
        idxf = s.sb("idxf", [P, K, NT])
        dv = s.sb("dv", [P, K, NT])
        den = s.sb("den", [P, NT])
        iota_e = s.sb("iota_e", [P, E])
        tri = s.sb("tri", [P, P])
        masks = s.sb("masks", [P, KT, E])
        queue = masks if m.choice_major else s.sb("queue", [P, NT, E])
        tot = s.sb("tot", [P, F, E])
        pre = [s.sb(f"pre{j}", [P, F, E]) for j in range(2)]
        rank = s.sb("rank", [P, KT])
        sel = s.sb("sel", [P, KT, E])
        keep, base, slotf = s.sb("keep", [P, KT]), s.sb("base", [P, KT]), s.sb("slotf", [P, KT])
        dslot = t.dslot if m.shared else s.sb("dslot", [P, KT], I32)
        tokid = t.tokid if m.shared else s.sb("tokid", [P, NT])
        zero = s.sb("zero", [P, P])
        tab = s.sb("tab", [P, P])
        junk = s.sb("junk", [P, 2, D])
        ps_tr = [s.ps(f"ps_tr{j}") for j in range(2)]
        ps_l, ps_tot, ps_rk, ps_tab = (s.ps(n) for n in ("ps_l", "ps_tot", "ps_rk", "ps_tab"))
        w_in, consts, var_ready, std_ready, chain = (s.sem(n) for n in ("w_in", "consts", "var", "std", "chain"))
        xn_made, xn_out, tr_made, xT_made, l_made = (s.sem(n) for n in ("xn_made", "xn_out", "tr_made", "xT_made", "l_made"))
        ex_in, ex_made, q_ready, q_summed, slots_ready = (s.sem(n) for n in ("ex_in", "ex_made", "q_ready", "q_summed", "slots_ready"))
        scattered, tab_in, tab_tr, zeroed = (s.sem(n) for n in ("scattered", "tab_in", "tab_tr", "zeroed"))
        block = s.block()

        @block.sync
        def _(sp):
            sp.dma_start(wr[:], g[m.router]).then_inc(w_in, 16)
            if m.rms:
                sp.dma_start(t.norm_w[:], g["norm_w"]).then_inc(w_in, 16)
            sp.wait_ge(consts, 2)
            sp.dma_start(m.table.rearrange("(n p) o -> n (p o)", p=P), zero[0:GT, :]).then_inc(zeroed, 16)
            for tt in range(NT):
                sp.wait_ge(xn_made, tt + 1)
                sp.dma_start(m.xn_dram[tt * P:(tt + 1) * P, :], xn[:, tt, :]).then_inc(xn_out, 16)
            sp.wait_ge(xn_out, 16 * NT)
            if m.shared:
                sp.wait_ge(zeroed, 16)
            else:
                sp.wait_ge(scattered, 16 * KT)
                sp.dma_start(tab[0:GT, :], m.table.rearrange("(n p) o -> n (p o)", p=P)).then_inc(tab_in, 16)
                sp.wait_ge(tab_in, 16)

        @block.gpsimd
        def _(pool):
            pool.memset(t.gidx[:], 0).then_inc(consts, 1)
            pool.memset(zero[:], 0.0).then_inc(consts, 1)
            pool.iota(iota_e[:], pattern=[[1, E]], base=0, channel_multiplier=0, allow_small_or_imprecise_dtypes=True).then_inc(consts, 1)
            pool.iota(tokid[:], pattern=[[P, NT]], base=0, channel_multiplier=1, allow_small_or_imprecise_dtypes=True).then_inc(consts, 1)
            pool.memset(tri[:], 1.0).then_inc(consts, 1)
            pool.wait_ge(consts, 5)
            pool.affine_select(out=tri[:], in_=tri[:], compare_op=ALU.is_gt, fill=0.0, base=0,
                               pattern=[[1, P]], channel_multiplier=-1).then_inc(consts, 1)
            if not m.shared:
                pool.wait_ge(slots_ready, 1)
                pool.wait_ge(zeroed, 16)
                for c in range(KT):
                    put_token(pool, t, m, dslot, tokid, c).then_inc(scattered, 16)
                pool.wait_ge(scattered, 16 * KT)

        @block.tensor
        def _(pe):
            pe.wait_ge(w_in, 16)
            for tt in range(NT + 1):
                if tt < NT:
                    pe.wait_ge(xn_made, tt + 1)
                    if tt >= 2:
                        pe.wait_ge(xT_made, tt - 1)
                    for k in range(KD):
                        mm = pe.transpose(ps_tr[tt % 2][:, k * P:(k + 1) * P], xn[:, tt, k * P:(k + 1) * P], t.ident[:])
                    mm.then_inc(tr_made, 1)
                if tt >= 1:
                    pe.wait_ge(xT_made, tt)
                    for k in range(KD):
                        mm = pe.matmul(ps_l[:, (tt - 1) * E:tt * E], xT[(tt - 1) % 2][:, k * P:(k + 1) * P], wr[:, k, :], start=k == 0, stop=k == KD - 1)
                    mm.then_inc(l_made, 1)
            pe.wait_ge(q_ready, 1)
            pe.wait_ge(consts, 6)
            pe.matmul(ps_tot[:, 0:F * E], t.ones[:], queue[:, 0:F, :].rearrange("p f e -> p (f e)"), start=True, stop=True).then_inc(q_summed, 1)
            pe.matmul(ps_rk[:, 0:F * E], tri[:], queue[:, 0:F, :].rearrange("p f e -> p (f e)"), start=True, stop=True).then_inc(q_summed, 1)
            if not m.shared:
                pe.wait_ge(tab_in, 16)
                pe.transpose(ps_tab[:, 0:GT], tab[0:GT, :], t.ident[0:GT, 0:GT]).then_inc(tab_tr, 1)

        @block.scalar
        def _(act):
            act.wait_ge(var_ready, 1)
            act.activation(std[:], mv[:, :, 1], ACT.Sqrt, bias=t.ln_eps[:]).then_inc(std_ready, 1)
            if m.rms:
                for tt in range(NT):
                    act.wait_ge(chain, m.z_made + tt)
                    if tt >= 2:
                        act.wait_ge(ex_made, tt - 1)
                    act.activation(junk[:, tt % 2, :], xn[:, tt, :], ACT.Square, accum_out=den[:, tt:tt + 1]).then_inc(ex_made, 1)
                act.wait_ge(ex_made, NT)
                act.activation(std[:], den[:], ACT.Sqrt, bias=t.rms_eps[:], scale=1.0 / D).then_inc(std_ready, 1)
            for tt in range(NT):
                act.wait_ge(tr_made, tt + 1)
                if tt >= 2:
                    act.wait_ge(l_made, tt - 1)
                act.copy(xT[tt % 2][:], ps_tr[tt % 2][:]).then_inc(xT_made, 1)
            act.wait_ge(ex_in, 1)
            act.activation(ex[:], lg[:], ACT.Exp).then_inc(ex_made, 1)
            act.activation(dv[:], dv[:], ACT.Exp).then_inc(ex_made, 1)

        @block.vector
        def _(dve):
            n = [0]

            def link(ins):
                n[0] += 1
                ins.then_inc(chain, 1)
                dve.wait_ge(chain, n[0])

            for tt in range(NT):
                ins = dve.bn_stats(stats[:, tt, :], t.x[:, tt, :])
            link(ins)
            for tt in range(NT):
                ins = dve.bn_aggr(mv[:, tt, :], stats[:, tt, :])
            ins.then_inc(var_ready, 1)
            dve.wait_ge(std_ready, 1)
            link(dve.reciprocal(rstd[:], std[:]))
            assert n[0] == 2
            for tt in range(NT):
                ins = dve.tensor_scalar(xn[:, tt, :], t.x[:, tt, :], mv[:, tt, 0:1], rstd[:, tt:tt + 1], ALU.subtract, ALU.mult)
                if m.rms:
                    n[0] += 1
                    ins.then_inc(chain, 1)
                else:
                    ins.then_inc(xn_made, 1)
            if m.rms:
                dve.wait_ge(chain, n[0])
                link(dve.tensor_tensor(t.x[:], t.x[:], xn[:], ALU.add))
                dve.wait_ge(std_ready, 2)
                link(dve.reciprocal(rstd[:], std[:]))
                dve.wait_ge(w_in, 32)
                for tt in range(NT):
                    dve.scalar_tensor_tensor(out=xn[:, tt, :], in0=xn[:, tt, :], scalar=rstd[:, tt:tt + 1], in1=t.norm_w[:],
                                             op0=ALU.mult, op1=ALU.mult).then_inc(xn_made, 1)
            dve.wait_ge(l_made, NT)
            link(dve.tensor_copy(lg[:], ps_l[:, 0:NT * E].rearrange("p (t e) -> p t e", e=E)))
            for tt in range(NT):
                ins = dve.max(v8[:, tt, :], lg[:, tt, :])
            link(ins)
            for tt in range(NT):
                ins = dve.max_index(i8[:, tt, :], v8[:, tt, :], lg[:, tt, :])
            link(ins)
            link(dve.tensor_copy(idxf[:], i8[:, :, 0:K].rearrange("p t k -> p k t")))
            dve.tensor_tensor(dv[:], v8[:, :, 0:K].rearrange("p t k -> p k t"), v8[:, :, 0:1].rearrange("p t o -> p o t").to_broadcast([P, K, NT]), ALU.subtract)
            dve.tensor_tensor(lg[:], lg[:], v8[:, :, 0:1].to_broadcast([P, NT, E]), ALU.subtract).then_inc(ex_in, 1)
            dve.wait_ge(consts, 4)
            link(dve.tensor_tensor(masks[:], iota_e[:].rearrange("p (o e) -> p o e", o=1).to_broadcast([P, KT, E]),
                                   idxf[:].rearrange("p k (t o) -> p (k t) o", o=1).to_broadcast([P, KT, E]), ALU.is_equal))
            if not m.choice_major:
                link(dve.tensor_tensor(queue[:], masks[:, 0:NT, :], masks[:, NT:2 * NT, :], ALU.add))
                for k in range(2, K):
                    link(dve.tensor_tensor(queue[:], queue[:], masks[:, k * NT:(k + 1) * NT, :], ALU.add))
            dve.sem_inc(q_ready, 1)
            dve.wait_ge(ex_made, 2 + (NT if m.rms else 0))
            if m.renorm:
                link(dve.tensor_reduce(den[:], dv[:].rearrange("p k t -> p t k"), AX.X, ALU.add))
            else:
                link(dve.tensor_reduce(den[:], ex[:], AX.X, ALU.add))
            link(dve.reciprocal(den[:], den[:]))
            link(dve.tensor_tensor(t.gate[:, 0:KT].rearrange("p (k t) -> p k t", t=NT), dv[:], den[:].rearrange("p (o t) -> p o t", o=1).to_broadcast([P, K, NT]), ALU.mult))
            dve.wait_ge(q_summed, 2)
            link(dve.tensor_copy(tot[:], ps_tot[:, 0:F * E].rearrange("p (f e) -> p f e", e=E)))
            src, step, j = tot, 1, 0
            while step < F:
                dve.tensor_copy(pre[j][:, 0:step, :], src[:, 0:step, :])
                link(dve.tensor_tensor(pre[j][:, step:F, :], src[:, step:F, :], src[:, 0:F - step, :], ALU.add))
                src, step, j = pre[j], step * 2, 1 - j
            link(dve.tensor_tensor(tot[:], src[:], tot[:], ALU.subtract))
            link(dve.tensor_tensor(tot[:], ps_rk[:, 0:F * E].rearrange("p (f e) -> p f e", e=E), tot[:], ALU.add))
            if m.choice_major:
                link(dve.tensor_tensor(sel[:], masks[:], tot[:], ALU.mult))
            else:
                for k in range(K):
                    ins = dve.tensor_tensor(sel[:, k * NT:(k + 1) * NT, :], masks[:, k * NT:(k + 1) * NT, :], tot[:], ALU.mult)
                link(ins)
            link(dve.tensor_reduce(rank[:], sel[:], AX.X, ALU.add))
            link(dve.tensor_scalar(base[:], idxf[:].rearrange("p k t -> p (k t)"), float(cap), None, ALU.mult))
            link(dve.tensor_scalar(keep[:], rank[:], float(cap), None, ALU.is_lt))
            link(dve.tensor_scalar(slotf[:], keep[:], -float(2 * SLOTS), float(2 * SLOTS), ALU.mult, ALU.add))
            link(dve.tensor_tensor(slotf[:], slotf[:], rank[:], ALU.add))
            link(dve.tensor_tensor(slotf[:], slotf[:], base[:], ALU.add))
            link(dve.tensor_copy(dslot[:], slotf[:]))
            dve.sem_inc(slots_ready, 1)
            if m.shared:
                link(dve.tensor_scalar(rank[:], rank[:], float(cap - 1), float(NSH * cap), ALU.min, ALU.add))
            else:
                link(dve.tensor_scalar(rank[:], rank[:], float(cap - 1), None, ALU.min))
            link(dve.tensor_tensor(rank[:], rank[:], base[:], ALU.add))
            link(dve.tensor_copy(t.slot[:, 0:KT], rank[:]))
            if m.drop_weight:
                link(dve.tensor_tensor(t.gate[:, 0:KT], t.gate[:, 0:KT], keep[:], ALU.mult))
            if m.shared:
                link(dve.tensor_copy(t.gidx[:, 0:NT], tokid[:]))
            else:
                dve.wait_ge(tab_tr, 1)
                link(dve.tensor_copy(t.gidx[:, 0:GT], ps_tab[:, 0:GT]))


def put_token(pool, t, m, dslot, tokid, c):
    return pool.indirect_dma_start(out=m.table, out_offset=bass.IndirectOffsetOnAxis(ap=dslot[:, c:c + 1], axis=0),
                                   in_=tokid[:, c % NT:c % NT + 1], in_offset=None,
                                   bounds_check=m.E * m.cap - 1, oob_is_err=False)


def experts(nc, t, g, m):
    NE = m.E + (NSH if m.shared else 0)
    cap, I = m.cap, m.I
    CT = cap // P
    CH = cap // m.chunks
    IS = [min(P, I - i) for i in range(0, I, P)]
    IT = len(IS)
    NGU = IT * m.chunks
    PIECES = KD + IT
    KT, GT = m.K * NT, m.E * m.cap // P
    with Scope(nc, f"ex{m.name}") as s:
        wgu = [s.sb(f"wgu{j}", [P, KD, 2 * I]) for j in range(2)]
        wd = [s.sb(f"wd{j}", [P, IT, D]) for j in range(2)]
        wgu_h, wgu_l = ([s.sb(f"wgu_{part}{j}", [P, KD, 2 * I], F32R) for j in range(2)] for part in "hl")
        wd_h, wd_l = ([s.sb(f"wd_{part}{j}", [P, IT, D], F32R) for j in range(2)] for part in "hl")
        idx = [s.sb(f"idx{j}", [P, CT], I32) for j in range(2)]
        xg = [s.sb(f"xg{j}", [P, CT, D]) for j in range(2)]
        xT_h, xT_l = (s.sb(f"xT_{part}", [P, KD, cap], F32R) for part in "hl")
        sg = [s.sb(f"sg{j}", [P, CH]) for j in range(2)]
        h = [s.sb(f"h{j}", [P, CH]) for j in range(2)]
        hT_h, hT_l = (s.sb(f"hT_{part}", [P, IT, cap], F32R) for part in "hl")
        y = [s.sb(f"y{c}", [P, D]) for c in range(CT)]
        ps_tr = [s.ps(f"ps_tr{j}") for j in range(2)]
        ps_g = [s.ps(f"ps_g{j}") for j in range(2)]
        ps_u = [s.ps(f"ps_u{j}") for j in range(2)]
        ps_y = [s.ps(f"ps_y{j}") for j in range(2)]
        turn, turned = s.sb("turn", [P, 2]), s.sem("turned")
        tab = s.sb("tab", [P, P]) if m.shared else None
        scattered, tab_in, tab_tr, tab_put = (s.sem(n) for n in ("scattered", "tab_in", "tab_tr", "tab_put"))
        w_in = [s.sem(f"w_in{j}") for j in range(2)]
        x_in = [s.sem(f"x_in{j}") for j in range(2)]
        w_high, w_low, idx_made, tr_made, x_high, x_low = (s.sem(n) for n in ("w_high", "w_low", "idx_made", "tr_made", "x_high", "x_low"))
        gu_made, sg_made, h_made, h_high, h_low = (s.sem(n) for n in ("gu_made", "sg_made", "h_made", "h_high", "h_low"))
        y_made, y_put = s.sem("y_made"), s.sem("y_put")
        y_out = [s.sem(f"y_out{c}") for c in range(CT)]
        block = s.block()
        WD = 16 * (2 if IS[-1] == P else 3)

        def all_experts(eng, before, body):
            before((0, 0, 0))
            if m.shared:
                for e in range(NSH):
                    body((e, e // 2, e % 2), last=False, table=e - NSH)
            with eng.Fori(NSH // 2 if m.shared else 0, NE // 2 - 1) as ep:
                body((ep * 2, ep, 0), last=False)
                body((ep * 2 + 1, ep, 1), last=False)
            body((NE - 2, NE // 2 - 1, 0), last=False)
            body((NE - 1, NE // 2 - 1, 1), last=True)

        def following(expert):
            e, ep, j = expert
            return e + 1, ep + j, 1 - j

        def piece(j, n):
            if n < KD:
                return wgu[j][:, n, :], wgu_h[j][:, n, :], wgu_l[j][:, n, :]
            r = IS[n - KD]
            return wd[j][0:r, n - KD, :], wd_h[j][0:r, n - KD, :], wd_l[j][0:r, n - KD, :]

        @block.sync
        def _(sp):
            def load_weights(e, j):
                sp.dma_start(wgu[j][:], g[m.wgu][bass.ds(e, 1), :, :, :].rearrange("o p k i -> (o p) k i")).then_inc(w_in[j], 16)
                full = I // P * P
                sp.dma_start(wd[j][:, 0:I // P, :], g[m.wd][bass.ds(e, 1), 0:full, :].rearrange("o (i p) d -> (o p) i d", p=P)).then_inc(w_in[j], 16)
                if full < I:
                    sp.dma_start(wd[j][0:I - full, IT - 1, :], g[m.wd][bass.ds(e, 1), full:I, :].rearrange("o p d -> (o p) d")).then_inc(w_in[j], 16)

            def store(e):
                for c in range(CT):
                    sp.wait_ge(y_put, e * CT + c + 3)
                    sp.dma_start(m.y_dram[bass.ds((e * CT + c) * P, P), :], y[c][:]).then_inc(y_out[c], 16)

            for c in range(CT):
                sp.sem_inc(y_out[c], 16)
            load_weights(0, 0)
            load_weights(1, 1)

            def body(expert, last, table=0):
                e, ep, j = expert
                if table == -1:
                    sp.wait_ge(scattered, 16 * KT)
                    sp.dma_start(tab[0:GT, :], m.table.rearrange("(n p) o -> n (p o)", p=P)).then_inc(tab_in, 16)
                sp.wait_ge(w_low, ep * (2 * PIECES) + (j + 1) * PIECES)
                load_weights(e + 2, j)
                store(e)

            if m.shared:
                for e in range(NSH):
                    body((e, e // 2, e % 2), last=False, table=e - NSH)
            with sp.Fori(NSH // 2 if m.shared else 0, NE // 2 - 1) as ep:
                for j in range(2):
                    body((ep * 2 + j, ep, j), last=False)
            store(NE - 2)
            store(NE - 1)
            for c in range(CT):
                sp.wait_ge(y_out[c], 16 * NE + 16)

        @block.gpsimd
        def _(pool):
            def gather(j):
                for c in range(CT):
                    pool.indirect_dma_start(out=xg[j][:, c, :], out_offset=None, in_=m.xn_dram,
                                            in_offset=bass.IndirectOffsetOnAxis(ap=idx[j][:, c:c + 1], axis=0),
                                            bounds_check=last_token, oob_is_err=False).then_inc(x_in[j], 16)

            last_token = pool.to_reg(N - 1)
            pool.memset(turn[:], 0.0).then_inc(turned, 1)
            pool.wait_ge(turned, 1)
            if m.shared:
                for e in range(NSH):
                    pool.wait_ge(idx_made, e + 1)
                    pool.wait_ge(turned, e + 1)
                    pool.tensor_tensor(turn[:, 1:2], turn[:, 0:1], turn[:, 0:1], ALU.add).then_inc(turned, 1)
                    gather(e % 2)
                    for c in range(max(e - 1, 0) * (KT // NSH), e * (KT // NSH) if e < NSH - 1 else KT):
                        put_token(pool, t, m, t.dslot, t.tokid, c).then_inc(scattered, 16)
            with pool.Fori(NSH // 2 if m.shared else 0, NE // 2) as ep:
                for j in range(2):
                    e = ep * 2 + j
                    pool.wait_ge(idx_made, e + 1)
                    pool.wait_ge(turned, e + 1)
                    pool.tensor_tensor(turn[:, 1:2], turn[:, 0:1], turn[:, 0:1], ALU.add).then_inc(turned, 1)
                    gather(j)

        @block.tensor
        def _(pe):
            def three(out, w_parts, x_parts, start, stop):
                (wh, wl), (xh, xl) = w_parts, x_parts
                pe.matmul(out, wh, xh, start=start, stop=False)
                pe.matmul(out, wh, xl, start=False, stop=False)
                return pe.matmul(out, wl, xh, start=False, stop=stop)

            def transposes(expert):
                e, ep, j = expert
                pe.wait_ge(x_in[j], ep * (16 * CT) + 16 * CT)
                for c in range(CT):
                    pe.wait_ge(x_low, e * CT + c + 1)
                    for k in range(KD):
                        mm = pe.transpose(ps_tr[(j * CT + c) % 2][:, k * P:(k + 1) * P], xg[j][:, c, k * P:(k + 1) * P], t.ident[:])
                    mm.then_inc(tr_made, 1)

            def gate_up(expert):
                e, ep, j = expert
                pe.wait_ge(w_low, e * PIECES + PIECES)
                pe.wait_ge(x_low, e * CT + CT + 2)
                for a in range(NGU):
                    it, ch = a // m.chunks, a % m.chunks
                    cols = slice(ch * CH, (ch + 1) * CH)
                    pe.wait_ge(h_made, e * NGU + a + 1)
                    for base, ps in ((0, ps_g), (I, ps_u)):
                        rows = slice(base + it * P, base + it * P + IS[it])
                        for k in range(KD):
                            mm = three(ps[a % 2][0:IS[it], 0:CH], (wgu_h[j][:, k, rows], wgu_l[j][:, k, rows]),
                                       (xT_h[:, k, cols], xT_l[:, k, cols]), k == 0, k == KD - 1)
                    mm.then_inc(gu_made, 1)

            def down(expert):
                e, ep, j = expert
                pe.wait_ge(h_low, e * NGU + NGU + 2)
                for c in range(CT):
                    pe.wait_ge(y_put, e * CT + c + 1)
                    cols = slice(c * P, (c + 1) * P)
                    for it in range(IT):
                        r = IS[it]
                        mm = three(ps_y[(j * CT + c) % 2][:], (hT_h[0:r, it, cols], hT_l[0:r, it, cols]),
                                   (wd_h[j][0:r, it, :], wd_l[j][0:r, it, :]), it == 0, it == IT - 1)
                    mm.then_inc(y_made, 1)

            def body(expert, last, table=0):
                gate_up(expert)
                if table == -1:
                    down(expert)
                    pe.wait_ge(tab_in, 16)
                    pe.transpose(ps_tr[1][:, 0:GT], tab[0:GT, :], t.ident[0:GT, 0:GT]).then_inc(tab_tr, 1)
                    transposes(following(expert))
                    return
                if not last:
                    transposes(following(expert))
                down(expert)

            pe.sem_inc(x_low, 2)
            pe.sem_inc(h_made, 2)
            pe.sem_inc(h_low, 2)
            pe.sem_inc(y_put, 2)
            pe.sem_inc(y_made, CT)
            all_experts(pe, transposes, body)

        @block.scalar
        def _(act):
            def split_weights(expert, pieces):
                e, ep, j = expert
                for n in pieces:
                    raw, high, low = piece(j, n)
                    if n == 0:
                        act.wait_ge(w_in[j], ep * WD + WD)
                        act.wait_ge(y_made, e * CT)
                    act.copy(high, raw).then_inc(w_high, 1)

            def high_x(expert):
                e, ep, j = expert
                for c in range(CT):
                    act.wait_ge(tr_made, e * CT + c + 1)
                    act.copy(xT_h[:, :, c * P:(c + 1) * P], ps_tr[(j * CT + c) % 2][:].rearrange("p (k c) -> p k c", c=P)).then_inc(x_high, 1)

            def before(expert):
                split_weights(expert, range(PIECES))
                high_x(expert)

            def body(expert, last, table=0):
                e, ep, j = expert
                if not last:
                    split_weights(following(expert), range(KD))
                for a in range(NGU):
                    i = e * NGU + a
                    it, ch = a // m.chunks, a % m.chunks
                    r = IS[it]
                    act.wait_ge(gu_made, i + 1)
                    act.wait_ge(h_made, i + 1)
                    act.activation(sg[a % 2][0:r, :], ps_g[a % 2][0:r, 0:CH], ACT.Silu).then_inc(sg_made, 1)
                    act.wait_ge(h_made, i + 3)
                    act.copy(hT_h[0:r, it, ch * CH:(ch + 1) * CH], h[a % 2][0:r, :]).then_inc(h_high, 1)
                    if a == 0 and not last:
                        split_weights(following(expert), range(KD, PIECES))
                if not last:
                    high_x(following(expert))

            all_experts(act, before, body)

        @block.vector
        def _(dve):
            def stage_idx(e, j):
                dve.tensor_copy(idx[j][:], t.gidx[:, bass.ds(e * CT, CT)]).then_inc(idx_made, 1)

            def split_weights(expert, pieces):
                e, ep, j = expert
                for n in pieces:
                    raw, high, low = piece(j, n)
                    dve.wait_ge(w_high, e * PIECES + n + 1)
                    dve.tensor_tensor(low, raw, high.bitcast(F32), ALU.subtract).then_inc(w_low, 1)

            def low_x(expert):
                e, ep, j = expert
                for c in range(CT):
                    cols = slice(c * P, (c + 1) * P)
                    dve.wait_ge(x_high, e * CT + c + 1)
                    dve.tensor_tensor(xT_l[:, :, cols], ps_tr[(j * CT + c) % 2][:].rearrange("p (k c) -> p k c", c=P),
                                      xT_h[:, :, cols].bitcast(F32), ALU.subtract).then_inc(x_low, 1)

            def put(expert):
                e, ep, j = expert
                for c in range(CT):
                    dve.wait_ge(y_made, e * CT + c + 1 + CT)
                    dve.wait_ge(y_out[c], e * 16 + 16)
                    dve.tensor_copy(y[c][:], ps_y[(j * CT + c) % 2][:]).then_inc(y_put, 1)

            def before(expert):
                split_weights(expert, range(PIECES))
                low_x(expert)

            def body(expert, last, table=0):
                e, ep, j = expert
                if table < -2 or table == 0:
                    stage_idx(e + 2, j)
                if not last:
                    split_weights(following(expert), range(KD))
                for a in range(NGU):
                    i = e * NGU + a
                    it, ch = a // m.chunks, a % m.chunks
                    r, cols = IS[it], slice(ch * CH, (ch + 1) * CH)
                    dve.wait_ge(sg_made, i + 1)
                    dve.wait_ge(h_low, i + 1)
                    dve.tensor_tensor(h[a % 2][0:r, :], ps_u[a % 2][0:r, 0:CH], sg[a % 2][0:r, :], ALU.mult).then_inc(h_made, 1)
                    dve.wait_ge(h_high, i + 1)
                    dve.tensor_tensor(hT_l[0:r, it, cols], h[a % 2][0:r, :], hT_h[0:r, it, cols].bitcast(F32), ALU.subtract).then_inc(h_low, 1)
                    if a == 0 and not last:
                        split_weights(following(expert), range(KD, PIECES))
                if table == -1:
                    put(expert)
                    dve.wait_ge(tab_tr, 1)
                    dve.tensor_copy(t.gidx[:, NT:NT + GT], ps_tr[1][:, 0:GT]).then_inc(tab_put, 1)
                    dve.wait_ge(tab_put, 1)
                    stage_idx(e + 1, 1 - j)
                    stage_idx(e + 2, j)
                    low_x(following(expert))
                    return
                if not last:
                    low_x(following(expert))
                put(expert)

            for j in range(2):
                stage_idx(j, j)
            all_experts(dve, before, body)


def combine(nc, t, g, m):
    K = m.K
    RING = 8
    with Scope(nc, f"co{m.name}") as s:
        row = [s.sb(f"row{r}", [P, D]) for r in range(RING)]
        row_in = [s.sem(f"row_in{r}") for r in range(RING)]
        added = s.sem("added")
        sh, sh_in = (s.sb("sh", [P, NT, D]), s.sem("sh_in")) if m.shared else (None, None)
        block = s.block()
        todo = [(tt, k) for tt in range(NT) for k in range(K)]

        @block.sync
        def _(sp):
            if m.shared:
                sp.dma_start(sh[:], m.y_dram[0:N, :].rearrange("(t p) d -> p t d", p=P)).then_inc(sh_in, 16)

        @block.gpsimd
        def _(pool):
            for n, (tt, k) in enumerate(todo):
                if n >= RING:
                    pool.wait_ge(added, n - RING + 1 + m.shared)
                c = k * NT + tt
                pool.indirect_dma_start(out=row[n % RING][:], out_offset=None, in_=m.y_dram,
                                        in_offset=bass.IndirectOffsetOnAxis(ap=t.slot[:, c:c + 1], axis=0),
                                        bounds_check=m.y_rows - 1, oob_is_err=False).then_inc(row_in[n % RING], 16)

        @block.vector
        def _(dve):
            if m.shared:
                dve.wait_ge(sh_in, 16)
                dve.tensor_tensor(t.x[:], t.x[:], sh[:], ALU.add).then_inc(added, 0 + 1)
            for n, (tt, k) in enumerate(todo):
                c = k * NT + tt
                dve.wait_ge(row_in[n % RING], 16 * (n // RING + 1))
                if n or m.shared:
                    dve.wait_ge(added, n + m.shared)
                dve.scalar_tensor_tensor(out=t.x[:, tt, :], in0=row[n % RING][:], scalar=t.gate[:, c:c + 1], in1=t.x[:, tt, :],
                                         op0=ALU.mult, op1=ALU.add).then_inc(added, 1)
            dve.wait_ge(added, len(todo) + m.shared)


def causal_attention(nc, t, g):
    SC = float(np.float32(1.0) / np.sqrt(np.float32(HD)))
    R3 = 3 * HD
    with Scope(nc, "ca") as s:
        wq, wk, wv, wo = s.sb("wq", [P, KD, D]), s.sb("wk", [P, D]), s.sb("wv", [P, D]), s.sb("wo", [P, KD, D])
        ctxT = s.sb("ctxT", [P, S])
        stats, mv = s.sb("stats", [P, TB, 6]), s.sb("mv", [P, TB, 2])
        std, rstd = s.sb("std", [P, TB]), s.sb("rstd", [P, TB])
        hq, hqT = s.sb("hq", [P, TB, D]), s.sb("hqT", [P, KD, S])
        v = s.sb("v", [P, TB, D])
        wqs, wks = s.sb("wqs", [P, KD, P]), s.sb("wks", [P, P])
        vp = [s.sb(f"vp{j}", [P, TB, P]) for j in range(GH)]
        pick = s.sb("pick", [P, 2, 2, GH, P], F32R)
        pickf = s.sb("pickf", [P, 2, 2, GH, P])
        negf, neg = s.sb("negf", [P, 2, P]), s.sb("neg", [P, 2, P], F32R)
        identr = s.sb("identr", [P, P], F32R)
        qh, ql = s.sb("qh", [P, S], F32R), s.sb("ql", [P, S], F32R)
        kh, kl = s.sb("kh", [P, S], F32R), s.sb("kl", [P, S], F32R)
        qs = [s.sb(f"qs{j}", [R3 + 1, S], F32R) for j in range(GH)]
        ks = [s.sb(f"ks{j}", [R3 + 1, S], F32R) for j in range(GH)]
        nmax = [s.sb(f"nmax{j}", [P, TB], F32R) for j in range(GH)]
        probs = [s.sb(f"probs{j}", [P, TB, S]) for j in range(2)]
        spare = s.sb("spare", [P, 1])
        rec = [s.sb(f"rec{j}", [P // 2, S]) for j in range(2)]
        oT = s.sb("oT", [P, NG, S])
        pa, pb = s.ps("pa"), s.ps("pb")
        ps_max = [s.ps(f"ps_max{j}") for j in range(2)]
        ps_s = [s.ps(f"ps_s{j}") for j in range(2)]
        ps_o = [s.ps(f"ps_o{j}") for j in range(2)]
        w_in, ctx_in, consts, made = (s.sem(n) for n in ("w_in", "ctx_in", "consts", "made"))
        ln_seq, ln_var, ln_std, hq_made, hq_tr, hqT_made = (s.sem(n) for n in ("ln_seq", "ln_var", "ln_std", "hq_made", "hq_tr", "hqT_made"))
        v_made, v_put, staged, proj, high, low = (s.sem(n) for n in ("v_made", "v_put", "staged", "proj", "high", "low"))
        stacked, q_put, k_put, smax, maxed, nm_row, nm_put = (s.sem(n) for n in ("stacked", "q_put", "k_put", "smax", "maxed", "nm_row", "nm_put"))
        s_made, p_made, weighed, rec_made, o_put, y_made, y_added = (s.sem(n) for n in ("s_made", "p_made", "weighed", "rec_made", "o_put", "y_made", "y_added"))
        block = s.block()
        PAIRS = H1 // 2

        def heads(eng, b, before, step, after):
            before((b * NG, 0, 0))
            step((b * NG, 0, 0), first=True)
            step((b * NG, 0, 1))
            with eng.Fori(0, NG - 1) as gr:
                step((b * NG + gr, gr, 2), projects=True)
                step((b * NG + gr, gr, 3), pair_due=True)
                step((b * NG + gr + 1, gr + 1, 0))
                step((b * NG + gr + 1, gr + 1, 1), pair_due=True)
            step((b * NG + NG - 1, NG - 1, 2), ahead=False)
            step((b * NG + NG - 1, NG - 1, 3), pair_due=True, ahead=False, last=True)
            after((b * NG + NG - 1, NG - 1, GH - 1))

        def next_group(head):
            it, gr, j = head
            return it + 1, gr + 1, 0

        def following(head, d=1):
            it, gr, j = head
            other = (j + d) // GH
            return it + other, gr + other, (j + d) % GH

        @block.sync
        def _(sp):
            sp.dma_start(wq[:], g["wq1"]).then_inc(w_in, 16)
            sp.dma_start(wk[:], g["wk1"]).then_inc(w_in, 16)
            sp.dma_start(wv[:], g["wv1"]).then_inc(w_in, 16)
            sp.dma_start(wo[:], g["wo1"]).then_inc(w_in, 16)
            sp.sem_inc(o_put, 2)
            with sp.Fori(0, B) as b:
                sp.wait_ge(o_put, b * PAIRS + 2)
                sp.dma_start(ctxT[:], g["ctxT"][:, bass.ds(b * S, S)]).then_inc(ctx_in, 16)

        @block.gpsimd
        def _(pool):
            pool.memset(pickf[:], 0.0).then_inc(consts, 1)
            pool.memset(negf[:], 0.0).then_inc(consts, 1)
            for j in range(GH):
                pool.memset(vp[j][:], 0.0).then_inc(consts, 1)
            pool.wait_ge(consts, 2 + GH)
            for j in range(GH):
                head = slice(j * HD, (j + 1) * HD)
                pool.memset(vp[j][:, :, P // 2 + j % 2 * HD:P // 2 + (j % 2 + 1) * HD], 1.0).then_inc(consts, 1)
                for x, part, blk in ((0, 0, 0), (0, 1, 1), (0, 0, 2), (1, 0, 0), (1, 0, 1), (1, 1, 2)):
                    pool.tensor_copy(pickf[:, x, part, j, blk * HD:(blk + 1) * HD], t.ident[:, head]).then_inc(consts, 1)
            pool.affine_select(out=negf[:, 0, :], in_=negf[:, 0, :], compare_op=ALU.is_ge, fill=NEG, base=0,
                               pattern=[[-1, P]], channel_multiplier=1).then_inc(consts, 1)
            pool.affine_select(out=negf[:, 1, :], in_=negf[:, 1, :], compare_op=ALU.is_ge, fill=NEG, base=0,
                               pattern=[[1, P]], channel_multiplier=-1).then_inc(consts, 1)
            pool.wait_ge(w_in, 64)
            pool.sem_inc(proj, 1)
            pool.sem_inc(weighed, GH)
            with pool.Fori(0, B) as b:
                with pool.Fori(0, NG) as gr:
                    it = b * NG + gr
                    pool.wait_ge(proj, it * 2 + 1)
                    pool.tensor_tensor(spare[:], t.ln_eps[:], t.ln_eps[:], ALU.add)
                    pool.tensor_copy(wqs[:], wq[:, :, bass.ds(gr * P, P)]).then_inc(staged, 1)
                    pool.tensor_copy(wks[:], wk[:, bass.ds(gr * P, P)]).then_inc(staged, 1)
                    for j in range(GH):
                        if j == 0:
                            pool.wait_ge(v_put, b * TB + TB)
                        pool.wait_ge(weighed, (it * GH) + j + 1)
                        pool.tensor_copy(vp[j][:, :, j % 2 * HD:(j % 2 + 1) * HD], v[:, :, bass.ds(gr * P + j * HD, HD)]).then_inc(staged, 1)

        @block.tensor
        def _(pe):
            def project(head, waits):
                it, gr, j = head
                pe.wait_ge(staged, it * (2 + GH) + 2)
                if waits:
                    pe.wait_ge(q_put, it * GH)
                    pe.wait_ge(k_put, it * GH)
                for k in range(KD):
                    mm = pe.matmul(pa[:], wqs[:, k, :], hqT[:, k, :], start=k == 0, stop=k == KD - 1)
                mm.then_inc(proj, 1)
                pe.matmul(pb[:], wks[:], ctxT[:], start=True, stop=True).then_inc(proj, 1)

            def stack(head):
                it, gr, j = head
                if j == 0:
                    pe.wait_ge(low, it * 2 + 2)
                else:
                    pe.wait_ge(q_put, it * GH + j)
                    pe.wait_ge(k_put, it * GH + j)
                pe.matmul(pa[0:R3, :], pick[:, 0, 0, j, 0:R3], qh[:], start=True, stop=False)
                pe.matmul(pa[0:R3, :], pick[:, 0, 1, j, 0:R3], ql[:], start=False, stop=True).then_inc(stacked, 1)
                pe.matmul(pb[0:R3, :], pick[:, 1, 0, j, 0:R3], kh[:], start=True, stop=False)
                pe.matmul(pb[0:R3, :], pick[:, 1, 1, j, 0:R3], kl[:], start=False, stop=True).then_inc(stacked, 1)

            def for_max(head, st):
                it, gr, j = head
                i = it * GH + j
                if st == 0:
                    pe.wait_ge(q_put, i + 1)
                    pe.wait_ge(k_put, i + 1)
                if st >= 2:
                    pe.wait_ge(maxed, i * TB + st - 1)
                w = (st + 1) * P
                pe.matmul(ps_max[st % 2][:, 0:w], qs[j][0:R3, st * P:w], ks[j][0:R3, 0:w], start=True, stop=False)
                pe.matmul(ps_max[st % 2][:, st * P:w], identr[:], neg[:, 0, :], start=False, stop=True).then_inc(smax, 1)

            def max_row(head):
                it, gr, j = head
                pe.wait_ge(maxed, (it * GH + j) * TB + TB)
                for st in range(TB):
                    mm = pe.matmul(ps_max[0][0:1, st * P:(st + 1) * P], nmax[j][:, st:st + 1], identr[:], start=True, stop=True)
                mm.then_inc(nm_row, 1)

            def scores(head, l, first):
                it, gr, j = head
                i = it * GH + j
                if l == 0:
                    pe.wait_ge(nm_put, i + 1)
                if l >= 2 or not first:
                    pe.wait_ge(p_made, i * TB + l - 1)
                pe.matmul(ps_s[l % 2][:, 0:S - l * P], ks[j][:, l * P:(l + 1) * P], qs[j][:, l * P:S], start=True, stop=False)
                pe.matmul(ps_s[l % 2][:, 0:P], identr[:], neg[:, 1, :], start=False, stop=True).then_inc(s_made, 1)

            def weigh(head, l):
                it, gr, j = head
                i = it * GH + j
                if l == 0:
                    pe.wait_ge(p_made, i * TB + TB)
                    pe.wait_ge(staged, it * (2 + GH) + 2 + j + 1)
                    if j % 2 == 0:
                        pe.wait_ge(o_put, it * 2 + j // 2 + 1)
                mm = pe.matmul(ps_o[j // 2][:, l * P:S], vp[j][:, l, :], probs[j % 2][:, l, l * P:S],
                               start=j % 2 == 0 and l == 0, stop=j % 2 == 1 and l == TB - 1)
                if l == TB - 1:
                    mm.then_inc(weighed, 1)

            def weigh_all(head):
                for l in range(TB):
                    weigh(head, l)

            def before(head):
                project(head, False)
                stack(head)
                stack(following(head))
                for st in range(TB):
                    for_max(head, st)
                max_row(head)

            def step(head, first=False, last=False, projects=False, pair_due=False, ahead=True):
                nxt, prev = following(head), following(head, -1)
                scores(head, 0, first)
                scores(head, 1, first)
                if not last:
                    for_max(nxt, 0)
                    for_max(nxt, 1)
                if projects:
                    project(next_group(head), True)
                elif ahead:
                    stack(following(head, 2))
                if not first:
                    weigh(prev, 0)
                if not last:
                    for_max(nxt, 2)
                    for_max(nxt, 3)
                scores(head, 2, first)
                if not first:
                    weigh(prev, 1)
                scores(head, 3, first)
                if not last:
                    max_row(nxt)
                if projects:
                    stack(following(head, 2))
                if not first:
                    weigh(prev, 2)
                    weigh(prev, 3)

            pe.sem_inc(y_added, 2)
            pe.wait_ge(w_in, 64)
            pe.wait_ge(made, 3 + GH)
            pe.wait_ge(consts, 4 + 8 * GH)
            with pe.Fori(0, B) as b:
                for k in range(KD):
                    pe.wait_ge(hq_made, b * TB + TB)
                    if k == 0:
                        pe.wait_ge(y_added, b * TB + 2)
                    if k >= 2:
                        pe.wait_ge(hqT_made, b * KD + k - 1)
                    for tt in range(TB):
                        tr = pe.transpose(ps_s[k % 2][:, tt * P:(tt + 1) * P], hq[:, tt, k * P:(k + 1) * P], t.ident[:])
                    tr.then_inc(hq_tr, 1)
                for tt in range(TB):
                    pe.wait_ge(ctx_in, b * 16 + 16)
                    if tt >= 2:
                        pe.wait_ge(v_put, b * TB + tt - 1)
                    pe.matmul(ps_max[tt % 2][:], ctxT[:, tt * P:(tt + 1) * P], wv[:], start=True, stop=True).then_inc(v_made, 1)
                pe.wait_ge(hqT_made, b * KD + KD)
                pe.wait_ge(v_put, b * TB + TB)
                heads(pe, b, before, step, weigh_all)
                for tt in range(TB):
                    pe.wait_ge(o_put, b * PAIRS + PAIRS + 2)
                    pe.wait_ge(y_added, b * TB + tt + 1)
                    for k in range(NG):
                        mm = pe.matmul(ps_s[tt % 2][:], oT[:, k, tt * P:(tt + 1) * P], wo[:, k, :], start=k == 0, stop=k == NG - 1)
                    mm.then_inc(y_made, 1)

        @block.scalar
        def _(act):
            def high_parts(head):
                it, gr, j = head
                act.wait_ge(proj, it * 2 + 2)
                act.activation(qh[:], pa[:], ACT.Copy, scale=SC).then_inc(high, 1)
                act.wait_ge(proj, it * 2 + 3)
                act.copy(kh[:], pb[:]).then_inc(high, 1)

            def put_q(head):
                it, gr, j = head
                act.wait_ge(stacked, (it * GH + j) * 2 + 1)
                act.copy(qs[j][0:R3, :], pa[0:R3, :]).then_inc(q_put, 1)

            def put_max(head):
                it, gr, j = head
                act.wait_ge(nm_row, it * GH + j + 1)
                act.copy(qs[j][R3:R3 + 1, :], ps_max[0][0:1, :]).then_inc(nm_put, 1)

            def exps(head, l):
                it, gr, j = head
                act.wait_ge(s_made, (it * GH + j) * TB + l + 1)
                act.activation(probs[j % 2][:, l, l * P:S], ps_s[l % 2][:, 0:S - l * P], ACT.Exp).then_inc(p_made, 1)

            def before(head):
                high_parts(head)
                put_q(head)
                put_q(following(head))
                put_max(head)

            def step(head, first=False, last=False, projects=False, pair_due=False, ahead=True):
                exps(head, 0)
                exps(head, 1)
                if projects:
                    high_parts(next_group(head))
                elif ahead:
                    put_q(following(head, 2))
                exps(head, 2)
                exps(head, 3)
                if not last:
                    put_max(following(head))
                if projects:
                    put_q(following(head, 2))

            with act.Fori(0, B) as b:
                act.wait_ge(ln_var, b + 1)
                act.activation(std[:], mv[:, :, 1], ACT.Sqrt, bias=t.ln_eps[:]).then_inc(ln_std, 1)
                for k in range(KD):
                    act.wait_ge(hq_tr, b * KD + k + 1)
                    act.copy(hqT[:, k, :], ps_s[k % 2][:]).then_inc(hqT_made, 1)
                for tt in range(TB):
                    act.wait_ge(v_made, b * TB + tt + 1)
                    act.copy(v[:, tt, :], ps_max[tt % 2][:]).then_inc(v_put, 1)
                heads(act, b, before, step, lambda head: None)

        @block.vector
        def _(dve):
            def low_parts(head):
                it, gr, j = head
                dve.wait_ge(high, it * 2 + 1)
                dve.scalar_tensor_tensor(out=ql[:], in0=pa[:], scalar=SC, in1=qh[:].bitcast(F32), op0=ALU.mult, op1=ALU.subtract).then_inc(low, 1)
                dve.wait_ge(high, it * 2 + 2)
                dve.tensor_tensor(kl[:], pb[:], kh[:].bitcast(F32), ALU.subtract).then_inc(low, 1)

            def put_k(head):
                it, gr, j = head
                dve.wait_ge(stacked, (it * GH + j) * 2 + 2)
                dve.tensor_copy(ks[j][0:R3, :], pb[0:R3, :]).then_inc(k_put, 1)

            def maximum(head, st):
                it, gr, j = head
                dve.wait_ge(smax, (it * GH + j) * TB + st + 1)
                dve.tensor_reduce(nmax[j][:, st:st + 1], ps_max[st % 2][:, 0:(st + 1) * P], AX.X, ALU.max, negate=True).then_inc(maxed, 1)

            def normalize(head):
                it, gr, j = head
                pair = j // 2
                dve.wait_ge(weighed, it * GH + j + 1 + GH)
                dve.reciprocal(rec[pair][:], ps_o[pair][P // 2:P, :]).then_inc(rec_made, 1)
                dve.wait_ge(rec_made, it * 2 + pair + 1)
                dve.tensor_tensor(oT[pair * (P // 2):(pair + 1) * (P // 2), bass.ds(gr, 1), :].rearrange("p o s -> p (o s)"),
                                  ps_o[pair][0:P // 2, :], rec[pair][:], ALU.mult).then_inc(o_put, 1)

            def before(head):
                low_parts(head)
                put_k(head)
                put_k(following(head))
                for st in range(TB):
                    maximum(head, st)

            def step(head, first=False, last=False, projects=False, pair_due=False, ahead=True):
                nxt = following(head)
                if not last:
                    maximum(nxt, 0)
                    maximum(nxt, 1)
                if projects:
                    low_parts(next_group(head))
                elif ahead:
                    put_k(following(head, 2))
                if not last:
                    maximum(nxt, 2)
                    maximum(nxt, 3)
                if projects:
                    put_k(following(head, 2))
                if pair_due:
                    normalize(following(head, -2))

            for j in range(GH):
                dve.memset(ks[j][R3:R3 + 1, :].bitcast(F32), 1.0).then_inc(made, 1)
            dve.wait_ge(consts, 4 + 8 * GH)
            dve.tensor_copy(pick[:], pickf[:]).then_inc(made, 1)
            dve.tensor_copy(neg[:], negf[:]).then_inc(made, 1)
            dve.tensor_copy(identr[:], t.ident[:]).then_inc(made, 1)
            with dve.Fori(0, B) as b:
                for tt in range(TB):
                    dve.bn_stats(stats[:, tt, :], t.x[:, bass.ds(b * TB + tt, 1), :].rearrange("p o d -> p (o d)")).then_inc(ln_seq, 1)
                dve.wait_ge(ln_seq, b * (TB + 1) + TB)
                dve.memset(rstd[:], 0.0)
                for tt in range(TB):
                    ag = dve.bn_aggr(mv[:, tt, :], stats[:, tt, :])
                ag.then_inc(ln_var, 1)
                dve.wait_ge(ln_std, b + 1)
                dve.reciprocal(rstd[:], std[:]).then_inc(ln_seq, 1)
                dve.wait_ge(ln_seq, b * (TB + 1) + TB + 1)
                for tt in range(TB):
                    dve.tensor_scalar(hq[:, tt, :], t.x[:, bass.ds(b * TB + tt, 1), :].rearrange("p o d -> p (o d)"), mv[:, tt, 0:1], rstd[:, tt:tt + 1],
                                      ALU.subtract, ALU.mult).then_inc(hq_made, 1)
                heads(dve, b, before, step, normalize)
                for tt in range(TB):
                    dve.wait_ge(y_made, b * TB + tt + 1)
                    xt = t.x[:, bass.ds(b * TB + tt, 1), :].rearrange("p o d -> p (o d)")
                    dve.tensor_tensor(xt, ps_s[tt % 2][:], xt, ALU.add).then_inc(y_added, 1)


def build_program(nc, g, out):
    with Scope(nc, "all") as s:
        t = Shared()
        t.x = s.sb("x", [P, NT, D])
        t.ident, t.ones = s.sb("ident", [P, P]), s.sb("ones", [P, P])
        t.ln_eps, t.rms_eps = s.sb("ln_eps", [P, 1]), s.sb("rms_eps", [P, 1])
        with Scope(nc, "l0w") as w:
            t.wa, t.mo, t.wkr = w.sb("wa", [P, H0, KD, R]), w.sb("mo", [P, H0, D]), w.sb("wkr", [P, H0, R])
            fold_weights(nc, t, g)
            latent_attention(nc, t, g)
        moe_layer(nc, t, g, LAYER0_MOE)
        causal_attention(nc, t, g)
        moe_layer(nc, t, g, LAYER1_MOE)
        store_x(nc, t, out)


def moe_layer(nc, t, g, m):
    NE = m.E + (NSH if m.shared else 0)
    CT = m.cap // P
    m.y_rows = NE * m.cap
    m.xn_dram = nc.dram_tensor(f"xn_{m.name}", (N, D), F32).ap()
    m.y_dram = nc.dram_tensor(f"y_{m.name}", (m.y_rows, D), F32).ap()
    m.table = nc.dram_tensor(f"table_{m.name}", (m.E * m.cap, 1), F32).ap()
    with Scope(nc, f"moe{m.name}") as s:
        t.gate = s.sb("gate", [P, m.K * NT])
        t.slot = s.sb("slot", [P, m.K * NT], I32)
        t.gidx = s.sb("gidx", [P, (NE + 2) * CT], I32)
        if m.shared:
            t.dslot, t.tokid = s.sb("dslot", [P, m.K * NT], I32), s.sb("tokid", [P, NT])
        if m.rms:
            t.norm_w = s.sb("norm_w", [P, D])
        route(nc, t, g, m)
        experts(nc, t, g, m)
        combine(nc, t, g, m)


LAYER0_MOE = MoeLayer(name="0", E=E0, K=K0, I=I0, cap=CAP0, chunks=2, router="wr0", wgu="wgu0", wd="wd0", rms=False,
                  shared=False, choice_major=True, renorm=False, drop_weight=True, z_made=None)
LAYER1_MOE = MoeLayer(name="1", E=E1, K=K1, I=I1, cap=CAP1, chunks=1, router="wr1", wgu="wgu1", wd="wd1", rms=True,
                  shared=True, choice_major=False, renorm=True, drop_weight=False, z_made=3)


def store_x(nc, t, out):
    with Scope(nc, "st") as s:
        stored = s.sem("stored")
        block = s.block()

        @block.sync
        def _(sp):
            sp.dma_start(out.rearrange("(t p) d -> p t d", p=P), t.x[:]).then_inc(stored, 16)
            sp.wait_ge(stored, 16)


def _rope_tables():
    inv = (np.float32(1.0) / np.float32(10000.0) ** (np.arange(0, DC, 2, dtype=np.float32) / np.float32(DC))).astype(np.float32)
    ang = np.arange(SK, dtype=np.float32)[:, None] * inv[None, :]
    def lay(a):
        a = np.repeat(a, 2, axis=-1).astype(np.float32)
        return np.ascontiguousarray(a.reshape(LT, P, DC).transpose(1, 0, 2))
    return lay(np.cos(ang)), lay(np.sin(ang))


def kernel(x, ctx_512, L0_xattn_Wq, L0_xattn_w_kc_q, L0_xattn_w_kc_kv, L0_xattn_W_qr, L0_xattn_W_kr, L0_xattn_Wo,
           L0_ffn_Wr, L0_ffn_Wg, L0_ffn_Wu, L0_ffn_Wd, L1_xattn_Wq, L1_xattn_Wkv_expand, L1_xattn_Wout,
           L1_ffn_norm_w, L1_ffn_gate_w, L1_ffn_w13, L1_ffn_w2, L1_ffn_shared_gate_w, L1_ffn_shared_up_w,
           L1_ffn_shared_down_w):
    import concourse.bacc as _bacc
    from concourse.bass_utils import run_bass_kernel_spmd as _run

    def rows(a, r, p=P):
        return np.asarray(a).reshape(r // p, p, -1).transpose(1, 0, 2)

    cos, sin = _rope_tables()
    lay = {
        "x": np.asarray(x).reshape(N, D),
        "ctx": np.asarray(ctx_512).reshape(B * SK, DC),
        "cos": cos, "sin": sin,
        "w_kc_qT": np.asarray(L0_xattn_w_kc_q).transpose(2, 0, 1).reshape(KQ, P, H0, HK).transpose(1, 0, 2, 3),
        "w_qr": np.asarray(L0_xattn_W_qr).transpose(1, 0, 2).reshape(KQ, P, H0, R).transpose(1, 0, 2, 3),
        "wq0": rows(L0_xattn_Wq, H0 * HK),
        "w_kc_kv": np.asarray(L0_xattn_w_kc_kv).transpose(1, 0, 2),
        "wo0": rows(np.asarray(L0_xattn_Wo).T, H0 * HK),
        "w_kr": np.asarray(L0_xattn_W_kr).transpose(1, 0, 2),
        "wr0": rows(np.asarray(L0_ffn_Wr).T, D),
        "wgu0": np.concatenate([np.asarray(L0_ffn_Wg), np.asarray(L0_ffn_Wu)], axis=1).transpose(0, 2, 1).reshape(E0, KD, P, 2 * I0).transpose(0, 2, 1, 3),
        "wd0": np.asarray(L0_ffn_Wd).transpose(0, 2, 1),
        "ctxT": np.asarray(ctx_512)[:, 0:S, :].transpose(2, 0, 1).reshape(DC, B * S),
        "wq1": rows(np.asarray(L1_xattn_Wq).T, D),
        "wk1": np.asarray(L1_xattn_Wkv_expand)[0:D].T,
        "wv1": np.asarray(L1_xattn_Wkv_expand)[D:2 * D].T,
        "wo1": rows(np.asarray(L1_xattn_Wout).T, D),
        "norm_w": np.tile(np.asarray(L1_ffn_norm_w)[None], (P, 1)),
        "wr1": rows(np.asarray(L1_ffn_gate_w).T, D),
        "wgu1": np.concatenate([np.concatenate([np.asarray(L1_ffn_shared_gate_w), np.asarray(L1_ffn_shared_up_w)], axis=1)[None]] * NSH + [np.asarray(L1_ffn_w13)])
                .reshape(E1 + NSH, KD, P, 2 * I1).transpose(0, 2, 1, 3),
        "wd1": np.concatenate([np.asarray(L1_ffn_shared_down_w)[None]] * NSH + [np.asarray(L1_ffn_w2)]),
    }
    nc = _bacc.Bacc("TRN2", target_bir_lowering=False, num_devices=1)
    arrays, g = {}, {}
    for name, a in lay.items():
        a = np.ascontiguousarray(a)
        arrays[f"in_{name}"] = a
        g[name] = nc.dram_tensor(f"in_{name}", a.shape, mybir.dt.from_np(a.dtype), kind="ExternalInput").ap()
    out = nc.dram_tensor("out_x", (N, D), F32, kind="ExternalOutput").ap()
    build_program(nc, g, out)
    r = _run(nc, [arrays], core_ids=[0])
    return r.results[0]["out_x"].reshape(B, S, D)
```
